# Optimizing a Trainium2 kernel written in Bass

```python
import numpy as np
import jax
import jax.numpy as jnp

def _softmax(x, axis=-1):
    return jax.nn.softmax(x, axis=axis)

def _gelu(x):
    return jax.nn.gelu(x, approximate=True)

def _silu(x):
    return jax.nn.silu(x)

def _sigmoid(x):
    return jax.nn.sigmoid(x)

def _layernorm(x, axis=-1, eps=1e-05):
    m = jnp.mean(x, axis=axis, keepdims=True)
    v = jnp.var(x, axis=axis, keepdims=True)
    return (x - m) / jnp.sqrt(v + eps)

def _scatter_add(tgt, idx, src, axis=0):
    return tgt.at[idx].add(src)

def _segment_sum(src, seg, n):
    return jax.ops.segment_sum(src, seg, n)
kernel_name = 'mk_gnn_resnorm_d4_gnn_r8_b72629'

def setup_inputs(seed: int=0):
    np.random.seed(seed)
    _w = jnp.asarray

    def _rec_inputs():
        import jax
        import jax.numpy as jnp
        _gk = jax.random.key(seed)
        x = -0.0003713 + 1 * jax.random.normal(jax.random.fold_in(_gk, 1), (6250, 256), jnp.float32)
        _s = jax.random.randint(jax.random.fold_in(_gk, 2), (50000,), 0, 6250, jnp.int32)
        _d = jax.random.randint(jax.random.fold_in(_gk, 3), (50000,), 0, 6250, jnp.int32)
        _loop = jnp.arange(6250, dtype=jnp.int32)
        src = jnp.concatenate([_s, _d, _loop])
        dst = jnp.concatenate([_d, _s, _loop])
        _o = jnp.argsort(dst, stable=True)
        src = src[_o]
        dst = dst[_o]
        edge_attr_256 = 9.41057e-06 + 1 * jax.random.normal(jax.random.fold_in(_gk, 11), (106250, 256), jnp.float32)
        return (x, src, dst, edge_attr_256)
    x, src, dst, edge_attr_256 = _rec_inputs()

    def _L0_gnn_setup():
        import jax, jax.numpy as jnp
        import numpy as np
        N = 6250
        E = 200000
        D = 256
        H = 256
        EPS = 1e-05

        def _gnn_layer(x, row, col, W, b, g, beta):
            n = x.shape[0]
            neigh = x[col]
            agg = jax.ops.segment_sum(neigh, row, num_segments=n)
            deg = jax.ops.segment_sum(jnp.ones((row.shape[0],), x.dtype), row, num_segments=n)
            deg = jnp.maximum(deg, 1.0)[:, None]
            h = (x + agg / deg) @ W.T + b
            mu = jnp.mean(h, axis=-1, keepdims=True)
            var = jnp.mean(jnp.square(h - mu), axis=-1, keepdims=True)
            hn = (h - mu) * jax.lax.rsqrt(var + EPS) * g + beta
            return jax.nn.silu(hn)
        key = jax.random.key(seed)
        ks = jax.random.split(key, 12)
        x = jax.random.normal(ks[0], (N, D), dtype=jnp.float32)
        edge_index = jax.random.randint(ks[1], (2, E), 0, N, dtype=jnp.int32)
        s0 = 1.0 / np.sqrt(D)
        s1 = 1.0 / np.sqrt(H)
        W0 = jax.random.uniform(ks[2], (H, D), jnp.float32, -s0, s0)
        b0 = jax.random.uniform(ks[3], (H,), jnp.float32, -s0, s0)
        g0 = jnp.ones((H,), jnp.float32)
        beta0 = jnp.zeros((H,), jnp.float32)
        W1 = jax.random.uniform(ks[4], (H, H), jnp.float32, -s1, s1)
        b1 = jax.random.uniform(ks[5], (H,), jnp.float32, -s1, s1)
        g1 = jnp.ones((H,), jnp.float32)
        beta1 = jnp.zeros((H,), jnp.float32)
        return {'x': x, 'edge_index': edge_index, 'W0': W0, 'b0': b0, 'g0': g0, 'beta0': beta0, 'W1': W1, 'b1': b1, 'g1': g1, 'beta1': beta1}
    _L0_gnn_all = _L0_gnn_setup()
    _L0_gnn_in = {k: v for k, v in _L0_gnn_all.items() if k in ('W0', 'b0', 'g0', 'beta0', 'W1', 'b1', 'g1', 'beta1')}
    del _L0_gnn_all

    def _L1_gnn_setup():
        import jax, jax.numpy as jnp
        import numpy as np
        N_NODES = 6250
        N_EDGES = 100000
        D = 256
        H = 512
        LN_EPS = 1e-05
        key = jax.random.key(seed)
        ks = jax.random.split(key, 8)
        x = jax.random.normal(ks[0], (N_NODES, D), dtype=jnp.float32)
        edge_index = jax.random.randint(ks[1], (2, N_EDGES), 0, N_NODES, dtype=jnp.int64)
        edge_attr = jax.random.normal(ks[2], (N_EDGES, D), dtype=jnp.float32)
        s1 = 1.0 / np.sqrt(H)
        s2 = 1.0 / np.sqrt(H)
        W1 = jax.random.uniform(ks[3], (H, H), jnp.float32, -s1, s1)
        b1 = jax.random.uniform(ks[4], (H,), jnp.float32, -s1, s1)
        W2 = jax.random.uniform(ks[5], (H, D), jnp.float32, -s2, s2)
        b2 = jax.random.uniform(ks[6], (D,), jnp.float32, -s2, s2)
        gamma = jnp.ones((D,), jnp.float32)
        beta = jnp.zeros((D,), jnp.float32)
        return {'x': x, 'edge_index': edge_index, 'edge_attr': edge_attr, 'W1': W1, 'b1': b1, 'W2': W2, 'b2': b2, 'gamma': gamma, 'beta': beta}
    _L1_gnn_all = _L1_gnn_setup()
    _L1_gnn_in = {k: v for k, v in _L1_gnn_all.items() if k in ('W1', 'b1', 'W2', 'b2', 'gamma', 'beta')}
    del _L1_gnn_all

    def _L2_gnn_setup():
        import jax, jax.numpy as jnp
        import numpy as np
        N_NODES = 6250
        N_EDGES = 200000
        IN_DIM, OUT_DIM, N_HEADS = (256, 64, 4)
        EPS = 1e-12
        key = jax.random.key(seed)
        k1, k2, k3, k4, k5 = jax.random.split(key, 5)
        h = jax.random.normal(k1, (N_NODES, IN_DIM), dtype=jnp.float32)
        edge_index = jax.random.randint(k2, (2, N_EDGES), 0, N_NODES, dtype=jnp.int32)
        W = jax.random.normal(k3, (IN_DIM, OUT_DIM), dtype=jnp.float32) * 0.05
        Wl = jax.random.normal(k4, (N_HEADS, OUT_DIM), dtype=jnp.float32) * 0.05
        Wr = jax.random.normal(k5, (N_HEADS, OUT_DIM), dtype=jnp.float32) * 0.05
        b = jnp.zeros((OUT_DIM,), dtype=jnp.float32)
        return {'h': h, 'W': W, 'Wl': Wl, 'Wr': Wr, 'b': b, 'edge_index': edge_index}
    _L2_gnn_all = _L2_gnn_setup()
    _L2_gnn_in = {k: v for k, v in _L2_gnn_all.items() if k in ('W', 'Wl', 'Wr', 'b')}
    del _L2_gnn_all

    def _L3_gnn_setup():
        import jax, jax.numpy as jnp
        import numpy as np
        N, E = (6250, 100000)
        IN, H, C = (256, 8, 32)
        NEG_SLOPE = 0.2
        EPS = 1e-05
        key = jax.random.key(seed)
        ks = jax.random.split(key, 6)
        x = jax.random.normal(ks[0], (N, IN), jnp.float32)
        edge_index = jax.random.randint(ks[1], (2, E), 0, N, dtype=jnp.int32)
        W = jax.random.normal(ks[2], (IN, H * C), jnp.float32) / np.sqrt(IN).astype(np.float32)
        att_src = jax.random.normal(ks[3], (H, C), jnp.float32) * 0.1
        att_dst = jax.random.normal(ks[4], (H, C), jnp.float32) * 0.1
        bias = jnp.zeros((H * C,), jnp.float32)
        gamma = jnp.ones((H * C,), jnp.float32)
        beta = jnp.zeros((H * C,), jnp.float32)
        return {'x': x, 'edge_index': edge_index, 'W': W, 'att_src': att_src, 'att_dst': att_dst, 'bias': bias, 'gamma': gamma, 'beta': beta}
    _L3_gnn_all = _L3_gnn_setup()
    _L3_gnn_in = {k: v for k, v in _L3_gnn_all.items() if k in ('W', 'att_src', 'att_dst', 'bias', 'gamma', 'beta')}
    del _L3_gnn_all
    return {'x': x, 'src': src, 'dst': dst, 'edge_attr_256': edge_attr_256, 'L0_gnn_W0': _L0_gnn_in['W0'], 'L0_gnn_b0': _L0_gnn_in['b0'], 'L0_gnn_g0': _L0_gnn_in['g0'], 'L0_gnn_beta0': _L0_gnn_in['beta0'], 'L0_gnn_W1': _L0_gnn_in['W1'], 'L0_gnn_b1': _L0_gnn_in['b1'], 'L0_gnn_g1': _L0_gnn_in['g1'], 'L0_gnn_beta1': _L0_gnn_in['beta1'], 'L1_gnn_W1': _L1_gnn_in['W1'], 'L1_gnn_b1': _L1_gnn_in['b1'], 'L1_gnn_W2': _L1_gnn_in['W2'], 'L1_gnn_b2': _L1_gnn_in['b2'], 'L1_gnn_gamma': _L1_gnn_in['gamma'], 'L1_gnn_beta': _L1_gnn_in['beta'], 'L2_gnn_W': _L2_gnn_in['W'], 'L2_gnn_Wl': _L2_gnn_in['Wl'], 'L2_gnn_Wr': _L2_gnn_in['Wr'], 'L2_gnn_b': _L2_gnn_in['b'], 'L3_gnn_W': _L3_gnn_in['W'], 'L3_gnn_att_src': _L3_gnn_in['att_src'], 'L3_gnn_att_dst': _L3_gnn_in['att_dst'], 'L3_gnn_bias': _L3_gnn_in['bias'], 'L3_gnn_gamma': _L3_gnn_in['gamma'], 'L3_gnn_beta': _L3_gnn_in['beta']}

def reference(x, src, dst, edge_attr_256, L0_gnn_W0, L0_gnn_b0, L0_gnn_g0, L0_gnn_beta0, L0_gnn_W1, L0_gnn_b1, L0_gnn_g1, L0_gnn_beta1, L1_gnn_W1, L1_gnn_b1, L1_gnn_W2, L1_gnn_b2, L1_gnn_gamma, L1_gnn_beta, L2_gnn_W, L2_gnn_Wl, L2_gnn_Wr, L2_gnn_b, L3_gnn_W, L3_gnn_att_src, L3_gnn_att_dst, L3_gnn_bias, L3_gnn_gamma, L3_gnn_beta):
    import jax
    import jax.numpy as jnp

    def _L0_gnn_ref(x, edge_index, W0, b0, g0, beta0, W1, b1, g1, beta1):
        import jax, jax.numpy as jnp
        import numpy as np
        N = 6250
        E = 200000
        D = 256
        H = 256
        EPS = 1e-05

        def _gnn_layer(x, row, col, W, b, g, beta):
            n = x.shape[0]
            neigh = x[col]
            agg = jax.ops.segment_sum(neigh, row, num_segments=n)
            deg = jax.ops.segment_sum(jnp.ones((row.shape[0],), x.dtype), row, num_segments=n)
            deg = jnp.maximum(deg, 1.0)[:, None]
            h = (x + agg / deg) @ W.T + b
            mu = jnp.mean(h, axis=-1, keepdims=True)
            var = jnp.mean(jnp.square(h - mu), axis=-1, keepdims=True)
            hn = (h - mu) * jax.lax.rsqrt(var + EPS) * g + beta
            return jax.nn.silu(hn)
        row, col = (edge_index[0], edge_index[1])
        x = _gnn_layer(x, row, col, W0, b0, g0, beta0)
        x = _gnn_layer(x, row, col, W1, b1, g1, beta1)
        return x

    def _L1_gnn_ref(x, edge_index, edge_attr, W1, b1, W2, b2, gamma, beta):
        import jax, jax.numpy as jnp
        import numpy as np
        N_NODES = 6250
        N_EDGES = 100000
        D = 256
        H = 512
        LN_EPS = 1e-05
        i = edge_index[0]
        agg = jax.ops.segment_sum(edge_attr, i, num_segments=x.shape[0])
        h = jnp.concatenate([x, agg], axis=-1)
        h = jax.nn.silu(h @ W1 + b1)
        h = h @ W2 + b2
        mu = jnp.mean(h, axis=-1, keepdims=True)
        var = jnp.mean(jnp.square(h - mu), axis=-1, keepdims=True)
        h = (h - mu) * jax.lax.rsqrt(var + LN_EPS) * gamma + beta
        return h + x

    def _L2_gnn_ref(h, W, Wl, Wr, b, edge_index):
        import jax, jax.numpy as jnp
        import numpy as np
        N_NODES = 6250
        N_EDGES = 200000
        IN_DIM, OUT_DIM, N_HEADS = (256, 64, 4)
        EPS = 1e-12
        N = h.shape[0]
        H = Wl.shape[0]
        x = h @ W
        el = x @ Wl.T
        er = x @ Wr.T
        src, dst = (edge_index[0], edge_index[1])
        e = el[src] + er[dst]
        e = jnp.exp(jax.nn.leaky_relu(e, negative_slope=0.2))
        rowsum = jax.ops.segment_sum(e, src, num_segments=N)
        w = e / jnp.maximum(rowsum, EPS)[src]
        heads = [jax.ops.segment_sum(w[:, hd:hd + 1] * x[dst], src, num_segments=N) for hd in range(H)]
        out = jnp.stack(heads, axis=1)
        out = jax.nn.elu(out + b)
        return out.reshape(N, H * x.shape[1])

    def _L3_gnn_ref(x, edge_index, W, att_src, att_dst, bias, gamma, beta):
        import jax, jax.numpy as jnp
        import numpy as np
        N, E = (6250, 100000)
        IN, H, C = (256, 8, 32)
        NEG_SLOPE = 0.2
        EPS = 1e-05
        n = x.shape[0]
        xl = (x @ W).reshape(n, H, C)
        a_src = jnp.einsum('nhc,hc->nh', xl, att_src)
        a_dst = jnp.einsum('nhc,hc->nh', xl, att_dst)
        loops = jnp.arange(n, dtype=edge_index.dtype)
        src = jnp.concatenate([edge_index[0], loops])
        dst = jnp.concatenate([edge_index[1], loops])
        logits = jax.nn.leaky_relu(a_src[src] + a_dst[dst], NEG_SLOPE)
        seg_max = jax.ops.segment_max(logits, dst, num_segments=n)
        ex = jnp.exp(logits - seg_max[dst])
        denom = jax.ops.segment_sum(ex, dst, num_segments=n)
        alpha = ex / denom[dst]
        msgs = xl[src] * alpha[:, :, None]
        out = jax.ops.segment_sum(msgs, dst, num_segments=n).reshape(n, H * C) + bias
        mu = jnp.mean(out, axis=-1, keepdims=True)
        var = jnp.var(out, axis=-1, keepdims=True)
        return (out - mu) / jnp.sqrt(var + EPS) * gamma + beta
    edge_index = jnp.stack([src, dst])
    x = _layernorm(x + _L0_gnn_ref(x, edge_index, L0_gnn_W0, L0_gnn_b0, L0_gnn_g0, L0_gnn_beta0, L0_gnn_W1, L0_gnn_b1, L0_gnn_g1, L0_gnn_beta1), axis=-1)
    x = _layernorm(x + _L1_gnn_ref(x, edge_index, edge_attr_256, L1_gnn_W1, L1_gnn_b1, L1_gnn_W2, L1_gnn_b2, L1_gnn_gamma, L1_gnn_beta), axis=-1)
    x = _layernorm(x + _L2_gnn_ref(x, L2_gnn_W, L2_gnn_Wl, L2_gnn_Wr, L2_gnn_b, edge_index), axis=-1)
    x = _layernorm(x + _L3_gnn_ref(x, edge_index, L3_gnn_W, L3_gnn_att_src, L3_gnn_att_dst, L3_gnn_bias, L3_gnn_gamma, L3_gnn_beta), axis=-1)
    return x

_drawn_inputs = setup_inputs


def setup_inputs(seed=0):
    import zlib

    import numpy as np

    out = dict(_drawn_inputs(seed))
    spreads = {'L0_gnn_g0': (1.0, 0.2),
     'L0_gnn_beta0': (0.0, 0.1),
     'L0_gnn_g1': (1.0, 0.2),
     'L0_gnn_beta1': (0.0, 0.1),
     'L1_gnn_gamma': (1.0, 0.2),
     'L1_gnn_beta': (0.0, 0.1),
     'L2_gnn_b': (0.0, 0.1),
     'L3_gnn_bias': (0.0, 0.1),
     'L3_gnn_gamma': (1.0, 0.2),
     'L3_gnn_beta': (0.0, 0.1)}
    factors = {'L1_gnn_b1': 5.135, 'L2_gnn_Wl': 5.1}
    for name, (base, spread) in spreads.items():
        noise = np.random.default_rng([zlib.crc32(name.encode()), seed]).standard_normal(out[name].shape)
        drawn = base * np.exp(spread * noise) if base else spread * noise
        out[name] = jnp.asarray(drawn.astype(out[name].dtype))
    for name, factor in factors.items():
        out[name] = (out[name] * factor).astype(out[name].dtype)
    return out
```

```python
import concourse.bass as bass
from concourse import mybir
from contextlib import ExitStack

F32 = mybir.dt.float32
I32 = mybir.dt.int32
U32 = mybir.dt.uint32
I16 = mybir.dt.int16
BF16 = mybir.dt.bfloat16
ALU = mybir.AluOpType
ACT = mybir.ActivationFunctionType
AX = mybir.AxisListType.X

P = 128
NODES = 6250
EDGES = 106250
D = 256
NT = -(-NODES // P)
NODES_UP = NT * P
U = 8
ST = -(-((EDGES + (P - 1) * NT) // P) // (2 * U)) * (2 * U)
SLOTS = ST * P
NB = ST // U
ROWS = EDGES // P
TAIL = EDGES - ROWS * P
COLS = ROWS + 2
SU = 10
SB = ROWS // SU
EW = 2 + D
ER_W = EW + 2
H2, C2 = 4, 64
H3, C3 = 8, 32
W3 = D + H3
W2 = C2 + H2
ACC1 = 2 * (D + 1)
ACC2 = D + H2
G = 7
NG = NT // G
HALF = ST // 2
BIG = 1e30
EPS = 1e-5
assert ROWS == SB * SU and SB % 2 == 1 and NG * G == NT and C2 * H2 == D and C3 * H3 == D and NB % 2 == 0


def gnn_kernel(nc, x, src2, dst2, edge_attr, w0t, b0, g0, be0, w1t, b1, g1, be1, lw1, lb1, lw2, lb2, lga, lbe,
               aw, awlr, ab, gw, gsrc, gdst, gb, gga, gbe, out):
    ctx = ExitStack()
    made = {}

    def sb(name, shape, dt=F32):
        return ctx.enter_context(nc.sbuf_tensor(name, shape, dt))

    def sig(name):
        if name not in made:
            made[name] = ctx.enter_context(nc.semaphore(name))
        return made[name]

    def dram(name, shape, dt=F32):
        return nc.dram_tensor(name, shape, dt, kind="Internal").ap()

    by_src = dram("by_src", (SLOTS, EW))
    by_low = dram("by_low", (P * COLS, 2), I32)
    by_dst = dram("by_dst", (SLOTS, 2), I32)
    h1_tab = dram("h1_tab", (NODES_UP, D))
    x2_tab = dram("x2_tab", (NODES_UP, D))
    p2_tab = dram("p2_tab", (NODES_UP, W2))
    x3_tab = dram("x3_tab", (NODES_UP, D))
    p3_tab = dram("p3_tab", (NODES_UP, W3))

    with ctx:
        acc = sb("acc", [P, NT * ACC1])

        def space(n, dt=F32, wide=1):
            v = acc[:, n * COLS:(n + wide) * COLS]
            return v if dt is F32 else v.bitcast(dt)

        key, seg, other, mask, rank, zero, place = (space(n) for n in range(7))
        src_i, dst_i, tmp_i = (space(n, I32) for n in range(7, 10))
        pair_i = space(10, I32, 2).rearrange("p (c w) -> p c w", w=2)
        reach = acc[0:NT, 14 * COLS:14 * COLS + ST]
        slot_no = acc[0:NT, 16 * COLS:16 * COLS + ST]
        RB = -(-ST // P)
        dst_rows = acc[:, 18 * COLS:18 * COLS + RB * 2 * P].bitcast(I32).rearrange("p (t e w) -> p t e w", t=RB, w=2)
        dst_rowf = acc[:, 21 * COLS:21 * COLS + RB * 2 * P].rearrange("p (t w e) -> p t w e", t=RB, w=2)
        seg_off = acc[:, 24 * COLS:24 * COLS + ST]

        ring_e = sb("ring_e", [P, 2, SU, ER_W])
        ring_x = sb("ring_x", [P, 2, U, W3])
        hot = sb("hot", [P, 2, U, P])
        hot_t = sb("hot_t", [P, U, P])
        idx_ring = sb("idx_ring", [P, 2, SU], I32)
        pair_ring = sb("pair_ring", [P, 2, SU, 2], I32)
        seg_a, seg_b = sb("seg_a", [P, ST], BF16), sb("seg_b", [P, ST], BF16)
        idx_a, idx_b = sb("idx_a", [P, ST], I16), sb("idx_b", [P, ST], I16)
        tile_a, tile_b = sb("tile_a", [1, ST], I16), sb("tile_b", [1, ST], I16)
        last_a = sb("last_a", [1, NT], I32)
        lane = sb("lane", [P, P])
        lane1 = sb("lane1", [P, P])
        ident = sb("ident", [P, P])
        below = acc[:, 26 * COLS:26 * COLS + P]
        upto = acc[:, 26 * COLS + P:26 * COLS + 2 * P]
        ones = sb("ones", [P, P])
        counts = acc[:, 26 * COLS + 2 * P:26 * COLS + 3 * P]
        start_m1 = acc[:, 26 * COLS + 3 * P:26 * COLS + 4 * P]
        small = sb("small", [P, 8])
        small_i = sb("small_i", [P, 8], I32)
        spread = acc[:, 26 * COLS + 4 * P:26 * COLS + 5 * P]
        wsq = sb("wsq", [P, 2, D])
        lw1s = sb("lw1s", [P, 4, 2 * D])
        lw2s = sb("lw2s", [P, 4, D])
        aws = sb("aws", [P, 2, C2])
        awlrs = sb("awlrs", [C2, 2 * H2])
        rows = sb("rows", [1, 3, D])
        lb1s = sb("lb1s", [P, 4])
        vec = sb("vec", [P, 6, D])
        V_G0, V_BE0, V_G1, V_BE1, V_LGA, V_LBE = range(6)
        V_GSRC, V_GDST, V_GB, V_GGA, V_GBE = range(5)
        abv = sb("abv", [P, C2])
        rdeg = sb("rdeg", [P, NT])
        el = sb("el", [P, NT * H2])
        ma = sb("ma", [P, NT * 2 * H3])
        xin2, ub = (sb(n, [P, G, D]) for n in ("xin2", "ub"))
        stat = sb("stat", [P, G, 6])
        mv = sb("mv", [P, G, 2])
        sd = sb("sd", [P, 4, G])
        behind = [NT * W3]

        def tail(parts, n):
            behind[0] += n
            return acc[0:parts, behind[0] - n:behind[0]]

        cmp = tail(P, 2 * U * H3).rearrange("p (a n) -> p a n", a=2)
        rowsb = tail(U * H3, 2 * P).rearrange("p (a n) -> p a n", a=2)
        lastm, pen, scan, sv = (tail(U * H3, P) for _ in range(4))
        svt = tail(P, U * (H3 + 1)).rearrange("p (u h) -> p u h", u=U)
        cand = tail(P, U * H3).rearrange("p (u h) -> p u h", u=U)
        ees = tail(P, U * 2 * H3).rearrange("p (u h) -> p u h", u=U)
        zz = tail(P, 4 * U * H3).rearrange("p (s u h) -> p s u h", s=4, u=U)
        present = sb("present", [P, U])
        mold = sb("mold", [P, 2, 2 * H3])
        resc = sb("resc", [P, 4, 2, H3])
        zl = sb("zl", [P, 2, U, H2])
        eps_c = sb("eps_c", [P, 1])
        ps = ctx.enter_context(nc.psum_tensor("ps", [P, 8, 512], F32))
        psf = ps[:, :, :].rearrange("p a b -> p (a b)")

        acc1 = acc[:, :].rearrange("p (k a w) -> p k a w", a=2, w=D + 1)
        hot_f = hot[:, :, :, :].rearrange("p a b c -> p (a b c)")
        ring_ef = ring_e[:, :, :, :].rearrange("p a b c -> p (a b c)")
        ring_xf = ring_x[:, :, :, :].rearrange("p a b c -> p (a b c)")
        xin = hot_f[:, 0:G * D].rearrange("p (t w) -> p t w", w=D)
        op_t = ring_ef[:, 0:4 * G * P]
        hid_t = ring_xf[:, 0:4 * G * P]
        prj2 = ring_ef[:, 4 * G * P:4 * G * P + G * W2].rearrange("p (t w) -> p t w", w=W2)
        prj3 = ring_xf[:, 0:G * W3].rearrange("p (t w) -> p t w", w=W3)
        mring = ring_ef[:, 0:2 * U * ACC2].rearrange("p (a u w) -> p a u w", a=2, u=U)
        self_t = hot_t[:, :, :].rearrange("p a b -> p (a b)")[:, 0:8 * G * H3].rearrange("p (s t h) -> p s t h", s=8, h=H3)
        none_i = seg_b[:, :].bitcast(I32)
        zero_row = ring_x[:, 0, 0, 0:EW]

        ORDER = {"src": 0, "low": 1, "dst": 2}
        KEYS = {"src": 0, "low": NT, "dst": NT + P}
        PASS = {"p1": 0, "p2": 1, "p3": 2, "p5": 3}
        STAGE = {"d0": 0, "d1": 1, "d2": 2, "d3": 3}
        NORM = {"d0a": (0, 1), "d1a": (NG, 4), "d1b": (NG + 1, 4), "d1d": (NG + 2, 4), "d1e": (NG + 3, 4),
                "d2a": (5 * NG, 1), "d3a": (6 * NG, 2), "d3b": (6 * NG + 1, 2)}
        TURN = {"d0a": (0, 1), "d1a": (NG, 3), "d1c": (NG + 1, 3), "d1f": (NG + 2, 3), "d2b": (4 * NG, 1)}

        def nth(of, s, g):
            return g * of[s][1] + of[s][0]

        block = ctx.enter_context(nc.Block())
        LOADS = 2 + 4 + 3 + 3 + 6

        def peeled(eng, n, body):
            body(0, True, False)
            with eng.Fori(1, n - 1) as i:
                body(i, False, False)
            body(n - 1, False, True)

        def sent(s, b, batches=None):
            whole = 16 * (SU * (SB // 2 + 1) if b == 0 else SU * (SB // 2) + 2)
            return ORDER[s] * whole + (whole if batches is None else 16 * SU * batches)

        def got(s, i):
            return PASS[s] * (16 * U * (NB // 2)) + 16 * U * i

        @block.sync
        def _(sp):
            def load(dst, src):
                sp.dma_start(dst, src).then_inc(sig("loaded"), 16)

            load(src_i, src2)
            load(dst_i, dst2)
            for w, d in ((wsq, w0t), (lw1s, lw1), (lw2s, lw2), (aws, aw)):
                load(w[:, :, :], d.rearrange("(a p) n -> p a n", p=P))
            load(awlrs[:, :], awlr)
            load(lb1s[:, :], lb1)
            load(abv[:, :], ab.partition_broadcast(P))
            for n, d in enumerate((b0, b1, lb2)):
                load(rows[0:1, n, :], d.rearrange("(a n) -> a n", a=1))
            for n, d in enumerate((g0, be0, g1, be1, lga, lbe)):
                load(vec[:, n, :], d.partition_broadcast(P))

            sp.wait_ge(sig("cleared"), 3)
            tiles = by_src.rearrange("(t p) w -> p t w", p=P)
            spare = EDGES // P
            n_pre = 0
            for t in range(spare, ST, G):
                n = min(G, ST - t)
                sp.dma_start(tiles[:, t:t + n, :], ring_x[:, 0, 0:1, 0:EW].broadcast_to([P, n, EW]))\
                  .then_inc(sig("src_prefill"), 16)
                n_pre += 1
            sp.wait_ge(sig("src_prefill"), 16 * n_pre)
            sp.wait_ge(sig("src_tables"), 1)
            with sp.Fori(0, NT) as k:
                last = nc.sync.value_load(last_a[0:1, bass.ds(k, 1)], min_val=0, max_val=ST - 1)
                sp.dma_start(by_src[bass.ds(last * P, P), :], zero_row).then_inc(sig("src_prefill"), 16)
                sp.wait_ge(sig("src_prefill"), 16 * (k + n_pre + 1))
                sp.sem_inc(sig("sp_pace"), 1)
            sp.sem_inc(sig("src_prefilled"), 1)

            attr = edge_attr[0:ROWS * P, :].rearrange("(p c) w -> p c w", c=ROWS)

            def attr_pair(i, first, last):
                for b in range(2):
                    if not first:
                        sp.wait_ge(sig(f"sent{b}"), sent("src", b, i))
                    sp.dma_start(ring_e[:, b, 0:SU, 2:EW], attr[:, bass.ds((2 * i + b) * SU, SU), :])\
                      .then_inc(sig(f"attr{b}"), 16)

            peeled(sp, SB // 2, attr_pair)
            sp.wait_ge(sig("sent0"), sent("src", 0, SB // 2))
            sp.dma_start(ring_e[:, 0, 0:SU, 2:EW], attr[:, (SB - 1) * SU:SB * SU, :]).then_inc(sig("attr0"), 16)
            sp.wait_ge(sig("sent1"), sent("src", 1, SB // 2))
            sp.dma_start(ring_e[0:TAIL, 1, 0, 2:EW], edge_attr[ROWS * P:EDGES, :]).then_inc(sig("attr1"), 16)

            sp.dma_start(by_dst.rearrange("(t p e) w -> p t (e w)", p=P, t=4),
                         none_i.unsqueeze(1).broadcast_to([P, 4, SLOTS // P // 2])).then_inc(sig("dst_prefill"), 16)
            for b in range(2):
                sp.wait_ge(sig(f"sent{b}"), sent("low", b))
            sp.dma_start(pair_i, by_low.rearrange("(p c) w -> p c w", c=COLS)).then_inc(sig("low_back"), 16)
            for b in range(2):
                sp.wait_ge(sig(f"sent{b}"), sent("dst", b))
            for t in range(RB):
                n = min(P, ST - t * P)
                sp.dma_start(dst_rows[0:n, t], by_dst[t * P * P:(t * P + n) * P, :]
                             .rearrange("(s e) w -> s e w", e=P)).then_inc(sig("dst_back"), 16)

            for b in range(2):
                sp.wait_ge(sig(f"sent{b}"), sent("src", b))

            def e_pair(i, first, last):
                for b in range(2):
                    if not first:
                        sp.wait_ge(sig("sum"), U * (2 * i + b - 1))
                    sp.dma_start(ring_e[:, b, 0:U, 0:EW], tiles[:, bass.ds((2 * i + b) * U, U), :])\
                      .then_inc(sig(f"p1_rows{b}"), 16)

            peeled(sp, NB // 2, e_pair)

            def nodes(t, g):
                return t[bass.ds(g * (G * P), G * P), :].rearrange("(t p) w -> p t w", p=P)

            for s, ins, outs in (("d0", [(x, xin)], [(h1_tab, ub)]),
                                 ("d1", [(h1_tab, xin), (x, xin2)], [(x2_tab, xin), (p2_tab, prj2)]),
                                 ("d2", [(x2_tab, xin)], [(x3_tab, xin), (p3_tab, prj3)]),
                                 ("d3", [(x3_tab, xin), (p3_tab, prj3)], [(out, ub)])):
                with sp.Fori(0, NG) as g:
                    sp.wait_ge(sig("free"), STAGE[s] * (NG + 1) + g + 1)
                    for t, s_in in ins:
                        sp.dma_start(s_in[:, :, :] if s_in is not prj3 else s_in, nodes(t, g)).then_inc(sig(f"{s}_in"), 16)
                    sp.wait_ge(sig("result"), STAGE[s] * NG + g + 1)
                    for t, s_out in outs:
                        sp.dma_start(nodes(t, g), s_out[:, :, :]).then_inc(sig(f"{s}_stored"), 16)
                    sp.wait_ge(sig(f"{s}_stored"), 16 * len(outs) * (g + 1))
                    sp.sem_inc(sig("free"), 1)
                for w in {"d0": [w1t], "d1": [gw]}.get(s, []):
                    sp.dma_start(wsq[:, :, :], w.rearrange("(a p) n -> p a n", p=P)).then_inc(sig(f"{s}_weights"), 16)
                if s == "d1":
                    for n, d in enumerate((gsrc, gdst, gb, gga, gbe)):
                        sp.dma_start(vec[:, n, :], d.partition_broadcast(P)).then_inc(sig("d1_vectors"), 16)

        @block.gpsimd
        def _(pool):
            pool.iota(lane[:, :], pattern=[[1, P]], base=0, channel_multiplier=0,
                      allow_small_or_imprecise_dtypes=True).then_inc(sig("made"), 1)
            pool.iota(lane1[:, :], pattern=[[1, P]], base=1, channel_multiplier=0,
                      allow_small_or_imprecise_dtypes=True).then_inc(sig("made"), 1)
            pool.iota(slot_no, pattern=[[1, ST]], base=0, channel_multiplier=0,
                      allow_small_or_imprecise_dtypes=True).then_inc(sig("made"), 1)
            for t, v in ((ident, 0.0), (below, 1.0), (upto, 1.0), (ones, 1.0)):
                pool.memset(t[:, :], v).then_inc(sig("made"), 1)
            pool.wait_ge(sig("made"), 7)
            for t, op, fill in ((ident, ALU.not_equal, 1.0), (below, ALU.is_gt, 0.0), (upto, ALU.is_ge, 0.0)):
                pool.affine_select(out=t[:, :], in_=t[:, :], compare_op=op, fill=fill, base=0,
                                   pattern=[[1, P]], channel_multiplier=-1).then_inc(sig("made"), 1)

            def scatter(s, table, bound, source):
                def send(b, n, waits):
                    for name, value in waits:
                        pool.wait_ge(sig(name), value)
                    pool.sem_inc(sig("pool_pace"), 1)
                    for u in range(n):
                        pool.indirect_dma_start(
                            table, bass.IndirectOffsetOnAxis(ap=idx_ring[:, b, u:u + 1], axis=0), source(b, u), None,
                            bounds_check=bound, oob_is_err=False).then_inc(sig(f"sent{b}"), 16)

                def waits(b, i):
                    w = [(f"staged{b}", ORDER[s] * (SB // 2 + 1) + i + 1)]
                    return w + [(f"attr{b}", 16 * (i + 1))] * (s == "src")

                def pair(i, first, last):
                    for b in range(2):
                        send(b, SU, waits(b, i))

                peeled(pool, SB // 2, pair)
                send(0, SU, waits(0, SB // 2))
                send(1, 2, waits(1, SB // 2))

            pool.wait_ge(sig("src_prefilled"), 1)
            scatter("src", by_src, SLOTS - 1, lambda b, u: ring_e[:, b, u, 0:EW])
            scatter("low", by_low, P * COLS - 1, lambda b, u: pair_ring[:, b, u, :])
            pool.wait_ge(sig("dst_prefill"), 16)
            scatter("dst", by_dst, SLOTS - 1, lambda b, u: pair_ring[:, b, u, :])

            def gather(s, table, width, freed):
                def pair(i, first, last):
                    for b in range(2):
                        pool.wait_ge(sig(f"idx{b}"), PASS[s] * (NB // 2) + i + 1)
                        if not first:
                            pool.wait_ge(sig(freed), PASS[s] * ST + U * (2 * i + b - 1) if freed == "sum" else 2 * i + b - 1)
                        pool.sem_inc(sig("pool_pace"), 1)
                        for u in range(U):
                            pool.indirect_dma_start(
                                ring_x[:, b, u, 0:width], None, table,
                                bass.IndirectOffsetOnAxis(ap=idx_ring[:, b, u:u + 1], axis=0)
                            ).then_inc(sig(f"got{b}"), 16)

                peeled(pool, NB // 2, pair)

            gather("p1", x, D, "sum")
            pool.wait_ge(sig("operand"), NG)
            pool.memset(acc1[:, :, 0, 0:D], 0.0).then_inc(sig("sums_cleared"), 1)
            pool.wait_ge(sig("d0_stored"), 16 * NG)
            gather("p2", h1_tab, D, "sum")
            pool.wait_ge(sig("d1_stored"), 32 * NG)
            gather("p3", p2_tab, W2, "p3_msg")
            pool.wait_ge(sig("d2_stored"), 32 * NG)
            gather("p5", p3_tab, W3, "sum")

        @block.scalar
        def _(act):
            def copy(dst, src):
                return act.activation(dst, src, ACT.Copy)

            def stage(s, parts):
                act.wait_ge(sig("placed"), 3 * (KEYS[s] + (NT if s != "low" else P)))

                def put(b, c, n):
                    for dst, src in parts(b, c, n):
                        copy(dst, src)
                    copy(idx_ring[:, b, 0:n], place[:, bass.ds(c, n)]).then_inc(sig(f"staged{b}"), 1)

                def pair(i, first, last):
                    for b in range(2):
                        if not first:
                            act.wait_ge(sig(f"sent{b}"), sent(s, b, i))
                        put(b, (2 * i + b) * SU, SU)

                peeled(act, SB // 2, pair)
                for b, n in ((0, SU), (1, 2)):
                    act.wait_ge(sig(f"sent{b}"), sent(s, b, SB // 2))
                    put(b, (SB - 1 + b) * SU, n)

            stage("src", lambda b, c, n: [(ring_e[:, b, 0:n, 0], seg[:, bass.ds(c, n)]),
                                          (ring_e[:, b, 0:n, 1], other[:, bass.ds(c, n)])])
            for s in ("low", "dst"):
                prev = "src" if s == "low" else "low"
                for b in range(2):
                    act.wait_ge(sig(f"sent{b}"), sent(prev, b))
                stage(s, lambda b, c, n: [(pair_ring[:, b, 0:n, :], pair_i[:, bass.ds(c, n), :])])
            for b in range(2):
                act.wait_ge(sig(f"sent{b}"), sent("dst", b))

            def indices(s, idx, extra=None):
                def pair(i, first, last):
                    for b in range(2):
                        if not first:
                            act.wait_ge(sig(f"got{b}"), got(s, i))
                        c = (2 * i + b) * U
                        if extra is not None:
                            extra(i, b, c)
                        copy(idx_ring[:, b, 0:U], idx[:, bass.ds(c, U)]).then_inc(sig(f"idx{b}"), 1)
                return pair

            def p1_pair(i, first, last):
                for b in range(2):
                    act.wait_ge(sig(f"p1_rows{b}"), 16 * (i + 1))
                    if not first:
                        act.wait_ge(sig(f"got{b}"), got("p1", i))
                    c = (2 * i + b) * U
                    copy(idx_ring[:, b, 0:U], ring_e[:, b, 0:U, 1])
                    copy(seg_a[:, bass.ds(c, U)], ring_e[:, b, 0:U, 0]).then_inc(sig(f"segs{b}"), 1)
                    copy(idx_a[:, bass.ds(c, U)], ring_e[:, b, 0:U, 1]).then_inc(sig(f"idx{b}"), 1)

            peeled(act, NB // 2, p1_pair)

            def ln_sqrt(s, g):
                act.wait_ge(sig("ln_var"), nth(NORM, s, g) + 1)
                act.activation(sd[:, 1, :], sd[:, 0, :], ACT.Sqrt).then_inc(sig("ln_sqrt"), 1)

            def ln_apply(s, g, dst, src):
                act.wait_ge(sig("ln_rstd"), nth(NORM, s, g) + 1)
                for t in range(G):
                    a = act.activation(dst[:, t, :], src(t), ACT.Identity, bias=sd[:, 3, t:t + 1], scale=sd[:, 2, t:t + 1])
                a.then_inc(sig("ln_normed"), 1)

            def take_t(s, g, n, dst):
                act.wait_ge(sig("turned"), nth(TURN, s, g) + 1)
                for c in range(0, n, 512):
                    m = min(512, n - c)
                    a = copy(dst[:, c:c + m], psf[:, c:c + m])
                a.then_inc(sig("taken"), 1)

            pt = lambda t: psf[:, 4 * 512 + t * D:4 * 512 + (t + 1) * D]

            with act.Fori(0, NG) as g:
                take_t("d0a", g, 2 * G * P, op_t)
                ln_sqrt("d0a", g)
                ln_apply("d0a", g, ub, pt)
                act.wait_ge(sig("d0_affine"), g + 1)
                act.activation(ub[:, :, :], ub[:, :, :], ACT.Silu).then_inc(sig("result"), 1)

            for b in range(2):
                act.wait_ge(sig(f"idx{b}"), NB // 2)
            peeled(act, NB // 2, indices("p2", idx_a))

            with act.Fori(0, NG) as g:
                take_t("d1a", g, 2 * G * P, op_t)
                ln_sqrt("d1a", g)
                ln_apply("d1a", g, ub, pt)
                act.wait_ge(sig("d1_affine"), g + 1)
                act.activation(ub[:, :, :], ub[:, :, :], ACT.Silu).then_inc(sig("d1_silu"), 1)
                ln_sqrt("d1b", g)
                ln_apply("d1b", g, ub, lambda t: ub[:, t, :])
                take_t("d1c", g, 4 * G * P, op_t)
                act.wait_ge(sig("d1_hidden"), g + 1)
                for m in range(4):
                    for h in range(2):
                        n = G * P // 2
                        act.activation(hid_t[:, m * G * P + h * n:m * G * P + (h + 1) * n], ps[:, 2 * m + h, 0:n],
                                       ACT.Silu, bias=lb1s[:, m:m + 1]).then_inc(sig("d1_hid_t"), 1)
                ln_sqrt("d1d", g)
                ln_apply("d1d", g, xin2, pt)
                ln_sqrt("d1e", g)
                ln_apply("d1e", g, xin, lambda t: xin2[:, t, :])
                take_t("d1f", g, 2 * G * P, op_t)
                act.wait_ge(sig("d1_proj"), g + 1)
                copy(prj2[:, :, 0:C2], psf[:, 4 * 512:4 * 512 + G * C2].rearrange("p (t w) -> p t w", w=C2))\
                    .then_inc(sig("d1_projc"), 1)
                act.wait_ge(sig("d1_projt"), g + 1)
                for c, m in ((0, 512), (512, G * P - 512)):
                    copy(hot_t[0:C2, :, :].rearrange("p a b -> p (a b)")[:, c:c + m], psf[0:C2, c:c + m])\
                        .then_inc(sig("d1_projtc"), 1)

            def p3_idx(i, b, first):
                if not first:
                    act.wait_ge(sig(f"got{b}"), got("p3", i))
                copy(idx_ring[:, b, 0:U], idx_a[:, bass.ds((2 * i + b) * U, U)]).then_inc(sig(f"idx{b}"), 1)

            def p3_turn(i, b, first):
                j = 2 * i + b
                act.wait_ge(sig("p3_hot_t"), j + 1)
                if not (first and b == 0):
                    act.wait_ge(sig("p3_el"), j)
                for h in range(2):
                    copy(hot_t[:, 4 * h:4 * h + 4, :].rearrange("p a b -> p (a b)"), ps[:, 4 + h, :])\
                        .then_inc(sig("p3_hot_tc"), 1)

            def p3_exp(i, b, first):
                j = 2 * i + b
                act.wait_ge(sig("p3_leaky"), j + 1)
                if not first:
                    act.wait_ge(sig("sum"), PASS["p3"] * ST + U * (j - 1))
                act.activation(mring[:, b, :, D:D + H2], zl[:, 1], ACT.Exp).then_inc(sig("p3_exp"), 1)

            def p3_pair(i, first, last):
                for b in range(2):
                    p3_idx(i, b, first)
                    p3_turn(i, b, first)
                    p3_exp(i, b, first)

            peeled(act, NB // 2, p3_pair)

            with act.Fori(0, NG) as g:
                act.wait_ge(sig("d2_low"), g + 1)
                act.activation(xin2[:, :, :], xin2[:, :, :], ACT.Exp).then_inc(sig("d2_exp"), 1)
                ln_sqrt("d2a", g)
                ln_apply("d2a", g, xin, lambda t: ub[:, t, :])
                take_t("d2b", g, 2 * G * P, op_t)
                act.wait_ge(sig("d2_proj"), g + 1)
                for t in range(G):
                    a = copy(prj3[:, t, 0:D], pt(t))
                a.then_inc(sig("d2_projc"), 1)

            def p5_pair(i, first, last):
                for b in range(2):
                    j = 2 * i + b
                    if not first:
                        act.wait_ge(sig(f"got{b}"), got("p5", i))
                    copy(idx_ring[:, b, 0:U], idx_b[:, bass.ds(j * U, U)]).then_inc(sig(f"idx{b}"), 1)
                    if not (first and b == 0):
                        act.wait_ge(sig("p5_rows_t"), j)
                    copy(cmp[:, 1, :].rearrange("p (u h) -> p u h", h=H3),
                         seg_b[:, bass.ds(j * U, U)].unsqueeze(2).broadcast_to([P, U, H3])).then_inc(sig("p5_cmp"), 1)
                    act.wait_ge(sig(f"got{b}"), got("p5", i + 1))
                    copy(cmp[:, 0, :].rearrange("p (u h) -> p u h", h=H3), ring_x[:, b, :, D:W3]).then_inc(sig("p5_cmp"), 1)
                    act.wait_ge(sig("p5_hot_t"), j + 1)
                    for h in range(2):
                        copy(hot_t[:, 4 * h:4 * h + 4, :].rearrange("p a b -> p (a b)"), ps[:, 4 + h, :])\
                            .then_inc(sig("p5_hot_tc"), 1)
                    act.wait_ge(sig("p5_rows_t"), j + 1)
                    copy(rowsb[:, :, :], ps[0:U * H3, 6, 0:2 * P].rearrange("p (a e) -> p a e", a=2)).then_inc(sig("p5_rows_c"), 1)
                    act.wait_ge(sig("p5_top_t"), j + 1)
                    copy(svt[:, :, 0:H3], ps[:, 6, 256:256 + U * H3].rearrange("p (u h) -> p u h", h=H3)).then_inc(sig("p5_top_c"), 1)
                    act.wait_ge(sig("p5_spread"), j + 1)
                    copy(ees[:, :, :], ps[:, 7, 128:128 + U * 2 * H3].rearrange("p (u h) -> p u h", h=2 * H3)).then_inc(sig("p5_spread_c"), 1)
                    act.wait_ge(sig("p5_fade"), j + 1)
                    act.activation(resc[:, 3, 0, :], resc[:, 2, 0, :], ACT.Exp).then_inc(sig("p5_fade_e"), 1)
                    act.wait_ge(sig("p5_logit"), j + 1)
                    act.activation(ring_x[:, b, :, D:W3], zz[:, 2], ACT.Exp).then_inc(sig("p5_exp"), 1)

            peeled(act, NB // 2, p5_pair)

            with act.Fori(0, NG) as g:
                act.wait_ge(sig("d3_logit"), g + 1)
                act.activation(self_t[:, 5], self_t[:, 4], ACT.Exp).then_inc(sig("d3_exp"), 1)
                ln_sqrt("d3a", g)
                ln_apply("d3a", g, ub, lambda t: ub[:, t, :])
                ln_sqrt("d3b", g)
                ln_apply("d3b", g, ub, lambda t: xin2[:, t, :])
                act.wait_ge(sig("ln_normed"), nth(NORM, "d3b", g) + 1)
                act.sem_inc(sig("result"), 1)

        @block.vector
        def _(dve):
            own = {"base": 0, "i": 0, "per": 0, "n": 0}

            def step(ins):
                ins.then_inc(sig("v_step"), 1)
                own["n"] += 1
                dve.wait_ge(sig("v_step"), own["i"] * own["per"] + (own["base"] + own["n"]))

            def groups(per, body):
                own.update(base=own["base"] + own["n"], per=per, n=0)
                with dve.Fori(0, NG) as g:
                    own["i"] = g
                    body(g)
                    assert own["n"] == per, own["n"]
                own.update(base=own["base"] + NG * per, i=0, per=0, n=0)

            def hold():
                dve.sem_inc(sig("v_pace"), 1)

            def copy(dst, src):
                return dve.tensor_copy(dst, src)

            def ts(dst, src, s1, s2, o1, o2=None):
                return dve.tensor_scalar(out=dst, in0=src, scalar1=s1, scalar2=s2, op0=o1, **({"op1": o2} if o2 is not None else {}))

            def tt(dst, a, b, op):
                return dve.tensor_tensor(out=dst, in0=a, in1=b, op=op)

            def stt(dst, a, s, b, o1, o2):
                return dve.scalar_tensor_tensor(out=dst, in0=a, scalar=s, in1=b, op0=o1, op1=o2)

            dve.memset(ring_e[:, :, :, :], 1.0).then_inc(sig("cleared"), 1)
            dve.memset(ring_x[:, :, :, :], 0.0).then_inc(sig("cleared"), 1)
            dve.memset(none_i, -1).then_inc(sig("cleared"), 1)
            dve.memset(zero, 0.0).then_inc(sig("cleared"), 1)
            dve.wait_ge(sig("cleared"), 4)
            dve.wait_ge(sig("loaded"), 16 * LOADS)
            dve.wait_ge(sig("made"), 10)

            def order(s, nb, padded, tile_of, last_of):
                step(dve.memset(place, float(2 * SLOTS)))
                with dve.Fori(0, nb) as k:
                    dve.tensor_scalar(out=mask, in0=key, scalar1=lane[:, bass.ds(k, 1)], scalar2=None, op0=ALU.is_equal,
                                      op1=ALU.add, accum_out=counts[:, bass.ds(k, 1)]).then_inc(sig("counted"), 1)
                    dve.wait_ge(sig("counted"), k + (KEYS[s] + 1))
                dve.wait_ge(sig("total"), ORDER[s] + 1)
                if padded:
                    step(ts(small_i[0:NT, 0:1], ps[0:NT, 7, 0:1], float(P - 1), None, ALU.add))
                    step(ts(small_i[0:NT, 1:2], small_i[0:NT, 0:1], 7, None, ALU.logical_shift_right))
                    step(copy(small[0:NT, 1:2], small_i[0:NT, 1:2]))
                    ts(spread[0:NT, :], ones[0:NT, :], small[0:NT, 1:2], float(P), ALU.mult, ALU.mult).then_inc(sig("spread"), 1)
                else:
                    ts(spread[:, :], ones[:, :], ps[:, 7, 0:1], None, ALU.mult).then_inc(sig("spread"), 1)
                dve.wait_ge(sig("start"), ORDER[s] + 1)
                step(ts(start_m1[:, 0:nb], ps[:, 7, 128:128 + nb], -1.0, None, ALU.add))
                if padded:
                    step(copy(small[0:NT, 2:3], ps[0:NT, 7, 8:9]))
                    if last_of is not None:
                        step(ts(last_of[0:1, :], ps[0:1, 7, 16:16 + NT], -1.0, 0.0, ALU.add, ALU.max))
                    ts(reach, slot_no, small[0:NT, 2:3], None, ALU.is_ge).then_inc(sig("reach"), 1)
                    dve.wait_ge(sig("cover"), (ORDER[s] + 2) // 2)
                    for h in range(2):
                        step(ts(tile_of[0:1, h * HALF:(h + 1) * HALF], ps[0:1, 5 + h, 0:HALF], -1.0, None, ALU.add))
                        step(ts(seg_off[:, h * HALF:(h + 1) * HALF], ps[:, 5 + h, 0:HALF], -float(P), float(P + 1), ALU.mult, ALU.add))
                    dve.sem_inc(sig(f"{s}_tables"), 1)
                with dve.Fori(0, nb) as k:
                    done = 3 * k + 3 * KEYS[s]
                    ts(mask, key, lane[:, bass.ds(k, 1)], None, ALU.is_equal).then_inc(sig("placed"), 1)
                    dve.wait_ge(sig("placed"), done + 1)
                    dve.tensor_tensor_scan(out=rank, data0=mask, data1=zero, initial=start_m1[:, bass.ds(k, 1)],
                                           op0=ALU.add, op1=ALU.add).then_inc(sig("placed"), 1)
                    dve.wait_ge(sig("placed"), done + 2)
                    hold()
                    dve.copy_predicated(place, mask.bitcast(U32), rank).then_inc(sig("placed"), 1)
                    dve.wait_ge(sig("placed"), done + 3)

            step(ts(tmp_i, src_i, 7, None, ALU.logical_shift_right))
            step(copy(key, tmp_i))
            step(copy(seg, src_i))
            step(stt(seg, key, -float(P), seg, ALU.mult, ALU.add))
            step(ts(seg, seg, 1.0, None, ALU.add))
            step(copy(other, dst_i))
            order("src", NT, True, tile_a, last_a)

            step(ts(tmp_i, dst_i, P - 1, None, ALU.bitwise_and))
            for b in range(2):
                dve.wait_ge(sig(f"sent{b}"), sent("src", b))
            step(copy(key, tmp_i))
            step(copy(pair_i[:, :, 0], dst_i))
            step(copy(pair_i[:, :, 1], src_i))
            order("low", P, False, None, None)

            for b in range(2):
                dve.wait_ge(sig(f"sent{b}"), sent("low", b))
            dve.wait_ge(sig("low_back"), 16)
            step(ts(tmp_i, pair_i[:, :, 0], 7, None, ALU.logical_shift_right))
            step(copy(key, tmp_i))
            order("dst", NT, True, tile_b, None)

            dve.wait_ge(sig("dst_back"), 16 * RB)
            step(dve.memset(dst_rowf, 0.0))
            for w in range(2):
                step(copy(dst_rowf[:, 0:RB - 1, w, :], dst_rows[:, 0:RB - 1, :, w]))
                n = ST - (RB - 1) * P
                step(copy(dst_rowf[0:n, RB - 1, w, :], dst_rows[0:n, RB - 1, :, w]))
            dve.sem_inc(sig("dst_rowf"), 1)
            dve.wait_ge(sig("dst_cols"), 1)
            step(tt(seg_b[:, :], psf[:, 0:ST], seg_off, ALU.add))
            step(ts(idx_b[:, :], psf[:, 1024:1024 + ST], 0.0, None, ALU.max))

            def clear(n):
                step(dve.memset(acc[:, 0:n], 0.0))

            clear(NT * ACC1)

            def one_hot(s, seg_of, j, b):
                tt(hot[:, b], lane1[:, :].unsqueeze(1).broadcast_to([P, U, P]),
                   seg_of[:, bass.ds(j * U, U)].unsqueeze(2).broadcast_to([P, U, P]), ALU.is_equal).then_inc(sig("hot"), 1)

            def tiles_of(eng, table, j):
                return [eng.value_load(table[0:1, bass.ds(j * U + u, 1)], min_val=0, max_val=NT - 1) for u in range(U)]

            def add_sums(s, j, first, table, width, both=False, k=None):
                k = k or tiles_of(nc.vector, table, j)
                for u in range(U):
                    dve.wait_ge(sig("sum"), j * U + (PASS[s] * ST + u + 1))
                    if not (first and u == 0):
                        dve.wait_ge(sig("add"), j * U + (PASS[s] * ST + u))
                    if both:
                        a = acc[:, bass.ds(k[u] * ACC1, ACC1)].rearrange("p (a w) -> p a w", a=2)
                        q = ps[:, 2 * (u % 4):2 * (u % 4) + 2, 0:D + 1]
                    elif width == D:
                        a, q = acc[:, bass.ds(k[u] * ACC1, D)], ps[:, u % 4, 0:D]
                    else:
                        a, q = acc[:, bass.ds(k[u] * width, width)], ps[:, u % 4, 0:width]
                    tt(a, a, q, ALU.add).then_inc(sig("add"), 1)

            def sum_pass(s, both):
                def hots(i, b):
                    if both:
                        dve.wait_ge(sig(f"segs{b}"), i + 1)
                    one_hot(s, seg_a, 2 * i + b, b)

                def pair(i, first, last):
                    hots(i, 1)
                    add_sums(s, 2 * i, first, tile_a, D, both)
                    if not last:
                        hots(i + 1, 0)
                    add_sums(s, 2 * i + 1, False, tile_a, D, both)

                hots(0, 0)
                peeled(dve, NB // 2, pair)

            def ln_stats(s, g, src):
                for t in range(G):
                    m = dve.bn_stats(stat[:, t, :], src(t))
                step(m)
                hold()
                for t in range(G):
                    m = dve.bn_aggr(mv[:, t, :], stat[:, t, :])
                step(m)
                ts(sd[:, 0, :], mv[:, :, 1], EPS, None, ALU.add).then_inc(sig("ln_var"), 1)
                dve.wait_ge(sig("ln_sqrt"), nth(NORM, s, g) + 1)
                step(dve.reciprocal(sd[:, 2, :], sd[:, 1, :]))
                stt(sd[:, 3, :], mv[:, :, 0], -1.0, sd[:, 2, :], ALU.mult, ALU.mult).then_inc(sig("ln_rstd"), 1)

            def over(v):
                return vec[:, v:v + 1, :].broadcast_to([P, G, D])

            def affine(s, g, buf, gamma, beta, ready):
                dve.wait_ge(sig("ln_normed"), nth(NORM, ready, g) + 1)
                step(tt(buf, buf, over(gamma), ALU.mult))
                return tt(buf, buf, over(beta), ALU.add)

            pt = lambda t: psf[:, 4 * 512 + t * D:4 * 512 + (t + 1) * D]

            sum_pass("p1", True)
            deg = acc[:, :].rearrange("p (k w) -> p k w", w=ACC1)[:, :, ACC1 - 1]
            dve.wait_ge(sig("add"), ST)
            step(ts(rdeg[:, :], deg, 1.0, None, ALU.max))
            step(dve.reciprocal(rdeg[:, :], rdeg[:, :]))

            def layer_in(s, g):
                for t in range(G):
                    k = g * G + t
                    a = acc[:, bass.ds(k * ACC1, D)]
                    m = stt(ub[:, t, :], a, rdeg[:, bass.ds(k, 1)], xin[:, t, :], ALU.mult, ALU.add)
                m.then_inc(sig("operand"), 1)

            def first_layer(g):
                dve.wait_ge(sig("d0_in"), 16 * (g + 1))
                layer_in("d0", g)
                dve.wait_ge(sig("d0_mm"), g + 1)
                ln_stats("d0a", g, pt)
                affine("d0", g, ub[:, :, :], V_G0, V_BE0, "d0a").then_inc(sig("d0_affine"), 1)

            dve.sem_inc(sig("free"), 1)
            groups(4, first_layer)
            dve.wait_ge(sig("sums_cleared"), 1)

            sum_pass("p2", False)
            dve.wait_ge(sig("add"), 2 * ST)
            def second_layer(g):
                dve.wait_ge(sig("d1_in"), 32 * (g + 1))
                layer_in("d1", g)
                dve.wait_ge(sig("operand"), NG + g + 1)
                hold()
                copy(xin[:, :, :], acc[:, bass.ds(g * (G * ACC1), G * ACC1)].rearrange("p (t w) -> p t w", w=ACC1)
                     [:, :, D + 1:2 * D + 1]).then_inc(sig("d1_edges"), 1)
                dve.wait_ge(sig("d1_mm"), g + 1)
                ln_stats("d1a", g, pt)
                affine("d1", g, ub[:, :, :], V_G1, V_BE1, "d1a").then_inc(sig("d1_affine"), 1)
                dve.wait_ge(sig("d1_silu"), g + 1)
                step(tt(ub[:, :, :], ub[:, :, :], xin2[:, :, :], ALU.add))
                ln_stats("d1b", g, lambda t: ub[:, t, :])
                dve.wait_ge(sig("d1_mm2"), g + 1)
                ln_stats("d1d", g, pt)
                step(affine("d1g", g, xin2[:, :, :], V_LGA, V_LBE, "d1d"))
                step(tt(xin2[:, :, :], xin2[:, :, :], ub[:, :, :], ALU.add))
                step(tt(xin2[:, :, :], xin2[:, :, :], ub[:, :, :], ALU.add))
                ln_stats("d1e", g, lambda t: xin2[:, t, :])
                dve.wait_ge(sig("d1_elr"), g + 1)
                hold()
                lr = psf[:, 6 * 512:6 * 512 + G * 2 * H2].rearrange("p (t w) -> p t w", w=2 * H2)
                step(copy(el[:, bass.ds(g * (G * H2), G * H2)].rearrange("p (t w) -> p t w", w=H2), lr[:, :, 0:H2]))
                copy(prj2[:, :, C2:W2], lr[:, :, H2:2 * H2]).then_inc(sig("result"), 1)

            dve.sem_inc(sig("free"), 1)
            groups(4 * 3 + 1 + 1 + 1 + 3 + 1, second_layer)
            dve.wait_ge(sig("d1_stored"), 32 * NG)
            clear(NT * ACC2)

            def p3_messages(i, b, first):
                j = 2 * i + b
                dve.wait_ge(sig("p3_el"), j + 1)
                dve.wait_ge(sig(f"got{b}"), got("p3", i + 1))
                tt(zl[:, 0], ps[:, 6 + b, 0:U * H2].rearrange("p (u h) -> p u h", h=H2), ring_x[:, b, :, C2:W2], ALU.add)\
                    .then_inc(sig("p3_z"), 1)
                dve.wait_ge(sig("p3_z"), j + 1)
                stt(zl[:, 1], zl[:, 0], 0.2, zl[:, 0], ALU.mult, ALU.max).then_inc(sig("p3_leaky"), 1)
                dve.wait_ge(sig("p3_exp"), j + 1)
                for u in range(U):
                    m = tt(mring[:, b, u, 0:D].rearrange("p (h c) -> p h c", c=C2),
                           ring_x[:, b, u, 0:C2].unsqueeze(1).broadcast_to([P, H2, C2]),
                           mring[:, b, u, D:D + H2].unsqueeze(2).broadcast_to([P, H2, C2]), ALU.mult)
                m.then_inc(sig("p3_msg"), 1)

            def p3_pair(i, first, last):
                one_hot("p3", seg_a, 2 * i + 1, 1)
                add_sums("p3", 2 * i, first, tile_a, ACC2)
                p3_messages(i, 1, first)
                if not last:
                    one_hot("p3", seg_a, 2 * i + 2, 0)
                add_sums("p3", 2 * i + 1, False, tile_a, ACC2)
                if not last:
                    p3_messages(i + 1, 0, False)

            one_hot("p3", seg_a, 0, 0)
            p3_messages(0, 0, True)
            peeled(dve, NB // 2, p3_pair)

            dve.wait_ge(sig("add"), 3 * ST)
            dve.wait_ge(sig("d1_vectors"), 16 * 5)
            def third_layer(g):
                a3 = acc[:, bass.ds(g * (G * ACC2), G * ACC2)].rearrange("p (t w) -> p t w", w=ACC2)
                rs = sd[:, :, :].rearrange("p a b -> p (a b)").rearrange("p (t h) -> p t h", h=H2)
                step(ts(rs, a3[:, :, D:ACC2], 1e-12, None, ALU.max))
                step(dve.reciprocal(rs, rs))
                for t in range(G):
                    m = tt(ub[:, t, :].rearrange("p (h c) -> p h c", c=C2), a3[:, t, 0:D].rearrange("p (h c) -> p h c", c=C2),
                           rs[:, t, :].unsqueeze(2).broadcast_to([P, H2, C2]), ALU.mult)
                step(m)
                ubh = ub[:, :, :].rearrange("p t (h c) -> p (t h) c", c=C2)
                step(tt(ubh, ubh, abv[:, :].unsqueeze(1).broadcast_to([P, G * H2, C2]), ALU.add))
                ts(xin2[:, :, :], ub[:, :, :], 0.0, None, ALU.min).then_inc(sig("d2_low"), 1)
                dve.wait_ge(sig("d2_exp"), g + 1)
                step(stt(ub[:, :, :], ub[:, :, :], 0.0, xin2[:, :, :], ALU.max, ALU.add))
                dve.wait_ge(sig("d2_in"), 16 * (g + 1))
                step(stt(ub[:, :, :], ub[:, :, :], -1.0, xin[:, :, :], ALU.add, ALU.add))
                ln_stats("d2a", g, lambda t: ub[:, t, :])
                dve.wait_ge(sig("d2_projc"), g + 1)
                mag = ma[:, bass.ds(g * (G * 2 * H3), G * 2 * H3)].rearrange("p (t w) -> p t w", w=2 * H3)
                for n, v in enumerate((V_GSRC, V_GDST)):
                    step(tt(ub[:, :, :], prj3[:, :, 0:D], over(v), ALU.mult))
                    step(dve.tensor_reduce(out=mag[:, :, n * H3:(n + 1) * H3],
                                           in_=ub[:, :, :].rearrange("p t (h c) -> p t h c", c=C3), axis=AX, op=ALU.add))
                hold()
                copy(prj3[:, :, D:W3], mag[:, :, 0:H3]).then_inc(sig("result"), 1)

            dve.sem_inc(sig("free"), 1)
            groups(4 + 2 + 3 + 4, third_layer)
            dve.wait_ge(sig("d2_stored"), 32 * NG)
            clear(NT * W3)
            step(dve.memset(lastm[:, :], 1.0))
            step(dve.memset(pen[:, :], -BIG))
            step(dve.memset(svt[:, :, :], 1.0))

            def leaky(dst, src):
                return stt(dst, src, 0.2, src, ALU.mult, ALU.max)

            def p5_pair(i, first, last):
                for b in range(2):
                    j = 2 * i + b
                    n = U * H3

                    def chain(name, ins):
                        ins.then_inc(sig("p5_v"), 1)
                        cnt[0] += 1
                        dve.wait_ge(sig("p5_v"), j * P5_V + cnt[0])

                    cnt = [0]
                    one_hot("p5", seg_b, j, b)
                    k = tiles_of(nc.vector, tile_b, j)
                    dve.wait_ge(sig("p5_rows_c"), j + 1)
                    chain("ends", tt(lastm[:, 0:P - 1], rowsb[:, 1, 0:P - 1], rowsb[:, 1, 1:P], ALU.not_equal))
                    chain("pen", ts(pen[:, 1:P], lastm[:, 0:P - 1], -BIG, None, ALU.mult))
                    chain("scan", dve.tensor_tensor_scan(out=scan[:, :], data0=pen[:, :], data1=rowsb[:, 0, :], initial=0.0,
                                                         op0=ALU.add, op1=ALU.max))
                    tt(sv[:, :], scan[:, :], lastm[:, :], ALU.mult).then_inc(sig("p5_top"), 1)
                    dve.wait_ge(sig("p5_max"), j + 1)
                    mx = ps[:, 7, 0:U * (H3 + 1)].rearrange("p (u w) -> p u w", w=H3 + 1)
                    chain("present", ts(present[:, :], mx[:, :, H3], 1.0, -1.0, ALU.min, ALU.add))
                    chain("absent", ts(present[:, :], present[:, :], BIG, None, ALU.mult))
                    chain("cand", tt(cand[:, :, :], mx[:, :, 0:H3], present[:, :].unsqueeze(2).broadcast_to([P, U, H3]), ALU.add))
                    chain("old", copy(mold[:, 0, :], ma[:, bass.ds(k[0] * (2 * H3), 2 * H3)]))
                    for u in range(U):
                        m = ma[:, bass.ds(k[u] * (2 * H3), H3)]
                        chain("max", tt(m, m, cand[:, u, :], ALU.max))
                    dve.sem_inc(sig("p5_newmax"), 1)
                    chain("new", copy(mold[:, 1, :], ma[:, bass.ds(k[0] * (2 * H3), 2 * H3)]))
                    chain("dz", tt(resc[:, 0], mold[:, :, 0:H3], mold[:, :, H3:2 * H3], ALU.add))
                    chain("dl", leaky(resc[:, 1], resc[:, 0]))
                    tt(resc[:, 2, 0, :], resc[:, 1, 0, :], resc[:, 1, 1, :], ALU.subtract).then_inc(sig("p5_fade"), 1)
                    dve.wait_ge(sig("p5_spread_c"), j + 1)
                    tt(zz[:, 0], ees[:, :, H3:2 * H3], ring_x[:, b, :, D:W3], ALU.add).then_inc(sig("p5_v"), 1)
                    cnt[0] += 1
                    chain("zm", tt(zz[:, 1], ees[:, :, H3:2 * H3], ees[:, :, 0:H3], ALU.add))
                    chain("zl", leaky(zz[:, 0:2], zz[:, 0:2]))
                    tt(zz[:, 2], zz[:, 0], zz[:, 1], ALU.subtract).then_inc(sig("p5_logit"), 1)
                    dve.wait_ge(sig("p5_fade_e"), j + 1)
                    a = acc[:, bass.ds(k[0] * W3, D)].rearrange("p (h c) -> p h c", c=C3)
                    chain("fade", tt(a, a, resc[:, 3, 0, :].unsqueeze(2).broadcast_to([P, H3, C3]), ALU.mult))
                    a = acc[:, bass.ds(k[0] * W3 + D, H3)]
                    chain("fade2", tt(a, a, resc[:, 3, 0, :], ALU.mult))
                    dve.wait_ge(sig("p5_exp"), j + 1)
                    for u in range(U):
                        v = ring_x[:, b, u, 0:D].rearrange("p (h c) -> p h c", c=C3)
                        m = tt(v, v, ring_x[:, b, u, D:W3].unsqueeze(2).broadcast_to([P, H3, C3]), ALU.mult)
                    m.then_inc(sig("p5_msg"), 1)
                    add_sums("p5", j, first and b == 0, tile_b, W3, k=k)
                    assert cnt[0] == P5_V, cnt[0]

            P5_V = 3 + 4 + U + 3 + 3 + 2
            peeled(dve, NB // 2, p5_pair)

            dve.wait_ge(sig("add"), 4 * ST)
            def fourth_layer(g):
                a3 = acc[:, bass.ds(g * (G * W3), G * W3)].rearrange("p (t w) -> p t w", w=W3)
                mag = ma[:, bass.ds(g * (G * 2 * H3), G * 2 * H3)].rearrange("p (t w) -> p t w", w=2 * H3)
                dve.wait_ge(sig("d3_in"), 32 * (g + 1))
                step(tt(self_t[:, 0], prj3[:, :, D:W3], mag[:, :, H3:2 * H3], ALU.add))
                step(tt(self_t[:, 1], mag[:, :, 0:H3], mag[:, :, H3:2 * H3], ALU.add))
                step(leaky(self_t[:, 2], self_t[:, 0]))
                step(leaky(self_t[:, 3], self_t[:, 1]))
                tt(self_t[:, 4], self_t[:, 2], self_t[:, 3], ALU.subtract).then_inc(sig("d3_logit"), 1)
                dve.wait_ge(sig("d3_exp"), g + 1)
                step(tt(self_t[:, 6], a3[:, :, D:W3], self_t[:, 5], ALU.add))
                step(dve.reciprocal(self_t[:, 7], self_t[:, 6]))
                for t in range(G):
                    u3 = ub[:, t, :].rearrange("p (h c) -> p h c", c=C3)
                    m = tt(u3, prj3[:, t, 0:D].rearrange("p (h c) -> p h c", c=C3),
                           self_t[:, 5, t, :].unsqueeze(2).broadcast_to([P, H3, C3]), ALU.mult)
                step(m)
                step(tt(ub[:, :, :], ub[:, :, :], a3[:, :, 0:D], ALU.add))
                for t in range(G):
                    u3 = ub[:, t, :].rearrange("p (h c) -> p h c", c=C3)
                    m = tt(u3, u3, self_t[:, 7, t, :].unsqueeze(2).broadcast_to([P, H3, C3]), ALU.mult)
                step(m)
                step(tt(ub[:, :, :], ub[:, :, :], over(V_GB), ALU.add))
                ln_stats("d3a", g, lambda t: ub[:, t, :])
                step(affine("d3", g, ub[:, :, :], V_GGA, V_GBE, "d3a"))
                step(tt(xin2[:, :, :], ub[:, :, :], xin[:, :, :], ALU.add))
                ln_stats("d3b", g, lambda t: xin2[:, t, :])

            dve.sem_inc(sig("free"), 1)
            groups(4 + 2 + 4 + 2 * 3 + 2 + 1, fourth_layer)

        @block.tensor
        def _(pe):
            def mm(dst, lhs, rhs, start=True, stop=True):
                return pe.matmul(dst, lhsT=lhs, rhs=rhs, start=start, stop=stop)

            def hold():
                pe.sem_inc(sig("t_pace"), 1)

            def totals(s, nb, padded):
                pe.wait_ge(sig("counted"), KEYS[s] + nb)
                mm(ps[0:nb, 7, 0:1], counts[:, 0:nb], ones[:, 0:1]).then_inc(sig("total"), 1)
                pe.wait_ge(sig("spread"), ORDER[s] + 1)
                if padded:
                    mm(ps[0:NT, 7, 8:9], below[0:NT, 0:NT], small[0:NT, 1:2])
                    mm(ps[0:1, 7, 16:16 + NT], small[0:NT, 1:2], upto[0:NT, 0:NT])
                mm(ps[:, 7, 128:128 + nb], below[:, :], counts[:, 0:nb], stop=False)
                mm(ps[:, 7, 128:128 + nb], spread[0:nb, :], below[0:nb, 0:nb], start=False).then_inc(sig("start"), 1)
                if padded:
                    pe.wait_ge(sig("reach"), (ORDER[s] + 2) // 2)
                    for h in range(2):
                        m = mm(ps[:, 5 + h, 0:HALF], ones[0:NT, :], reach[:, h * HALF:(h + 1) * HALF])
                    m.then_inc(sig("cover"), 1)

            pe.wait_ge(sig("made"), 10)
            pe.wait_ge(sig("loaded"), 16 * LOADS)
            totals("src", NT, True)
            totals("low", P, False)
            totals("dst", NT, True)
            pe.wait_ge(sig("dst_rowf"), 1)
            for t in range(RB):
                n = min(P, ST - t * P)
                for w in range(2):
                    m = pe.transpose(psf[:, w * 1024 + t * P:w * 1024 + t * P + n], dst_rowf[0:n, t, w, :], ident[0:n, 0:n])
            m.then_inc(sig("dst_cols"), 1)

            def sums(s, j, b, i, first, width, src):
                pe.wait_ge(sig("hot"), j + (PASS[s] * NB + 1))
                for u in range(U):
                    if not (first and u < 4):
                        pe.wait_ge(sig("add"), j * U + (PASS[s] * ST + u - 3))
                    if s == "p1":
                        mm(ps[:, 2 * (u % 4), 0:D + 1], hot[:, b, u, :], ring_x[:, b, u, 0:D + 1])
                        m = mm(ps[:, 2 * (u % 4) + 1, 0:D + 1], hot[:, b, u, :], ring_e[:, b, u, 2:EW + 1])
                    else:
                        m = mm(ps[:, u % 4, 0:width], hot[:, b, u, :], src(b, u))
                    m.then_inc(sig("sum"), 1)

            def sum_pass(s, width, src):
                def pair(i, first, last):
                    for b in range(2):
                        pe.wait_ge(sig(f"got{b}"), got(s, i + 1))
                        if s == "p1":
                            pe.wait_ge(sig(f"p1_rows{b}"), 16 * (i + 1))
                        sums(s, 2 * i + b, b, i, first and b == 0, width, src)
                peeled(pe, NB // 2, pair)

            def turn(s, g, parts, name):
                for n, v in enumerate(parts):
                    m = pe.transpose(psf[:, n * P:(n + 1) * P], v, ident[:, :])
                m.then_inc(sig("turned"), 1)

            def layer(s, g, wts, row, name):
                pe.wait_ge(sig("operand"), STAGE[s] * NG + g + 1)
                turn(s, g, [ub[:, t, c * P:(c + 1) * P] for t in range(G) for c in range(2)], name)
                pe.wait_ge(sig("taken"), nth(TURN, name, g) + 1)
                for t in range(G):
                    o = psf[:, 4 * 512 + t * D:4 * 512 + (t + 1) * D]
                    mm(o, ones[0:1, :], rows[0:1, row, :], stop=False)
                    for c in range(2):
                        m = mm(o, op_t[:, (2 * t + c) * P:(2 * t + c + 1) * P], wts[:, c, :], start=False, stop=c == 1)
                m.then_inc(sig(f"{s}_mm"), 1)

            sum_pass("p1", D, None)
            with pe.Fori(0, NG) as g:
                layer("d0", g, wsq, 0, "d0a")
            sum_pass("p2", D, lambda b, u: ring_x[:, b, u, 0:D])
            pe.wait_ge(sig("d0_weights"), 16)
            with pe.Fori(0, NG) as g:
                layer("d1", g, wsq, 1, "d1a")
                pe.wait_ge(sig("ln_normed"), nth(NORM, "d1b", g) + 1)
                n = G * P // 2
                blocks = []
                for c in range(2):
                    blocks += [ub[:, t, c * P:(c + 1) * P] for t in range(G)]
                for c in range(2):
                    blocks += [xin[:, t, c * P:(c + 1) * P] for t in range(G)]
                pe.wait_ge(sig("d1_edges"), g + 1)
                turn("d1", g, blocks, "d1c")
                pe.wait_ge(sig("taken"), nth(TURN, "d1c", g) + 1)
                for m_ in range(4):
                    for h in range(2):
                        for c in range(4):
                            m = mm(ps[:, 2 * m_ + h, 0:n], lw1s[:, c, m_ * P:(m_ + 1) * P],
                                   op_t[:, c * G * P + h * n:c * G * P + (h + 1) * n], start=c == 0, stop=c == 3)
                m.then_inc(sig("d1_hidden"), 1)
                pe.wait_ge(sig("d1_hid_t"), 8 * (g + 1))
                for t in range(G):
                    o = psf[:, 4 * 512 + t * D:4 * 512 + (t + 1) * D]
                    mm(o, ones[0:1, :], rows[0:1, 2, :], stop=False)
                    for c in range(4):
                        m = mm(o, hid_t[:, c * G * P + t * P:c * G * P + (t + 1) * P], lw2s[:, c, :], start=False, stop=c == 3)
                m.then_inc(sig("d1_mm2"), 1)
                pe.wait_ge(sig("ln_normed"), nth(NORM, "d1e", g) + 1)
                turn("d1", g, [xin[:, t, c * P:(c + 1) * P] for t in range(G) for c in range(2)], "d1f")
                pe.wait_ge(sig("taken"), nth(TURN, "d1f", g) + 1)
                for t in range(G):
                    for c in range(2):
                        m = mm(psf[:, 4 * 512 + t * C2:4 * 512 + (t + 1) * C2], op_t[:, (2 * t + c) * P:(2 * t + c + 1) * P],
                               aws[:, c, :], start=c == 0, stop=c == 1)
                m.then_inc(sig("d1_proj"), 1)
                pe.wait_ge(sig("d1_projc"), g + 1)
                hold()
                for t in range(G):
                    m = pe.transpose(psf[0:C2, t * P:(t + 1) * P], prj2[:, t, 0:C2], ident[:, :])
                m.then_inc(sig("d1_projt"), 1)
                pe.wait_ge(sig("d1_projtc"), 2 * (g + 1))
                for t in range(G):
                    m = mm(psf[:, 6 * 512 + t * 2 * H2:6 * 512 + (t + 1) * 2 * H2], hot_t[0:C2, t, :], awlrs[:, :])
                m.then_inc(sig("d1_elr"), 1)

            def turn_hots(s, j, b, first):
                pe.wait_ge(sig("hot"), j + (PASS[s] * NB + 1))
                if not first:
                    pe.wait_ge(sig(f"{s}_hot_tc"), 2 * j)
                for u in range(U):
                    m = pe.transpose(ps[:, 4 + u // 4, (u % 4) * P:(u % 4 + 1) * P], hot[:, b, u, :], ident[:, :])
                m.then_inc(sig(f"{s}_hot_t"), 1)

            def tiles_of(table, j):
                return [nc.tensor.value_load(table[0:1, bass.ds(j * U + u, 1)], min_val=0, max_val=NT - 1) for u in range(U)]

            def p3_el(i, b):
                j = 2 * i + b
                k = tiles_of(tile_a, j)
                pe.wait_ge(sig("p3_hot_tc"), 2 * (j + 1))
                for u in range(U):
                    m = mm(ps[:, 6 + b, u * H2:(u + 1) * H2], hot_t[:, u, :], el[:, bass.ds(k[u] * H2, H2)])
                m.then_inc(sig("p3_el"), 1)

            def p3_sums(i, b, first):
                pe.wait_ge(sig("p3_msg"), 2 * i + b + 1)
                sums("p3", 2 * i + b, b, i, first, ACC2, lambda b, u: mring[:, b, u, :])

            def p3_pair(i, first, last):
                turn_hots("p3", 2 * i + 1, 1, False)
                p3_sums(i, 0, first)
                p3_el(i, 1)
                if not last:
                    turn_hots("p3", 2 * i + 2, 0, False)
                p3_sums(i, 1, False)
                if not last:
                    p3_el(i + 1, 0)

            turn_hots("p3", 0, 0, True)
            p3_el(0, 0)
            peeled(pe, NB // 2, p3_pair)

            pe.wait_ge(sig("d1_weights"), 16)
            with pe.Fori(0, NG) as g:
                pe.wait_ge(sig("ln_normed"), nth(NORM, "d2a", g) + 1)
                turn("d2", g, [xin[:, t, c * P:(c + 1) * P] for t in range(G) for c in range(2)], "d2b")
                pe.wait_ge(sig("taken"), nth(TURN, "d2b", g) + 1)
                for t in range(G):
                    for c in range(2):
                        m = mm(psf[:, 4 * 512 + t * D:4 * 512 + (t + 1) * D], op_t[:, (2 * t + c) * P:(2 * t + c + 1) * P],
                               wsq[:, c, :], start=c == 0, stop=c == 1)
                m.then_inc(sig("d2_proj"), 1)

            def p5_pair(i, first, last):
                for b in range(2):
                    j = 2 * i + b
                    head = first and b == 0
                    k = tiles_of(tile_b, j)
                    turn_hots("p5", j, b, head)
                    pe.wait_ge(sig("p5_cmp"), 2 * (j + 1))
                    hold()
                    n = U * H3
                    for w in range(2):
                        m = pe.transpose(ps[0:n, 6, w * P:(w + 1) * P], cmp[:, w, :], ident[:, :])
                    m.then_inc(sig("p5_rows_t"), 1)
                    pe.wait_ge(sig("p5_top"), j + 1)
                    hold()
                    pe.transpose(ps[:, 6, 256:256 + n], sv[:, :], ident[0:n, 0:n]).then_inc(sig("p5_top_t"), 1)
                    pe.wait_ge(sig("p5_top_c"), j + 1)
                    for u in range(U):
                        m = mm(ps[:, 7, u * (H3 + 1):(u + 1) * (H3 + 1)], hot[:, b, u, :], svt[:, u, :])
                    m.then_inc(sig("p5_max"), 1)
                    pe.wait_ge(sig("p5_newmax"), j + 1)
                    pe.wait_ge(sig("p5_hot_tc"), 2 * (j + 1))
                    for u in range(U):
                        m = mm(ps[:, 7, 128 + u * 2 * H3:128 + (u + 1) * 2 * H3], hot_t[:, u, :],
                               ma[:, bass.ds(k[u] * (2 * H3), 2 * H3)])
                    m.then_inc(sig("p5_spread"), 1)
                    pe.wait_ge(sig("p5_msg"), j + 1)
                    sums("p5", j, b, i, head, W3, lambda b, u: ring_x[:, b, u, :])

            peeled(pe, NB // 2, p5_pair)




def kernel(x, src, dst, edge_attr_256, L0_gnn_W0, L0_gnn_b0, L0_gnn_g0, L0_gnn_beta0, L0_gnn_W1, L0_gnn_b1, L0_gnn_g1,
           L0_gnn_beta1, L1_gnn_W1, L1_gnn_b1, L1_gnn_W2, L1_gnn_b2, L1_gnn_gamma, L1_gnn_beta, L2_gnn_W, L2_gnn_Wl,
           L2_gnn_Wr, L2_gnn_b, L3_gnn_W, L3_gnn_att_src, L3_gnn_att_dst, L3_gnn_bias, L3_gnn_gamma, L3_gnn_beta):
    import numpy as np
    import concourse.bacc as bacc
    from concourse.bass_utils import run_bass_kernel_spmd

    def columns(a):
        c = np.full((P, COLS), NODES_UP, np.int32)
        c[:, 0:ROWS] = a[0:ROWS * P].reshape(P, ROWS)
        c[0:TAIL, ROWS] = a[ROWS * P:EDGES]
        return c

    def padded(a):
        c = np.zeros((NODES_UP, D), np.float32)
        c[0:NODES] = a
        return c

    arrays = [
        padded(np.asarray(x)), columns(np.asarray(src)), columns(np.asarray(dst)), np.asarray(edge_attr_256),
        np.asarray(L0_gnn_W0).T, L0_gnn_b0, L0_gnn_g0, L0_gnn_beta0,
        np.asarray(L0_gnn_W1).T, L0_gnn_b1, L0_gnn_g1, L0_gnn_beta1,
        L1_gnn_W1, np.asarray(L1_gnn_b1).reshape(4, P).T, L1_gnn_W2, L1_gnn_b2, L1_gnn_gamma, L1_gnn_beta,
        L2_gnn_W, np.concatenate([np.asarray(L2_gnn_Wl).T, np.asarray(L2_gnn_Wr).T], axis=1), L2_gnn_b,
        L3_gnn_W, np.asarray(L3_gnn_att_src).reshape(-1), np.asarray(L3_gnn_att_dst).reshape(-1),
        L3_gnn_bias, L3_gnn_gamma, L3_gnn_beta,
    ]
    names = ["x", "src", "dst", "edge_attr", "w0t", "b0", "g0", "be0", "w1t", "b1", "g1", "be1", "lw1", "lb1", "lw2",
             "lb2", "lga", "lbe", "aw", "awlr", "ab", "gw", "gsrc", "gdst", "gb", "gga", "gbe"]
    arrays = {f"in_{n}": np.ascontiguousarray(np.asarray(a)) for n, a in zip(names, arrays)}
    nc = bacc.Bacc("TRN2", target_bir_lowering=False, num_devices=1)
    aps = [nc.dram_tensor(n, a.shape, mybir.dt.from_np(a.dtype), kind="ExternalInput").ap() for n, a in arrays.items()]
    out = nc.dram_tensor("out_x", (NODES_UP, D), F32, kind="ExternalOutput").ap()
    gnn_kernel(nc, *aps, out)
    r = run_bass_kernel_spmd(nc, [arrays], core_ids=[0])
    return np.asarray(r.results[0]["out_x"])[0:NODES]
```

```python
import concourse.bass as bass
from concourse import mybir
from contextlib import ExitStack

F32 = mybir.dt.float32
I32 = mybir.dt.int32
U32 = mybir.dt.uint32
I16 = mybir.dt.int16
BF16 = mybir.dt.bfloat16
ALU = mybir.AluOpType
ACT = mybir.ActivationFunctionType
AX = mybir.AxisListType.X

P = 128
NODES = 6250
EDGES = 106250
D = 256
NT = -(-NODES // P)
NODES_UP = NT * P
ST = -(-((EDGES + (P - 1) * NT) // P) // 16) * 16
ST5 = -(-((EDGES + (2 * P - 1) * NT) // (2 * P)) // 8) * 16
SLOTS = ST * P
SLOTS5 = ST5 * P
PAIRS = ST5 // 2
ROWS = EDGES // P
TAIL = EDGES - ROWS * P
COLS = ROWS + 2
SU = 10
SB = ROWS // SU
EW = 2 + D
ER_W = EW + 2
H2, C2 = 4, 64
H3, C3 = 8, 32
W3 = D + H3
W2 = C2 + H2
ACC1 = 2 * (D + 1)
ACC2 = D + H2
G = 7
NG = NT // G
HALF = ST // 2
CFG = {"p1": (4, 4, ST, 1), "p2": (8, 2, ST, 1), "p3": (8, 2, ST, 1), "p5": (8, 2, ST5, 2)}
U = 8
BIG = 1e30
EPS = 1e-5
assert ROWS == SB * SU and SB % 2 == 1 and NG * G == NT and C2 * H2 == D and C3 * H3 == D


def gnn_kernel(nc, x, src2, dst2, dst_next, dst_tail, pairs, edge_attr, w0t, b0, g0, be0, w1t, b1, g1, be1, lw1, lb1, lw2, lb2, lga, lbe,
               aw, awlr, ab, gw, gsrc, gdst, gb, gga, gbe, out):
    ctx = ExitStack()
    made = {}

    def sb(name, shape, dt=F32):
        return ctx.enter_context(nc.sbuf_tensor(name, shape, dt))

    def sig(name):
        if name not in made:
            made[name] = ctx.enter_context(nc.semaphore(name))
        return made[name]

    def dram(name, shape, dt=F32):
        return nc.dram_tensor(name, shape, dt, kind="Internal").ap()

    by_src = dram("by_src", (SLOTS, EW))
    by_low = dram("by_low", (P * COLS, 2), I32)
    by_dst = dram("by_dst", (SLOTS5, 2), I32)
    h1_tab = dram("h1_tab", (NODES_UP, D))
    x2_tab = dram("x2_tab", (NODES_UP, D))
    p2_tab = dram("p2_tab", (NODES_UP, W2))
    x3_tab = dram("x3_tab", (NODES_UP, D))
    p3_tab = dram("p3_tab", (NODES_UP, W3))

    with ctx:
        acc = sb("acc", [P, NT * ACC1])

        def space(n, dt=F32, wide=1):
            v = acc[:, n * COLS:(n + wide) * COLS]
            return v if dt is F32 else v.bitcast(dt)

        key, seg, other, mask, rank, zero, place = (space(n) for n in range(7))
        src_i, dst_i, tmp_i = (space(n, I32) for n in range(7, 10))
        pair_i = space(10, I32, 2).rearrange("p (c w) -> p c w", w=2)
        reach = acc[0:NT, 14 * COLS:14 * COLS + ST]
        slot_no = acc[0:NT, 16 * COLS:16 * COLS + ST]
        next_i = space(18, I32)[:, 0:ROWS]
        tail_i = space(19, I32)[0:1, 0:TAIL]
        RB = -(-ST5 // P)
        LATE = NT * ACC1 - 4 * RB * P
        dst_rows = acc[:, LATE:LATE + RB * 2 * P].bitcast(I32).rearrange("p (t e w) -> p t e w", t=RB, w=2)
        dst_rowf = acc[:, LATE + RB * 2 * P:LATE + RB * 4 * P].rearrange("p (t w e) -> p t w e", t=RB, w=2)
        assert LATE >= NT * ACC2 and 26 * COLS + 6 * P <= NT * ACC1

        ring_e = sb("ring_e", [P, 2 * SU, ER_W])
        ring_x = sb("ring_x", [P, 16, W3])
        hot = sb("hot", [P, 16, P])
        hot_t = sb("hot_t", [P, U, P])
        idx_ring = sb("idx_ring", [P, 2 * SU], I32)
        pair_ring = sb("pair_ring", [P, 2 * SU, 2], I32)
        seg_a, seg_b = sb("seg_a", [P, ST], BF16), sb("seg_b", [P, ST5], BF16)
        idx_a, idx_b = sb("idx_a", [P, ST], I16), sb("idx_b", [P, ST5], I16)
        tile_a, tile_b = sb("tile_a", [1, ST], I32), sb("tile_b", [1, PAIRS], I32)
        from_b = hot_t[0:1, :, :].rearrange("p a b -> p (a b)")[:, 0:PAIRS].bitcast(I32)
        seg_off = sb("seg_off", [P, PAIRS])
        flag_i = sb("flag_i", [1, 2], I32)
        last_a = sb("last_a", [1, NT], I32)
        lane = sb("lane", [P, P])
        lane1 = sb("lane1", [P, P])
        ident = sb("ident", [P, P])
        below = acc[:, 26 * COLS:26 * COLS + P]
        upto = acc[:, 26 * COLS + P:26 * COLS + 2 * P]
        ones = sb("ones", [P, P])
        counts = acc[:, 26 * COLS + 2 * P:26 * COLS + 3 * P]
        start_m1 = acc[:, 26 * COLS + 3 * P:26 * COLS + 4 * P]
        small = sb("small", [P, 8])
        small_i = sb("small_i", [P, 8], I32)
        spread = acc[:, 26 * COLS + 4 * P:26 * COLS + 5 * P]
        wsq = sb("wsq", [P, 2, D])
        lw1s = sb("lw1s", [P, 4, 2 * D])
        lw2s = sb("lw2s", [P, 4, D])
        aws = sb("aws", [P, 2, C2])
        awlrs = sb("awlrs", [C2, 2 * H2])
        rows = sb("rows", [1, 3, D])
        lb1s = sb("lb1s", [P, 4])
        vec = sb("vec", [P, 6, D])
        V_G0, V_BE0, V_G1, V_BE1, V_LGA, V_LBE = range(6)
        V_GSRC, V_GDST, V_GB, V_GGA, V_GBE = range(5)
        abv = sb("abv", [P, C2])
        rdeg = sb("rdeg", [P, NT])
        el = sb("el", [P, NT * H2])
        ma = sb("ma", [P, NT * 2 * H3])
        xin2, ub = (sb(n, [P, G, D]) for n in ("xin2", "ub"))
        stat = sb("stat", [P, G, 6])
        mv = sb("mv", [P, G, 2])
        sd = sb("sd", [P, 4, G])
        behind = [NT * W3]

        def tail(parts, n):
            behind[0] += n
            return acc[0:parts, behind[0] - n:behind[0]]

        cmp = tail(P, 2 * U * H3).rearrange("p (a n) -> p a n", a=2)
        rowsb = tail(U * H3, 2 * P).rearrange("p (a n) -> p a n", a=2)
        lastm, pen, scan, sv = (tail(U * H3, P) for _ in range(4))
        svt = tail(P, U * (H3 + 1)).rearrange("p (u h) -> p u h", u=U)
        cand = tail(P, U * H3).rearrange("p (u h) -> p u h", u=U)
        ees = tail(P, U * 2 * H3).rearrange("p (u h) -> p u h", u=U)
        zz = tail(P, 4 * U * H3).rearrange("p (s u h) -> p s u h", s=4, u=U)
        present = sb("present", [P, U])
        mold = sb("mold", [P, 2, 2 * H3])
        resc = sb("resc", [P, 4, 2, H3])
        zl = sb("zl", [P, 2, U, H2])
        ps = ctx.enter_context(nc.psum_tensor("ps", [P, 8, 512], F32))
        psf = ps[:, :, :].rearrange("p a b -> p (a b)")

        acc1 = acc[:, :].rearrange("p (k a w) -> p k a w", a=2, w=D + 1)
        hot_f = hot[:, :, :].rearrange("p b c -> p (b c)")
        ring_ef = ring_e[:, :, :].rearrange("p b c -> p (b c)")
        ring_xf = ring_x[:, :, :].rearrange("p b c -> p (b c)")
        xin = hot_f[:, 0:G * D].rearrange("p (t w) -> p t w", w=D)
        op_t = ring_ef[:, 0:4 * G * P]
        hid_t = ring_xf[:, 0:4 * G * P]
        prj2 = ring_ef[:, 4 * G * P:4 * G * P + G * W2].rearrange("p (t w) -> p t w", w=W2)
        prj3 = ring_xf[:, 0:G * W3].rearrange("p (t w) -> p t w", w=W3)
        mring = ring_ef[:, 0:2 * U * ACC2].rearrange("p (a u w) -> p a u w", a=2, u=U)
        self_t = hot_t[:, :, :].rearrange("p a b -> p (a b)")[:, 0:8 * G * H3].rearrange("p (s t h) -> p s t h", s=8, h=H3)
        none_i = seg_b[:, :].bitcast(I32)
        zero_row = ring_x[:, 0, 0:EW]

        def slot(s, b, u):
            return b * CFG[s][0] + u

        def batches(s):
            return CFG[s][2] // CFG[s][0]

        def earlier(s):
            return [q for q in CFG if q < s]

        def sums_before(s):
            return sum(CFG[q][2] // CFG[q][3] for q in earlier(s))

        def hots_before(s):
            return sum(batches(q) for q in earlier(s))

        def rounds_before(s, b):
            return sum(batches(q) // CFG[q][1] for q in earlier(s) if CFG[q][1] > b)

        def got(s, b, i):
            return sum(16 * CFG[q][0] * (batches(q) // CFG[q][1]) for q in earlier(s) if CFG[q][1] > b) + 16 * CFG[s][0] * i

        def used(s, i, b):
            u, ring, _, unit = CFG[s]
            return (i * ring + (b - ring + 1)) * (u // unit) + sums_before(s)

        ORDER = {"src": 0, "dst_tiles": 1, "low": 2, "dst": 3}
        COUNTED = {"src": 0, "dst_tiles": NT, "low": 2 * NT, "dst": 2 * NT + P}
        PLACED = {"src": 0, "low": NT, "dst": NT + P}
        SENT = {"src": 0, "low": 1, "dst": 2}
        STAGE = {"d0": 0, "d1": 1, "d2": 2, "d3": 3}
        NORM = {"d0a": (0, 1), "d1a": (NG, 4), "d1b": (NG + 1, 4), "d1d": (NG + 2, 4), "d1e": (NG + 3, 4),
                "d2a": (5 * NG, 1), "d3a": (6 * NG, 2), "d3b": (6 * NG + 1, 2)}
        TURN = {"d0a": (0, 1), "d1a": (NG, 3), "d1c": (NG + 1, 3), "d1f": (NG + 2, 3), "d2b": (4 * NG, 1)}

        def nth(of, s, g):
            return g * of[s][1] + of[s][0]

        block = ctx.enter_context(nc.Block())
        LOADS = 4 + 4 + 3 + 3 + 6

        def peeled(eng, n, body):
            body(0, True, False)
            with eng.Fori(1, n - 1) as i:
                body(i, False, False)
            body(n - 1, False, True)

        def sent(s, b, batches=None):
            whole = 16 * (SU * (SB // 2 + 1) if b == 0 else SU * (SB // 2) + 2)
            return SENT[s] * whole + (whole if batches is None else 16 * SU * batches)

        @block.sync
        def _(sp):
            def load(dst, src):
                sp.dma_start(dst, src).then_inc(sig("loaded"), 16)

            load(src_i, src2)
            load(dst_i, dst2)
            load(next_i, dst_next)
            load(tail_i, dst_tail)
            for w, d in ((wsq, w0t), (lw1s, lw1), (lw2s, lw2), (aws, aw)):
                load(w[:, :, :], d.rearrange("(a p) n -> p a n", p=P))
            load(awlrs[:, :], awlr)
            load(lb1s[:, :], lb1)
            load(abv[:, :], ab.partition_broadcast(P))
            for n, d in enumerate((b0, b1, lb2)):
                load(rows[0:1, n, :], d.rearrange("(a n) -> a n", a=1))
            for n, d in enumerate((g0, be0, g1, be1, lga, lbe)):
                load(vec[:, n, :], d.partition_broadcast(P))

            sp.wait_ge(sig("cleared"), 3)
            tiles = by_src.rearrange("(t p) w -> p t w", p=P)
            spare = EDGES // P
            n_pre = 0
            for t in range(spare, ST, G):
                n = min(G, ST - t)
                sp.dma_start(tiles[:, t:t + n, :], ring_x[:, 0:1, 0:EW].broadcast_to([P, n, EW]))\
                  .then_inc(sig("src_prefill"), 16)
                n_pre += 1
            sp.wait_ge(sig("src_prefill"), 16 * n_pre)
            sp.wait_ge(sig("src_tables"), 1)
            with sp.Fori(0, NT) as k:
                last = nc.sync.value_load(last_a[0:1, bass.ds(k, 1)], min_val=0, max_val=ST - 1)
                sp.dma_start(by_src[bass.ds(last * P, P), :], zero_row).then_inc(sig("src_prefill"), 16)
                sp.wait_ge(sig("src_prefill"), 16 * (k + n_pre + 1))
                sp.sem_inc(sig("sp_pace"), 1)
            sp.sem_inc(sig("src_prefilled"), 1)

            attr = edge_attr[0:ROWS * P, :].rearrange("(p c) w -> p c w", c=ROWS)

            def attr_pair(i, first, last):
                for b in range(2):
                    if not first:
                        sp.wait_ge(sig(f"sent{b}"), sent("src", b, i))
                    sp.dma_start(ring_e[:, b * SU:(b + 1) * SU, 2:EW], attr[:, bass.ds((2 * i + b) * SU, SU), :])\
                      .then_inc(sig(f"attr{b}"), 16)

            peeled(sp, SB // 2, attr_pair)
            sp.wait_ge(sig("sent0"), sent("src", 0, SB // 2))
            sp.dma_start(ring_e[:, 0:SU, 2:EW], attr[:, (SB - 1) * SU:SB * SU, :]).then_inc(sig("attr0"), 16)
            sp.wait_ge(sig("sent1"), sent("src", 1, SB // 2))
            sp.dma_start(ring_e[0:TAIL, SU, 2:EW], edge_attr[ROWS * P:EDGES, :]).then_inc(sig("attr1"), 16)

            sp.wait_ge(sig("flagged"), 1)
            with sp.If(nc.sync.value_load(flag_i[0:1, 0:1], min_val=0, max_val=1)):
                sp.dma_start(by_dst.rearrange("(t p e) w -> p t (e w)", p=P, t=4),
                             none_i.unsqueeze(1).broadcast_to([P, 4, SLOTS5 // P // 2])).then_inc(sig("dst_prefill"), 16)
                for b in range(2):
                    sp.wait_ge(sig(f"sent{b}"), sent("low", b))
                sp.dma_start(pair_i, by_low.rearrange("(p c) w -> p c w", c=COLS)).then_inc(sig("low_back"), 16)

            for b in range(2):
                sp.wait_ge(sig(f"sent{b}"), sent("src", b))

            def e_round(i, first, last):
                u, ring = CFG["p1"][0:2]
                for b in range(ring):
                    if not first:
                        sp.wait_ge(sig("sum"), used("p1", i, b))
                    sp.dma_start(ring_e[:, slot("p1", b, 0):slot("p1", b, u), 0:EW],
                                 tiles[:, bass.ds((ring * i + b) * u, u), :]).then_inc(sig(f"p1_rows{b}"), 16)

            peeled(sp, batches("p1") // CFG["p1"][1], e_round)

            def nodes(t, g):
                return t[bass.ds(g * (G * P), G * P), :].rearrange("(t p) w -> p t w", p=P)

            for s, ins, outs in (("d0", [(x, xin)], [(h1_tab, ub)]),
                                 ("d1", [(h1_tab, xin), (x, xin2)], [(x2_tab, xin), (p2_tab, prj2)]),
                                 ("d2", [(x2_tab, xin)], [(x3_tab, xin), (p3_tab, prj3)]),
                                 ("d3", [(x3_tab, xin), (p3_tab, prj3)], [(out, ub)])):
                with sp.Fori(0, NG) as g:
                    sp.wait_ge(sig("free"), STAGE[s] * (NG + 1) + g + 1)
                    for t, s_in in ins:
                        sp.dma_start(s_in[:, :, :] if s_in is not prj3 else s_in, nodes(t, g)).then_inc(sig(f"{s}_in"), 16)
                    sp.wait_ge(sig("result"), STAGE[s] * NG + g + 1)
                    for t, s_out in outs:
                        sp.dma_start(nodes(t, g), s_out[:, :, :]).then_inc(sig(f"{s}_stored"), 16)
                    sp.wait_ge(sig(f"{s}_stored"), 16 * len(outs) * (g + 1))
                    sp.sem_inc(sig("free"), 1)
                if s == "d0":
                    with sp.If(nc.sync.value_load(flag_i[0:1, 1:2], min_val=0, max_val=1)):
                        with sp.Fori(0, PAIRS) as q:
                            at = nc.sync.value_load(from_b[0:1, bass.ds(q, 1)], min_val=0, max_val=EDGES)
                            sp.dma_start(by_dst[bass.ds(q * (2 * P), 2 * P), :], pairs[bass.ds(at, 2 * P), :])\
                              .then_inc(sig("copied"), 16)
                        sp.wait_ge(sig("copied"), 16 * PAIRS)
                if s == "d1":
                    with sp.If(nc.sync.value_load(flag_i[0:1, 0:1], min_val=0, max_val=1)):
                        for b in range(2):
                            sp.wait_ge(sig(f"sent{b}"), sent("dst", b))
                    for t in range(RB):
                        n = min(P, ST5 - t * P)
                        sp.dma_start(dst_rows[0:n, t], by_dst[t * P * P:(t * P + n) * P, :]
                                     .rearrange("(s e) w -> s e w", e=P)).then_inc(sig("dst_back"), 16)
                for w in {"d0": [w1t], "d1": [gw]}.get(s, []):
                    sp.dma_start(wsq[:, :, :], w.rearrange("(a p) n -> p a n", p=P)).then_inc(sig(f"{s}_weights"), 16)
                if s == "d1":
                    for n, d in enumerate((gsrc, gdst, gb, gga, gbe)):
                        sp.dma_start(vec[:, n, :], d.partition_broadcast(P)).then_inc(sig("d1_vectors"), 16)

        @block.gpsimd
        def _(pool):
            pool.iota(lane[:, :], pattern=[[1, P]], base=0, channel_multiplier=0,
                      allow_small_or_imprecise_dtypes=True).then_inc(sig("made"), 1)
            pool.iota(lane1[:, :], pattern=[[1, P]], base=1, channel_multiplier=0,
                      allow_small_or_imprecise_dtypes=True).then_inc(sig("made"), 1)
            pool.iota(slot_no, pattern=[[1, ST]], base=0, channel_multiplier=0,
                      allow_small_or_imprecise_dtypes=True).then_inc(sig("made"), 1)
            for t, v in ((ident, 0.0), (below, 1.0), (upto, 1.0), (ones, 1.0)):
                pool.memset(t[:, :], v).then_inc(sig("made"), 1)
            pool.wait_ge(sig("made"), 7)
            for t, op, fill in ((ident, ALU.not_equal, 1.0), (below, ALU.is_gt, 0.0), (upto, ALU.is_ge, 0.0)):
                pool.affine_select(out=t[:, :], in_=t[:, :], compare_op=op, fill=fill, base=0,
                                   pattern=[[1, P]], channel_multiplier=-1).then_inc(sig("made"), 1)

            def scatter(s, table, bound, source):
                def send(b, n, waits):
                    for name, value in waits:
                        pool.wait_ge(sig(name), value)
                    pool.sem_inc(sig("pool_pace"), 1)
                    for u in range(n):
                        pool.indirect_dma_start(
                            table, bass.IndirectOffsetOnAxis(ap=idx_ring[:, b * SU + u:b * SU + u + 1], axis=0), source(b, u), None,
                            bounds_check=bound, oob_is_err=False).then_inc(sig(f"sent{b}"), 16)

                def waits(b, i):
                    w = [(f"staged{b}", SENT[s] * (SB // 2 + 1) + i + 1)]
                    return w + [(f"attr{b}", 16 * (i + 1))] * (s == "src")

                def pair(i, first, last):
                    for b in range(2):
                        send(b, SU, waits(b, i))

                peeled(pool, SB // 2, pair)
                send(0, SU, waits(0, SB // 2))
                send(1, 2, waits(1, SB // 2))

            pool.wait_ge(sig("src_prefilled"), 1)
            scatter("src", by_src, SLOTS - 1, lambda b, u: ring_e[:, b * SU + u, 0:EW])
            pool.wait_ge(sig("flagged"), 1)
            with pool.If(nc.gpsimd.value_load(flag_i[0:1, 0:1], min_val=0, max_val=1)):
                scatter("low", by_low, P * COLS - 1, lambda b, u: pair_ring[:, b * SU + u, :])
                pool.wait_ge(sig("dst_prefill"), 16)
                scatter("dst", by_dst, SLOTS5 - 1, lambda b, u: pair_ring[:, b * SU + u, :])

            def gather(s, table, width, freed="sum"):
                u_n, ring = CFG[s][0:2]

                def round_(i, first, last):
                    for b in range(ring):
                        pool.wait_ge(sig(f"idx{b}"), i + (rounds_before(s, b) + 1))
                        if not first:
                            pool.wait_ge(sig(freed), used(s, i, b) if freed == "sum" else ring * i + (b - ring + 1))
                        pool.sem_inc(sig("pool_pace"), 1)
                        for u in range(u_n):
                            n = slot(s, b, u)
                            pool.indirect_dma_start(
                                ring_x[:, n, 0:width], None, table,
                                bass.IndirectOffsetOnAxis(ap=idx_ring[:, n:n + 1], axis=0)
                            ).then_inc(sig(f"got{b}"), 16)

                peeled(pool, batches(s) // ring, round_)

            gather("p1", x, D)
            pool.wait_ge(sig("operand"), NG)
            pool.memset(acc1[:, :, 0, 0:D], 0.0).then_inc(sig("sums_cleared"), 1)
            pool.wait_ge(sig("d0_stored"), 16 * NG)
            gather("p2", h1_tab, D)
            pool.wait_ge(sig("d1_stored"), 32 * NG)
            gather("p3", p2_tab, W2, "p3_msg")
            pool.wait_ge(sig("d2_stored"), 32 * NG)
            gather("p5", p3_tab, W3)

        @block.scalar
        def _(act):
            def copy(dst, src):
                return act.activation(dst, src, ACT.Copy)

            def stage(s, parts):
                act.wait_ge(sig("placed"), 3 * (PLACED[s] + (NT if s != "low" else P)))

                def put(b, c, n):
                    for dst, src in parts(b, c, n):
                        copy(dst, src)
                    copy(idx_ring[:, b * SU:b * SU + n], place[:, bass.ds(c, n)]).then_inc(sig(f"staged{b}"), 1)

                def pair(i, first, last):
                    for b in range(2):
                        if not first:
                            act.wait_ge(sig(f"sent{b}"), sent(s, b, i))
                        put(b, (2 * i + b) * SU, SU)

                peeled(act, SB // 2, pair)
                for b, n in ((0, SU), (1, 2)):
                    act.wait_ge(sig(f"sent{b}"), sent(s, b, SB // 2))
                    put(b, (SB - 1 + b) * SU, n)

            stage("src", lambda b, c, n: [(ring_e[:, b * SU:b * SU + n, 0], seg[:, bass.ds(c, n)]),
                                          (ring_e[:, b * SU:b * SU + n, 1], other[:, bass.ds(c, n)])])
            act.wait_ge(sig("flagged"), 1)
            with act.If(nc.scalar.value_load(flag_i[0:1, 0:1], min_val=0, max_val=1)):
                for s, prev in (("low", "src"), ("dst", "low")):
                    for b in range(2):
                        act.wait_ge(sig(f"sent{b}"), sent(prev, b))
                    stage(s, lambda b, c, n: [(pair_ring[:, b * SU:b * SU + n, :], pair_i[:, bass.ds(c, n), :])])
                for b in range(2):
                    act.wait_ge(sig(f"sent{b}"), sent("dst", b))

            def p1_round(i, first, last):
                u, ring = CFG["p1"][0:2]
                for b in range(ring):
                    act.wait_ge(sig(f"p1_rows{b}"), 16 * (i + 1))
                    if not first:
                        act.wait_ge(sig(f"got{b}"), got("p1", b, i))
                    c = (ring * i + b) * u
                    n = slot("p1", b, 0)
                    copy(idx_ring[:, n:n + u], ring_e[:, n:n + u, 1]).then_inc(sig(f"idx{b}"), 1)
                    copy(idx_a[:, bass.ds(c, u)], ring_e[:, n:n + u, 1]).then_inc(sig("kept"), 1)
                    copy(seg_a[:, bass.ds(c, u)], ring_e[:, n:n + u, 0]).then_inc(sig(f"segs{b}"), 1)

            peeled(act, batches("p1") // CFG["p1"][1], p1_round)

            def give_idx(s, idx, i, b, first):
                u, ring = CFG[s][0:2]
                if not first:
                    act.wait_ge(sig(f"got{b}"), got(s, b, i))
                n = slot(s, b, 0)
                copy(idx_ring[:, n:n + u], idx[:, bass.ds((ring * i + b) * u, u)]).then_inc(sig(f"idx{b}"), 1)

            def ln_sqrt(s, g):
                act.wait_ge(sig("ln_var"), nth(NORM, s, g) + 1)
                act.activation(sd[:, 1, :], sd[:, 0, :], ACT.Sqrt).then_inc(sig("ln_sqrt"), 1)

            def ln_apply(s, g, dst, src):
                act.wait_ge(sig("ln_rstd"), nth(NORM, s, g) + 1)
                for t in range(G):
                    a = act.activation(dst[:, t, :], src(t), ACT.Identity, bias=sd[:, 3, t:t + 1], scale=sd[:, 2, t:t + 1])
                a.then_inc(sig("ln_normed"), 1)

            def take_t(s, g, n, dst):
                act.wait_ge(sig("turned"), nth(TURN, s, g) + 1)
                for c in range(0, n, 512):
                    m = min(512, n - c)
                    a = copy(dst[:, c:c + m], psf[:, c:c + m])
                a.then_inc(sig("taken"), 1)

            pt = lambda t: psf[:, 4 * 512 + t * D:4 * 512 + (t + 1) * D]

            with act.Fori(0, NG) as g:
                take_t("d0a", g, 2 * G * P, op_t)
                ln_sqrt("d0a", g)
                ln_apply("d0a", g, ub, pt)
                act.wait_ge(sig("d0_affine"), g + 1)
                act.activation(ub[:, :, :], ub[:, :, :], ACT.Silu).then_inc(sig("result"), 1)

            act.wait_ge(sig("kept"), batches("p1"))

            def p2_round(i, first, last):
                for b in range(CFG["p2"][1]):
                    give_idx("p2", idx_a, i, b, first)

            peeled(act, batches("p2") // CFG["p2"][1], p2_round)

            with act.Fori(0, NG) as g:
                take_t("d1a", g, 2 * G * P, op_t)
                ln_sqrt("d1a", g)
                ln_apply("d1a", g, ub, pt)
                act.wait_ge(sig("d1_affine"), g + 1)
                act.activation(ub[:, :, :], ub[:, :, :], ACT.Silu).then_inc(sig("d1_silu"), 1)
                ln_sqrt("d1b", g)
                ln_apply("d1b", g, ub, lambda t: ub[:, t, :])
                take_t("d1c", g, 4 * G * P, op_t)
                act.wait_ge(sig("d1_hidden"), g + 1)
                for m in range(4):
                    for h in range(2):
                        n = G * P // 2
                        act.activation(hid_t[:, m * G * P + h * n:m * G * P + (h + 1) * n], ps[:, 2 * m + h, 0:n],
                                       ACT.Silu, bias=lb1s[:, m:m + 1]).then_inc(sig("d1_hid_t"), 1)
                ln_sqrt("d1d", g)
                ln_apply("d1d", g, xin2, pt)
                ln_sqrt("d1e", g)
                ln_apply("d1e", g, xin, lambda t: xin2[:, t, :])
                take_t("d1f", g, 2 * G * P, op_t)
                act.wait_ge(sig("d1_proj"), g + 1)
                copy(prj2[:, :, 0:C2], psf[:, 4 * 512:4 * 512 + G * C2].rearrange("p (t w) -> p t w", w=C2))\
                    .then_inc(sig("d1_projc"), 1)
                act.wait_ge(sig("d1_projt"), g + 1)
                for c, m in ((0, 512), (512, G * P - 512)):
                    copy(hot_t[0:C2, :, :].rearrange("p a b -> p (a b)")[:, c:c + m], psf[0:C2, c:c + m])\
                        .then_inc(sig("d1_projtc"), 1)

            def take_hots(s, j):
                act.wait_ge(sig(f"{s}_hot_t"), j + 1)
                for h in range(2):
                    copy(hot_t[:, 4 * h:4 * h + 4, :].rearrange("p a b -> p (a b)"), ps[:, 4 + h, :])\
                        .then_inc(sig(f"{s}_hot_tc"), 1)

            def p3_round(i, first, last):
                for b in range(2):
                    j = 2 * i + b
                    give_idx("p3", idx_a, i, b, first)
                    if not (first and b == 0):
                        act.wait_ge(sig("p3_el"), j)
                    take_hots("p3", j)
                    act.wait_ge(sig("p3_leaky"), j + 1)
                    if not first:
                        act.wait_ge(sig("sum"), used("p3", i, b))
                    act.activation(mring[:, b, :, D:D + H2], zl[:, 1], ACT.Exp).then_inc(sig("p3_exp"), 1)

            peeled(act, batches("p3") // 2, p3_round)

            with act.Fori(0, NG) as g:
                act.wait_ge(sig("d2_low"), g + 1)
                act.activation(xin2[:, :, :], xin2[:, :, :], ACT.Exp).then_inc(sig("d2_exp"), 1)
                ln_sqrt("d2a", g)
                ln_apply("d2a", g, xin, lambda t: ub[:, t, :])
                take_t("d2b", g, 2 * G * P, op_t)
                act.wait_ge(sig("d2_proj"), g + 1)
                for t in range(G):
                    a = copy(prj3[:, t, 0:D], pt(t))
                a.then_inc(sig("d2_projc"), 1)

            def p5_front(j, i, b, first):
                if not first:
                    act.wait_ge(sig("p5_rows_t"), j)
                copy(cmp[:, 1, :].rearrange("p (u h) -> p u h", h=H3),
                     seg_b[:, bass.ds(j * U, U)].unsqueeze(2).broadcast_to([P, U, H3]))
                act.wait_ge(sig(f"got{b}"), got("p5", b, i + 1))
                copy(cmp[:, 0, :].rearrange("p (u h) -> p u h", h=H3), ring_x[:, b * U:(b + 1) * U, D:W3])\
                    .then_inc(sig("p5_cmp"), 1)
                if not first:
                    act.wait_ge(sig("p5_spread"), j)
                take_hots("p5", j)
                act.wait_ge(sig("p5_rows_t"), j + 1)
                if not first:
                    act.wait_ge(sig("p5_top"), j)
                copy(rowsb[:, :, :], ps[0:U * H3, 6, 0:2 * P].rearrange("p (a e) -> p a e", a=2)).then_inc(sig("p5_rows_c"), 1)

            def p5_front_end(j):
                act.wait_ge(sig("p5_top_t"), j + 1)
                copy(svt[:, :, 0:H3], ps[:, 6, 256:256 + U * H3].rearrange("p (u h) -> p u h", h=H3)).then_inc(sig("p5_top_c"), 1)
                act.wait_ge(sig("p5_fade"), j + 1)
                act.activation(resc[:, 3, 0, :], resc[:, 2, 0, :], ACT.Exp).then_inc(sig("p5_fade_e"), 1)
                act.wait_ge(sig("p5_spread"), j + 1)
                copy(ees[:, :, :], ps[:, 7, 128:128 + U * 2 * H3].rearrange("p (u h) -> p u h", h=2 * H3)).then_inc(sig("p5_spread_c"), 1)

            def p5_exp(j, b):
                act.wait_ge(sig("p5_logit"), j + 1)
                act.activation(ring_x[:, b * U:(b + 1) * U, D:W3], zz[:, 2], ACT.Exp).then_inc(sig("p5_exp"), 1)

            def p5_round(i, first, last):
                for b in range(2):
                    j = 2 * i + b
                    more = not (last and b == 1)
                    if b == 0:
                        give_idx("p5", idx_b, i, 1, first)
                    elif more:
                        give_idx("p5", idx_b, i + 1, 0, False)
                    if more:
                        p5_front(j + 1, i + b, 1 - b, False)
                    p5_exp(j, b)
                    if more:
                        p5_front_end(j + 1)

            give_idx("p5", idx_b, 0, 0, True)
            p5_front(0, 0, 0, True)
            p5_front_end(0)
            peeled(act, batches("p5") // 2, p5_round)

            with act.Fori(0, NG) as g:
                act.wait_ge(sig("d3_logit"), g + 1)
                act.activation(self_t[:, 5], self_t[:, 4], ACT.Exp).then_inc(sig("d3_exp"), 1)
                ln_sqrt("d3a", g)
                ln_apply("d3a", g, ub, lambda t: ub[:, t, :])
                ln_sqrt("d3b", g)
                ln_apply("d3b", g, ub, lambda t: xin2[:, t, :])
                act.wait_ge(sig("ln_normed"), nth(NORM, "d3b", g) + 1)
                act.sem_inc(sig("result"), 1)

        @block.vector
        def _(dve):
            own = {"base": 0, "i": 0, "per": 0, "n": 0, "name": "v_step"}

            def step(ins):
                ins.then_inc(sig(own["name"]), 1)
                own["n"] += 1
                dve.wait_ge(sig(own["name"]), own["i"] * own["per"] + (own["base"] + own["n"]))

            def groups(per, body):
                own.update(base=own["base"] + own["n"], per=per, n=0)
                with dve.Fori(0, NG) as g:
                    own["i"] = g
                    body(g)
                    assert own["n"] == per, own["n"]
                own.update(base=own["base"] + NG * per, i=0, per=0, n=0)

            def hold():
                dve.sem_inc(sig("v_pace"), 1)

            def copy(dst, src):
                return dve.tensor_copy(dst, src)

            def ts(dst, src, s1, s2, o1, o2=None):
                return dve.tensor_scalar(out=dst, in0=src, scalar1=s1, scalar2=s2, op0=o1, **({"op1": o2} if o2 is not None else {}))

            def tt(dst, a, b, op):
                return dve.tensor_tensor(out=dst, in0=a, in1=b, op=op)

            def stt(dst, a, s, b, o1, o2):
                return dve.scalar_tensor_tensor(out=dst, in0=a, scalar=s, in1=b, op0=o1, op1=o2)

            dve.memset(ring_e[:, :, :], 1.0).then_inc(sig("cleared"), 1)
            dve.memset(ring_x[:, :, :], 0.0).then_inc(sig("cleared"), 1)
            dve.memset(none_i, -1).then_inc(sig("cleared"), 1)
            dve.memset(zero, 0.0).then_inc(sig("cleared"), 1)
            dve.wait_ge(sig("cleared"), 4)
            dve.wait_ge(sig("loaded"), 16 * LOADS)
            dve.wait_ge(sig("made"), 10)

            def order(s, nb, pad=0, tables=(), places=True):
                stretches = (ST if pad == P else PAIRS) // 2
                with dve.Fori(0, nb) as k:
                    dve.tensor_scalar(out=mask, in0=key, scalar1=lane[:, bass.ds(k, 1)], scalar2=None, op0=ALU.is_equal,
                                      op1=ALU.add, accum_out=counts[:, bass.ds(k, 1)]).then_inc(sig("counted"), 1)
                    dve.wait_ge(sig("counted"), k + (COUNTED[s] + 1))
                dve.wait_ge(sig("total"), ORDER[s] + 1)
                if pad:
                    shift = pad.bit_length() - 1
                    step(ts(small_i[0:NT, 0:1], ps[0:NT, 7, 0:1], float(pad - 1), None, ALU.add))
                    step(ts(small_i[0:NT, 1:2], small_i[0:NT, 0:1], shift, None, ALU.logical_shift_right))
                    step(copy(small[0:NT, 1:2], small_i[0:NT, 1:2]))
                    step(stt(small[0:NT, 3:4], small[0:NT, 1:2], -float(pad), ps[0:NT, 7, 0:1], ALU.mult, ALU.add))
                    ts(spread[0:NT, :], ones[0:NT, :], small[0:NT, 1:2], float(pad), ALU.mult, ALU.mult).then_inc(sig("spread"), 1)
                else:
                    ts(spread[:, :], ones[:, :], ps[:, 7, 0:1], None, ALU.mult).then_inc(sig("spread"), 1)
                dve.wait_ge(sig("start"), ORDER[s] + 1)
                step(ts(start_m1[:, 0:nb], ps[:, 7, 128:128 + nb], -1.0, None, ALU.add))
                if "last" in tables:
                    step(ts(last_a[0:1, :], ps[0:1, 7, 16:16 + NT], -1.0, 0.0, ALU.add, ALU.max))
                if tables:
                    step(copy(small[0:NT, 2:3], ps[0:NT, 7, 8:9]))
                    step(tt(small[0:NT, 2:3], small[0:NT, 2:3], small[0:NT, 1:2], ALU.add))
                    ts(reach[:, 0:2 * stretches], slot_no[:, 0:2 * stretches], small[0:NT, 2:3], None, ALU.is_ge)\
                        .then_inc(sig("reach"), 1)
                    dve.wait_ge(sig("cover"), ORDER[s] + 1)
                    for h in range(2):
                        part = slice(h * stretches, (h + 1) * stretches)
                        table = tile_a if pad == P else tile_b
                        step(ts(table[0:1, part], ps[0:1, 5 + h, 0:stretches], float(NT - 1), None, ALU.min))
                        if "from" in tables:
                            step(ts(seg_off[:, part], ps[:, 5 + h, 0:stretches], -float(P), 1.0, ALU.mult, ALU.add))
                            step(stt(rank[0:1, part], slot_no[0:1, part], float(pad), ps[0:1, 3 + h, 0:stretches],
                                     ALU.mult, ALU.add))
                            step(ts(from_b[0:1, part], rank[0:1, part], float(EDGES), None, ALU.min))
                if not places:
                    return
                with dve.Fori(0, nb) as k:
                    done = 3 * k + 3 * PLACED[s]
                    ts(mask, key, lane[:, bass.ds(k, 1)], None, ALU.is_equal).then_inc(sig("placed"), 1)
                    dve.wait_ge(sig("placed"), done + 1)
                    dve.tensor_tensor_scan(out=rank, data0=mask, data1=zero, initial=start_m1[:, bass.ds(k, 1)],
                                           op0=ALU.add, op1=ALU.add).then_inc(sig("placed"), 1)
                    dve.wait_ge(sig("placed"), done + 2)
                    hold()
                    dve.copy_predicated(place, mask.bitcast(U32), rank).then_inc(sig("placed"), 1)
                    dve.wait_ge(sig("placed"), done + 3)

            NOWHERE = float(4 * SLOTS)
            step(ts(tmp_i, src_i, 7, None, ALU.logical_shift_right))
            step(copy(key, tmp_i))
            step(copy(seg, src_i))
            step(stt(seg, key, -float(P), seg, ALU.mult, ALU.add))
            step(ts(seg, seg, 1.0, None, ALU.add))
            step(copy(other, dst_i))
            step(dve.memset(place, NOWHERE))
            order("src", NT, P, ("last",))
            dve.sem_inc(sig("src_tables"), 1)

            step(tt(mask[:, 0:ROWS], dst_i[:, 0:ROWS], next_i, ALU.is_gt))
            step(dve.tensor_reduce(out=small[:, 4:5], in_=mask[:, 0:ROWS], axis=AX, op=ALU.max))
            step(tt(rank[0:1, 0:TAIL - 1], tail_i[:, 0:TAIL - 1], tail_i[:, 1:TAIL], ALU.is_gt))
            step(dve.tensor_reduce(out=small[0:1, 5:6], in_=rank[0:1, 0:TAIL - 1], axis=AX, op=ALU.max))
            tt(small[0:1, 4:5], small[0:1, 4:5], small[0:1, 5:6], ALU.add).then_inc(sig("checked"), 1)
            dve.wait_ge(sig("violations"), 1)
            step(ts(small[0:1, 6:7], ps[0:1, 7, 500:501], 1.0, None, ALU.min))
            step(copy(flag_i[0:1, 0:1], small[0:1, 6:7]))
            step(ts(flag_i[0:1, 1:2], small[0:1, 6:7], -1.0, 1.0, ALU.mult, ALU.add))
            step(ts(tmp_i, dst_i, 7, None, ALU.logical_shift_right))
            step(copy(key, tmp_i))
            order("dst_tiles", NT, 2 * P, ("from",), places=False)
            dve.sem_inc(sig("flagged"), 1)

            with dve.If(nc.vector.value_load(flag_i[0:1, 0:1], min_val=0, max_val=1)):
                outside = dict(own)
                own.update(base=0, i=0, per=0, n=0, name="v_branch")
                step(ts(tmp_i, dst_i, P - 1, None, ALU.bitwise_and))
                for b in range(2):
                    dve.wait_ge(sig(f"sent{b}"), sent("src", b))
                step(dve.memset(place, NOWHERE))
                step(copy(key, tmp_i))
                step(copy(pair_i[:, :, 0], dst_i))
                step(copy(pair_i[:, :, 1], src_i))
                order("low", P)
                for b in range(2):
                    dve.wait_ge(sig(f"sent{b}"), sent("low", b))
                dve.wait_ge(sig("low_back"), 16)
                step(dve.memset(place, NOWHERE))
                step(ts(tmp_i, pair_i[:, :, 0], 7, None, ALU.logical_shift_right))
                step(copy(key, tmp_i))
                order("dst", NT, 2 * P)
                for b in range(2):
                    dve.wait_ge(sig(f"staged{b}"), 3 * (SB // 2 + 1))
                own.update(outside)
            for b in range(2):
                dve.wait_ge(sig(f"staged{b}"), SB // 2 + 1)

            def clear(n):
                step(dve.memset(acc[:, 0:n], 0.0))

            clear(NT * ACC1)

            def one_hot(s, seg_of, j, b):
                u = CFG[s][0]
                n = slot(s, b, 0)
                tt(hot[:, n:n + u], lane1[:, :].unsqueeze(1).broadcast_to([P, u, P]),
                   seg_of[:, bass.ds(j * u, u)].unsqueeze(2).broadcast_to([P, u, P]), ALU.is_equal).then_inc(sig("hot"), 1)

            def tiles_of(table, j, n):
                return nc.values_load_multi_w_load_instructions(
                    table[0:1, bass.ds(j * n, n)], engines=[mybir.EngineType.DVE], min_val=0, max_val=NT - 1,
                    skip_runtime_bounds_check_because="the tables hold numbers of node tiles, capped at the last")[1]

            def add_sums(s, j, first, k, width):
                n = CFG[s][0] // CFG[s][3]
                for v in range(n):
                    dve.wait_ge(sig("sum"), j * n + (sums_before(s) + v + 1))
                    if s == "p1":
                        halves = [(0, D, 2 * (v % 4), 0, ACC1), (D + 1, 2 * (D + 1), 2 * (v % 4) + 1, 0, ACC1)]
                    else:
                        h, stride = width // 2, ACC1 if s == "p2" else width
                        halves = [(0, h, v % 4, 0, stride), (h, width, v % 4, h, stride)]
                    for m, (a0, a1, bank, c0, stride) in enumerate(halves):
                        if not (first and v == 0):
                            dve.wait_ge(sig("add"), j * (2 * n) + (2 * sums_before(s) + 2 * v - 1 + m))
                        a = acc[:, bass.ds(k[v] * stride + a0, a1 - a0)]
                        tt(a, a, ps[:, bank, c0:c0 + a1 - a0], ALU.add).then_inc(sig("add"), 1)

            def sum_pass(s):
                u, ring = CFG[s][0:2]

                def hots(i, b):
                    if s == "p1":
                        dve.wait_ge(sig(f"segs{b}"), i + 1)
                    one_hot(s, seg_a, ring * i + b, b)

                def round_(i, first, last):
                    for b in range(ring):
                        k = tiles_of(tile_a, ring * i + b, u)
                        if not (last and b == ring - 1):
                            hots(i + (b + 1) // ring, (b + 1) % ring)
                        add_sums(s, ring * i + b, first and b == 0, k, D)

                hots(0, 0)
                peeled(dve, batches(s) // ring, round_)

            def ln_stats(s, g, src):
                for t in range(G):
                    m = dve.bn_stats(stat[:, t, :], src(t))
                step(m)
                hold()
                for t in range(G):
                    m = dve.bn_aggr(mv[:, t, :], stat[:, t, :])
                step(m)
                ts(sd[:, 0, :], mv[:, :, 1], EPS, None, ALU.add).then_inc(sig("ln_var"), 1)
                dve.wait_ge(sig("ln_sqrt"), nth(NORM, s, g) + 1)
                step(dve.reciprocal(sd[:, 2, :], sd[:, 1, :]))
                stt(sd[:, 3, :], mv[:, :, 0], -1.0, sd[:, 2, :], ALU.mult, ALU.mult).then_inc(sig("ln_rstd"), 1)

            def over(v):
                return vec[:, v:v + 1, :].broadcast_to([P, G, D])

            def affine(s, g, buf, gamma, beta, ready):
                dve.wait_ge(sig("ln_normed"), nth(NORM, ready, g) + 1)
                step(tt(buf, buf, over(gamma), ALU.mult))
                return tt(buf, buf, over(beta), ALU.add)

            pt = lambda t: psf[:, 4 * 512 + t * D:4 * 512 + (t + 1) * D]

            sum_pass("p1")
            deg = acc[:, :].rearrange("p (k w) -> p k w", w=ACC1)[:, :, ACC1 - 1]
            dve.wait_ge(sig("add"), 2 * ST)
            step(ts(rdeg[:, :], deg, 1.0, None, ALU.max))
            step(dve.reciprocal(rdeg[:, :], rdeg[:, :]))

            def layer_in(s, g):
                for t in range(G):
                    k = g * G + t
                    a = acc[:, bass.ds(k * ACC1, D)]
                    m = stt(ub[:, t, :], a, rdeg[:, bass.ds(k, 1)], xin[:, t, :], ALU.mult, ALU.add)
                m.then_inc(sig("operand"), 1)

            def first_layer(g):
                dve.wait_ge(sig("d0_in"), 16 * (g + 1))
                layer_in("d0", g)
                dve.wait_ge(sig("d0_mm"), g + 1)
                ln_stats("d0a", g, pt)
                affine("d0", g, ub[:, :, :], V_G0, V_BE0, "d0a").then_inc(sig("d0_affine"), 1)

            dve.sem_inc(sig("free"), 1)
            groups(4, first_layer)
            dve.wait_ge(sig("sums_cleared"), 1)

            sum_pass("p2")
            dve.wait_ge(sig("add"), 4 * ST)
            def second_layer(g):
                dve.wait_ge(sig("d1_in"), 32 * (g + 1))
                layer_in("d1", g)
                dve.wait_ge(sig("operand"), NG + g + 1)
                hold()
                copy(xin[:, :, :], acc[:, bass.ds(g * (G * ACC1), G * ACC1)].rearrange("p (t w) -> p t w", w=ACC1)
                     [:, :, D + 1:2 * D + 1]).then_inc(sig("d1_edges"), 1)
                dve.wait_ge(sig("d1_mm"), g + 1)
                ln_stats("d1a", g, pt)
                affine("d1", g, ub[:, :, :], V_G1, V_BE1, "d1a").then_inc(sig("d1_affine"), 1)
                dve.wait_ge(sig("d1_silu"), g + 1)
                step(tt(ub[:, :, :], ub[:, :, :], xin2[:, :, :], ALU.add))
                ln_stats("d1b", g, lambda t: ub[:, t, :])
                dve.wait_ge(sig("d1_mm2"), g + 1)
                ln_stats("d1d", g, pt)
                step(affine("d1g", g, xin2[:, :, :], V_LGA, V_LBE, "d1d"))
                step(tt(xin2[:, :, :], xin2[:, :, :], ub[:, :, :], ALU.add))
                step(tt(xin2[:, :, :], xin2[:, :, :], ub[:, :, :], ALU.add))
                ln_stats("d1e", g, lambda t: xin2[:, t, :])
                dve.wait_ge(sig("d1_elr"), g + 1)
                hold()
                lr = psf[:, 6 * 512:6 * 512 + G * 2 * H2].rearrange("p (t w) -> p t w", w=2 * H2)
                step(copy(el[:, bass.ds(g * (G * H2), G * H2)].rearrange("p (t w) -> p t w", w=H2), lr[:, :, 0:H2]))
                copy(prj2[:, :, C2:W2], lr[:, :, H2:2 * H2]).then_inc(sig("result"), 1)

            dve.sem_inc(sig("free"), 1)
            groups(4 * 3 + 1 + 1 + 1 + 3 + 1, second_layer)
            dve.wait_ge(sig("d1_stored"), 32 * NG)
            clear(NT * ACC2)

            dve.wait_ge(sig("dst_back"), 16 * RB)
            step(dve.memset(dst_rowf, 0.0))
            for w in range(2):
                n = ST5 - (RB - 1) * P
                step(copy(dst_rowf[:, 0:RB - 1, w, :], dst_rows[:, 0:RB - 1, :, w]))
                step(copy(dst_rowf[0:n, RB - 1, w, :], dst_rows[0:n, RB - 1, :, w]))
            dve.sem_inc(sig("dst_rowf"), 1)
            dve.wait_ge(sig("dst_cols"), 1)
            step(tt(seg_b[:, :].rearrange("p (q t) -> p q t", t=2), psf[:, 0:ST5].rearrange("p (q t) -> p q t", t=2),
                    seg_off[:, :].unsqueeze(2).broadcast_to([P, PAIRS, 2]), ALU.add))
            step(ts(idx_b[:, :], psf[:, 1024:1024 + ST5], 0.0, None, ALU.max))

            def p3_messages(i, b):
                j = 2 * i + b
                dve.wait_ge(sig("p3_el"), j + 1)
                dve.wait_ge(sig(f"got{b}"), got("p3", b, i + 1))
                tt(zl[:, 0], ps[:, 6 + b, 0:U * H2].rearrange("p (u h) -> p u h", h=H2), ring_x[:, b * U:(b + 1) * U, C2:W2],
                   ALU.add).then_inc(sig("p3_z"), 1)
                dve.wait_ge(sig("p3_z"), j + 1)
                stt(zl[:, 1], zl[:, 0], 0.2, zl[:, 0], ALU.mult, ALU.max).then_inc(sig("p3_leaky"), 1)
                dve.wait_ge(sig("p3_exp"), j + 1)
                for u in range(U):
                    m = tt(mring[:, b, u, 0:D].rearrange("p (h c) -> p h c", c=C2),
                           ring_x[:, b * U + u, 0:C2].unsqueeze(1).broadcast_to([P, H2, C2]),
                           mring[:, b, u, D:D + H2].unsqueeze(2).broadcast_to([P, H2, C2]), ALU.mult)
                m.then_inc(sig("p3_msg"), 1)

            def p3_round(i, first, last):
                for b in range(2):
                    more = not (last and b == 1)
                    k = tiles_of(tile_a, 2 * i + b, U)
                    if more:
                        one_hot("p3", seg_a, 2 * i + b + 1, 1 - b)
                    add_sums("p3", 2 * i + b, first and b == 0, k, ACC2)
                    if more:
                        p3_messages(i + b, 1 - b)

            one_hot("p3", seg_a, 0, 0)
            p3_messages(0, 0)
            peeled(dve, batches("p3") // 2, p3_round)

            dve.wait_ge(sig("add"), 6 * ST)
            dve.wait_ge(sig("d1_vectors"), 16 * 5)

            def third_layer(g):
                a3 = acc[:, bass.ds(g * (G * ACC2), G * ACC2)].rearrange("p (t w) -> p t w", w=ACC2)
                rs = sd[:, :, :].rearrange("p a b -> p (a b)").rearrange("p (t h) -> p t h", h=H2)
                step(ts(rs, a3[:, :, D:ACC2], 1e-12, None, ALU.max))
                step(dve.reciprocal(rs, rs))
                for t in range(G):
                    m = tt(ub[:, t, :].rearrange("p (h c) -> p h c", c=C2), a3[:, t, 0:D].rearrange("p (h c) -> p h c", c=C2),
                           rs[:, t, :].unsqueeze(2).broadcast_to([P, H2, C2]), ALU.mult)
                step(m)
                ubh = ub[:, :, :].rearrange("p t (h c) -> p (t h) c", c=C2)
                step(tt(ubh, ubh, abv[:, :].unsqueeze(1).broadcast_to([P, G * H2, C2]), ALU.add))
                ts(xin2[:, :, :], ub[:, :, :], 0.0, None, ALU.min).then_inc(sig("d2_low"), 1)
                dve.wait_ge(sig("d2_exp"), g + 1)
                step(stt(ub[:, :, :], ub[:, :, :], 0.0, xin2[:, :, :], ALU.max, ALU.add))
                dve.wait_ge(sig("d2_in"), 16 * (g + 1))
                step(stt(ub[:, :, :], ub[:, :, :], -1.0, xin[:, :, :], ALU.add, ALU.add))
                ln_stats("d2a", g, lambda t: ub[:, t, :])
                dve.wait_ge(sig("d2_projc"), g + 1)
                mag = ma[:, bass.ds(g * (G * 2 * H3), G * 2 * H3)].rearrange("p (t w) -> p t w", w=2 * H3)
                for n, v in enumerate((V_GSRC, V_GDST)):
                    step(tt(ub[:, :, :], prj3[:, :, 0:D], over(v), ALU.mult))
                    step(dve.tensor_reduce(out=mag[:, :, n * H3:(n + 1) * H3],
                                           in_=ub[:, :, :].rearrange("p t (h c) -> p t h c", c=C3), axis=AX, op=ALU.add))
                hold()
                copy(prj3[:, :, D:W3], mag[:, :, 0:H3]).then_inc(sig("result"), 1)

            dve.sem_inc(sig("free"), 1)
            groups(4 + 2 + 3 + 4, third_layer)
            dve.wait_ge(sig("d2_stored"), 32 * NG)
            clear(NT * W3)
            step(dve.memset(lastm[:, :], 1.0))
            step(dve.memset(pen[:, :], -BIG))
            step(dve.memset(svt[:, :, :], 1.0))

            def leaky(dst, src):
                return stt(dst, src, 0.2, src, ALU.mult, ALU.max)

            V = U // 2

            def chain(name, per, j):
                n = [0]

                def put(ins, wait=True):
                    n[0] += 1
                    ins.then_inc(sig(name), 1)
                    if wait:
                        dve.wait_ge(sig(name), j * per + n[0])

                put.end = lambda: n[0] == per
                return put

            def maxima(j, b):
                k = tiles_of(tile_b, j, V)
                dve.wait_ge(sig("p5_rows_c"), j + 1)
                f = front = chain("p5_front", 10 + V, j)
                f(tt(lastm[:, 0:P - 1], rowsb[:, 1, 0:P - 1], rowsb[:, 1, 1:P], ALU.not_equal))
                f(ts(pen[:, 1:P], lastm[:, 0:P - 1], -BIG, None, ALU.mult))
                f(dve.tensor_tensor_scan(out=scan[:, :], data0=pen[:, :], data1=rowsb[:, 0, :], initial=0.0,
                                         op0=ALU.add, op1=ALU.max))
                tt(sv[:, :], scan[:, :], lastm[:, :], ALU.mult).then_inc(sig("p5_top"), 1)
                return k, f

            def new_maxima(j, k, f):
                dve.wait_ge(sig("p5_max"), j + 1)
                mx = ps[:, 7, 0:U * (H3 + 1)].rearrange("p (u w) -> p u w", w=H3 + 1)
                f(ts(present[:, :], mx[:, :, H3], 1.0, -1.0, ALU.min, ALU.add))
                f(stt(cand[:, :, :], present[:, :].unsqueeze(2).broadcast_to([P, U, H3]), BIG, mx[:, :, 0:H3], ALU.mult, ALU.add))
                pair = cand[:, :, :].rearrange("p (v t) h -> p v t h", t=2)
                f(tt(pair[:, :, 0, :], pair[:, :, 0, :], pair[:, :, 1, :], ALU.max), False)
                f(copy(mold[:, 0, :], ma[:, bass.ds(k[0] * (2 * H3), 2 * H3)]))
                for v in range(V):
                    m = ma[:, bass.ds(k[v] * (2 * H3), H3)]
                    f(tt(m, m, pair[:, v, 0, :], ALU.max))
                dve.sem_inc(sig("p5_newmax"), 1)
                f(copy(mold[:, 1, :], ma[:, bass.ds(k[0] * (2 * H3), 2 * H3)]))
                f(tt(resc[:, 0], mold[:, :, 0:H3], mold[:, :, H3:2 * H3], ALU.add))
                f(leaky(resc[:, 1], resc[:, 0]))
                tt(resc[:, 2, 0, :], resc[:, 1, 0, :], resc[:, 1, 1, :], ALU.subtract).then_inc(sig("p5_fade"), 1)
                assert f.end()

            def fade(j, k):
                dve.wait_ge(sig("p5_fade_e"), j + 1)
                a = acc[:, bass.ds(k[0] * W3, D)].rearrange("p (h c) -> p h c", c=C3)
                tt(a, a, resc[:, 3, 0, :].unsqueeze(2).broadcast_to([P, H3, C3]), ALU.mult).then_inc(sig("p5_faded"), 1)
                a = acc[:, bass.ds(k[0] * W3 + D, H3)]
                tt(a, a, resc[:, 3, 0, :], ALU.mult).then_inc(sig("p5_faded"), 1)

            def logits(j, b):
                dve.wait_ge(sig("p5_spread_c"), j + 1)
                f = chain("p5_back", 3, j)
                f(tt(zz[:, 0], ees[:, :, H3:2 * H3], ring_x[:, b * U:(b + 1) * U, D:W3], ALU.add), False)
                f(tt(zz[:, 1], ees[:, :, H3:2 * H3], ees[:, :, 0:H3], ALU.add))
                f(leaky(zz[:, 0:2], zz[:, 0:2]))
                assert f.end()
                tt(zz[:, 2], zz[:, 0], zz[:, 1], ALU.subtract).then_inc(sig("p5_logit"), 1)

            def messages(j, b):
                dve.wait_ge(sig("p5_exp"), j + 1)
                for u in range(U):
                    v = ring_x[:, b * U + u, 0:D].rearrange("p (h c) -> p h c", c=C3)
                    m = tt(v, v, ring_x[:, b * U + u, D:W3].unsqueeze(2).broadcast_to([P, H3, C3]), ALU.mult)
                m.then_inc(sig("p5_msg"), 1)

            def p5_round(i, first, last):
                for b in range(2):
                    j = 2 * i + b
                    more = not (last and b == 1)
                    if more:
                        one_hot("p5", seg_b, j + 1, 1 - b)
                    logits(j, b)
                    if more:
                        k1, f = maxima(j + 1, 1 - b)
                    messages(j, b)
                    if more:
                        new_maxima(j + 1, k1, f)
                    k = tiles_of(tile_b, j, V)
                    dve.wait_ge(sig("p5_faded"), 2 * (j + 1))
                    add_sums("p5", j, first and b == 0, k, W3)
                    if more:
                        dve.wait_ge(sig("add"), (j + 1) * (2 * V) + 2 * sums_before("p5"))
                        fade(j + 1, k1)

            one_hot("p5", seg_b, 0, 0)
            k1, f = maxima(0, 0)
            new_maxima(0, k1, f)
            fade(0, k1)
            peeled(dve, batches("p5") // 2, p5_round)

            dve.wait_ge(sig("add"), 6 * ST + ST5)
            def fourth_layer(g):
                a3 = acc[:, bass.ds(g * (G * W3), G * W3)].rearrange("p (t w) -> p t w", w=W3)
                mag = ma[:, bass.ds(g * (G * 2 * H3), G * 2 * H3)].rearrange("p (t w) -> p t w", w=2 * H3)
                dve.wait_ge(sig("d3_in"), 32 * (g + 1))
                step(tt(self_t[:, 0], prj3[:, :, D:W3], mag[:, :, H3:2 * H3], ALU.add))
                step(tt(self_t[:, 1], mag[:, :, 0:H3], mag[:, :, H3:2 * H3], ALU.add))
                step(leaky(self_t[:, 2], self_t[:, 0]))
                step(leaky(self_t[:, 3], self_t[:, 1]))
                tt(self_t[:, 4], self_t[:, 2], self_t[:, 3], ALU.subtract).then_inc(sig("d3_logit"), 1)
                dve.wait_ge(sig("d3_exp"), g + 1)
                step(tt(self_t[:, 6], a3[:, :, D:W3], self_t[:, 5], ALU.add))
                step(dve.reciprocal(self_t[:, 7], self_t[:, 6]))
                for t in range(G):
                    u3 = ub[:, t, :].rearrange("p (h c) -> p h c", c=C3)
                    m = tt(u3, prj3[:, t, 0:D].rearrange("p (h c) -> p h c", c=C3),
                           self_t[:, 5, t, :].unsqueeze(2).broadcast_to([P, H3, C3]), ALU.mult)
                step(m)
                step(tt(ub[:, :, :], ub[:, :, :], a3[:, :, 0:D], ALU.add))
                for t in range(G):
                    u3 = ub[:, t, :].rearrange("p (h c) -> p h c", c=C3)
                    m = tt(u3, u3, self_t[:, 7, t, :].unsqueeze(2).broadcast_to([P, H3, C3]), ALU.mult)
                step(m)
                step(tt(ub[:, :, :], ub[:, :, :], over(V_GB), ALU.add))
                ln_stats("d3a", g, lambda t: ub[:, t, :])
                step(affine("d3", g, ub[:, :, :], V_GGA, V_GBE, "d3a"))
                step(tt(xin2[:, :, :], ub[:, :, :], xin[:, :, :], ALU.add))
                ln_stats("d3b", g, lambda t: xin2[:, t, :])

            dve.sem_inc(sig("free"), 1)
            groups(4 + 2 + 4 + 2 * 3 + 2 + 1, fourth_layer)

        @block.tensor
        def _(pe):
            def mm(dst, lhs, rhs, start=True, stop=True):
                return pe.matmul(dst, lhsT=lhs, rhs=rhs, start=start, stop=stop)

            def hold():
                pe.sem_inc(sig("t_pace"), 1)

            def totals(s, nb, pad=0, tables=False, weigh=False):
                pe.wait_ge(sig("counted"), COUNTED[s] + nb)
                mm(ps[0:nb, 7, 0:1], counts[:, 0:nb], ones[:, 0:1]).then_inc(sig("total"), 1)
                pe.wait_ge(sig("spread"), ORDER[s] + 1)
                if pad:
                    mm(ps[0:NT, 7, 8:9], below[0:NT, 0:NT], small[0:NT, 1:2])
                    mm(ps[0:1, 7, 16:16 + NT], small[0:NT, 1:2], upto[0:NT, 0:NT])
                mm(ps[:, 7, 128:128 + nb], below[:, :], counts[:, 0:nb], stop=False)
                mm(ps[:, 7, 128:128 + nb], spread[0:nb, :], below[0:nb, 0:nb], start=False).then_inc(sig("start"), 1)
                if tables:
                    n = (ST if pad == P else PAIRS) // 2
                    pe.wait_ge(sig("reach"), ORDER[s] + 1)
                    for h in range(2):
                        m = mm(ps[:, 5 + h, 0:n], ones[0:NT, :], reach[:, h * n:(h + 1) * n])
                        if weigh:
                            m = mm(ps[0:1, 3 + h, 0:n], small[0:NT, 3:4], reach[:, h * n:(h + 1) * n])
                    m.then_inc(sig("cover"), 1)

            pe.wait_ge(sig("made"), 10)
            pe.wait_ge(sig("loaded"), 16 * LOADS)
            totals("src", NT, P, tables=True)
            pe.wait_ge(sig("checked"), 1)
            mm(ps[0:1, 7, 500:501], small[:, 4:5], ones[:, 0:1]).then_inc(sig("violations"), 1)
            totals("dst_tiles", NT, 2 * P, tables=True, weigh=True)
            pe.wait_ge(sig("flagged"), 1)
            with pe.If(nc.tensor.value_load(flag_i[0:1, 0:1], min_val=0, max_val=1)):
                totals("low", P)
                totals("dst", NT, 2 * P)

            def sums(s, j, b, first, width, src):
                u_n, _, _, unit = CFG[s]
                n = u_n // unit
                pe.wait_ge(sig("hot"), j + (hots_before(s) + 1))
                for v in range(n):
                    if not (first and v < 4):
                        pe.wait_ge(sig("add"), j * (2 * n) + (2 * sums_before(s) + 2 * (v - 3)))
                    for t in range(unit):
                        c = slot(s, b, v * unit + t)
                        if s == "p1":
                            mm(ps[:, 2 * (v % 4), 0:D], hot[:, c, :], ring_x[:, c, 0:D])
                            m = mm(ps[:, 2 * (v % 4) + 1, 0:D + 1], hot[:, c, :], ring_e[:, c, 2:EW + 1])
                        else:
                            m = mm(ps[:, v % 4, 0:width], hot[:, c, :], src(b, v * unit + t), start=t == 0, stop=t == unit - 1)
                    m.then_inc(sig("sum"), 1)

            def sum_pass(s, width, src):
                ring = CFG[s][1]

                def round_(i, first, last):
                    for b in range(ring):
                        pe.wait_ge(sig(f"got{b}"), got(s, b, i + 1))
                        if s == "p1":
                            pe.wait_ge(sig(f"p1_rows{b}"), 16 * (i + 1))
                        sums(s, ring * i + b, b, first and b == 0, width, src)
                peeled(pe, batches(s) // ring, round_)

            def turn(s, g, parts, name):
                for n, v in enumerate(parts):
                    m = pe.transpose(psf[:, n * P:(n + 1) * P], v, ident[:, :])
                m.then_inc(sig("turned"), 1)

            def layer(s, g, wts, row, name):
                pe.wait_ge(sig("operand"), STAGE[s] * NG + g + 1)
                turn(s, g, [ub[:, t, c * P:(c + 1) * P] for t in range(G) for c in range(2)], name)
                pe.wait_ge(sig("taken"), nth(TURN, name, g) + 1)
                for t in range(G):
                    o = psf[:, 4 * 512 + t * D:4 * 512 + (t + 1) * D]
                    mm(o, ones[0:1, :], rows[0:1, row, :], stop=False)
                    for c in range(2):
                        m = mm(o, op_t[:, (2 * t + c) * P:(2 * t + c + 1) * P], wts[:, c, :], start=False, stop=c == 1)
                m.then_inc(sig(f"{s}_mm"), 1)

            sum_pass("p1", D, None)
            with pe.Fori(0, NG) as g:
                layer("d0", g, wsq, 0, "d0a")
            sum_pass("p2", D, lambda b, u: ring_x[:, b * U + u, 0:D])
            pe.wait_ge(sig("d0_weights"), 16)
            with pe.Fori(0, NG) as g:
                layer("d1", g, wsq, 1, "d1a")
                pe.wait_ge(sig("ln_normed"), nth(NORM, "d1b", g) + 1)
                n = G * P // 2
                blocks = []
                for c in range(2):
                    blocks += [ub[:, t, c * P:(c + 1) * P] for t in range(G)]
                for c in range(2):
                    blocks += [xin[:, t, c * P:(c + 1) * P] for t in range(G)]
                pe.wait_ge(sig("d1_edges"), g + 1)
                turn("d1", g, blocks, "d1c")
                pe.wait_ge(sig("taken"), nth(TURN, "d1c", g) + 1)
                for m_ in range(4):
                    for h in range(2):
                        for c in range(4):
                            m = mm(ps[:, 2 * m_ + h, 0:n], lw1s[:, c, m_ * P:(m_ + 1) * P],
                                   op_t[:, c * G * P + h * n:c * G * P + (h + 1) * n], start=c == 0, stop=c == 3)
                m.then_inc(sig("d1_hidden"), 1)
                pe.wait_ge(sig("d1_hid_t"), 8 * (g + 1))
                for t in range(G):
                    o = psf[:, 4 * 512 + t * D:4 * 512 + (t + 1) * D]
                    mm(o, ones[0:1, :], rows[0:1, 2, :], stop=False)
                    for c in range(4):
                        m = mm(o, hid_t[:, c * G * P + t * P:c * G * P + (t + 1) * P], lw2s[:, c, :], start=False, stop=c == 3)
                m.then_inc(sig("d1_mm2"), 1)
                pe.wait_ge(sig("ln_normed"), nth(NORM, "d1e", g) + 1)
                turn("d1", g, [xin[:, t, c * P:(c + 1) * P] for t in range(G) for c in range(2)], "d1f")
                pe.wait_ge(sig("taken"), nth(TURN, "d1f", g) + 1)
                for t in range(G):
                    for c in range(2):
                        m = mm(psf[:, 4 * 512 + t * C2:4 * 512 + (t + 1) * C2], op_t[:, (2 * t + c) * P:(2 * t + c + 1) * P],
                               aws[:, c, :], start=c == 0, stop=c == 1)
                m.then_inc(sig("d1_proj"), 1)
                pe.wait_ge(sig("d1_projc"), g + 1)
                hold()
                for t in range(G):
                    m = pe.transpose(psf[0:C2, t * P:(t + 1) * P], prj2[:, t, 0:C2], ident[:, :])
                m.then_inc(sig("d1_projt"), 1)
                pe.wait_ge(sig("d1_projtc"), 2 * (g + 1))
                for t in range(G):
                    m = mm(psf[:, 6 * 512 + t * 2 * H2:6 * 512 + (t + 1) * 2 * H2], hot_t[0:C2, t, :], awlrs[:, :])
                m.then_inc(sig("d1_elr"), 1)

            def turn_hots(s, j, b, first):
                pe.wait_ge(sig("hot"), j + (hots_before(s) + 1))
                if not first:
                    pe.wait_ge(sig(f"{s}_hot_tc"), 2 * j)
                for u in range(U):
                    m = pe.transpose(ps[:, 4 + u // 4, (u % 4) * P:(u % 4 + 1) * P], hot[:, b * U + u, :], ident[:, :])
                m.then_inc(sig(f"{s}_hot_t"), 1)

            def tiles_of(table, j, n):
                return nc.values_load_multi_w_load_instructions(
                    table[0:1, bass.ds(j * n, n)], engines=[mybir.EngineType.PE], min_val=0, max_val=NT - 1,
                    skip_runtime_bounds_check_because="the tables hold numbers of node tiles, capped at the last")[1]

            pe.wait_ge(sig("dst_rowf"), 1)
            for t in range(RB):
                n = min(P, ST5 - t * P)
                for w in range(2):
                    m = pe.transpose(psf[:, w * 1024 + t * P:w * 1024 + t * P + n], dst_rowf[0:n, t, w, :], ident[0:n, 0:n])
            m.then_inc(sig("dst_cols"), 1)

            def p3_el(i, b):
                j = 2 * i + b
                k = tiles_of(tile_a, j, U)
                pe.wait_ge(sig("p3_hot_tc"), 2 * (j + 1))
                for u in range(U):
                    m = mm(ps[:, 6 + b, u * H2:(u + 1) * H2], hot_t[:, u, :], el[:, bass.ds(k[u] * H2, H2)])
                m.then_inc(sig("p3_el"), 1)

            def p3_round(i, first, last):
                for b in range(2):
                    j = 2 * i + b
                    more = not (last and b == 1)
                    if more:
                        turn_hots("p3", j + 1, 1 - b, False)
                    pe.wait_ge(sig("p3_msg"), j + 1)
                    sums("p3", j, b, first and b == 0, ACC2, lambda b, u: mring[:, b, u, :])
                    if more:
                        p3_el(i + b, 1 - b)

            turn_hots("p3", 0, 0, True)
            p3_el(0, 0)
            peeled(pe, batches("p3") // 2, p3_round)

            pe.wait_ge(sig("d1_weights"), 16)
            with pe.Fori(0, NG) as g:
                pe.wait_ge(sig("ln_normed"), nth(NORM, "d2a", g) + 1)
                turn("d2", g, [xin[:, t, c * P:(c + 1) * P] for t in range(G) for c in range(2)], "d2b")
                pe.wait_ge(sig("taken"), nth(TURN, "d2b", g) + 1)
                for t in range(G):
                    for c in range(2):
                        m = mm(psf[:, 4 * 512 + t * D:4 * 512 + (t + 1) * D], op_t[:, (2 * t + c) * P:(2 * t + c + 1) * P],
                               wsq[:, c, :], start=c == 0, stop=c == 1)
                m.then_inc(sig("d2_proj"), 1)

            n5 = U * H3

            def p5_front(j, b, first):
                turn_hots("p5", j, b, first)
                pe.wait_ge(sig("p5_cmp"), j + 1)
                if not first:
                    pe.wait_ge(sig("p5_rows_c"), j)
                hold()
                for w in range(2):
                    m = pe.transpose(ps[0:n5, 6, w * P:(w + 1) * P], cmp[:, w, :], ident[:, :])
                m.then_inc(sig("p5_rows_t"), 1)
                pe.wait_ge(sig("p5_top"), j + 1)
                hold()
                pe.transpose(ps[:, 6, 256:256 + n5], sv[:, :], ident[0:n5, 0:n5]).then_inc(sig("p5_top_t"), 1)
                pe.wait_ge(sig("p5_top_c"), j + 1)
                for u in range(U):
                    m = mm(ps[:, 7, u * (H3 + 1):(u + 1) * (H3 + 1)], hot[:, b * U + u, :], svt[:, u, :])
                m.then_inc(sig("p5_max"), 1)

            def p5_spread(j):
                k = tiles_of(tile_b, j, U // 2)
                pe.wait_ge(sig("p5_newmax"), j + 1)
                pe.wait_ge(sig("p5_hot_tc"), 2 * (j + 1))
                for u in range(U):
                    m = mm(ps[:, 7, 128 + u * 2 * H3:128 + (u + 1) * 2 * H3], hot_t[:, u, :],
                           ma[:, bass.ds(k[u // 2] * (2 * H3), 2 * H3)])
                m.then_inc(sig("p5_spread"), 1)

            def p5_round(i, first, last):
                for b in range(2):
                    j = 2 * i + b
                    more = not (last and b == 1)
                    if more:
                        p5_front(j + 1, 1 - b, False)
                    pe.wait_ge(sig("p5_msg"), j + 1)
                    sums("p5", j, b, first and b == 0, W3, lambda b, u: ring_x[:, b * U + u, :])
                    if more:
                        p5_spread(j + 1)

            p5_front(0, 0, True)
            p5_spread(0)
            peeled(pe, batches("p5") // 2, p5_round)


def kernel(x, src, dst, edge_attr_256, L0_gnn_W0, L0_gnn_b0, L0_gnn_g0, L0_gnn_beta0, L0_gnn_W1, L0_gnn_b1, L0_gnn_g1,
           L0_gnn_beta1, L1_gnn_W1, L1_gnn_b1, L1_gnn_W2, L1_gnn_b2, L1_gnn_gamma, L1_gnn_beta, L2_gnn_W, L2_gnn_Wl,
           L2_gnn_Wr, L2_gnn_b, L3_gnn_W, L3_gnn_att_src, L3_gnn_att_dst, L3_gnn_bias, L3_gnn_gamma, L3_gnn_beta):
    import numpy as np
    import concourse.bacc as bacc
    from concourse.bass_utils import run_bass_kernel_spmd

    def columns(a):
        c = np.full((P, COLS), NODES_UP, np.int32)
        c[:, 0:ROWS] = a[0:ROWS * P].reshape(P, ROWS)
        c[0:TAIL, ROWS] = a[ROWS * P:EDGES]
        return c

    def padded(a):
        c = np.zeros((NODES_UP, D), np.float32)
        c[0:NODES] = a
        return c

    src, dst = np.asarray(src), np.asarray(dst)
    both = np.full((EDGES + 2 * P, 2), -1, np.int32)
    both[0:EDGES, 0], both[0:EDGES, 1] = dst, src
    arrays = [
        padded(np.asarray(x)), columns(src), columns(dst), dst[1:ROWS * P + 1].reshape(P, ROWS),
        dst[ROWS * P:EDGES].reshape(1, TAIL), both, np.asarray(edge_attr_256),
        np.asarray(L0_gnn_W0).T, L0_gnn_b0, L0_gnn_g0, L0_gnn_beta0,
        np.asarray(L0_gnn_W1).T, L0_gnn_b1, L0_gnn_g1, L0_gnn_beta1,
        L1_gnn_W1, np.asarray(L1_gnn_b1).reshape(4, P).T, L1_gnn_W2, L1_gnn_b2, L1_gnn_gamma, L1_gnn_beta,
        L2_gnn_W, np.concatenate([np.asarray(L2_gnn_Wl).T, np.asarray(L2_gnn_Wr).T], axis=1), L2_gnn_b,
        L3_gnn_W, np.asarray(L3_gnn_att_src).reshape(-1), np.asarray(L3_gnn_att_dst).reshape(-1),
        L3_gnn_bias, L3_gnn_gamma, L3_gnn_beta,
    ]
    names = ["x", "src", "dst", "dst_next", "dst_tail", "pairs", "edge_attr", "w0t", "b0", "g0", "be0", "w1t", "b1", "g1", "be1", "lw1", "lb1", "lw2",
             "lb2", "lga", "lbe", "aw", "awlr", "ab", "gw", "gsrc", "gdst", "gb", "gga", "gbe"]
    arrays = {f"in_{n}": np.ascontiguousarray(np.asarray(a)) for n, a in zip(names, arrays)}
    nc = bacc.Bacc("TRN2", target_bir_lowering=False, num_devices=1)
    aps = [nc.dram_tensor(n, a.shape, mybir.dt.from_np(a.dtype), kind="ExternalInput").ap() for n, a in arrays.items()]
    out = nc.dram_tensor("out_x", (NODES_UP, D), F32, kind="ExternalOutput").ap()
    gnn_kernel(nc, *aps, out)
    r = run_bass_kernel_spmd(nc, [arrays], core_ids=[0])
    return np.asarray(r.results[0]["out_x"])[0:NODES]
```

```python
import concourse.bass as bass
from concourse import mybir
from contextlib import ExitStack

F32 = mybir.dt.float32
I32 = mybir.dt.int32
U32 = mybir.dt.uint32
I16 = mybir.dt.int16
BF16 = mybir.dt.bfloat16
ALU = mybir.AluOpType
ACT = mybir.ActivationFunctionType
AX = mybir.AxisListType.X

P = 128
NODES = 6250
EDGES = 106250
D = 256
NT = -(-NODES // P)
NODES_UP = NT * P
ST = -(-((EDGES + (P - 1) * NT) // P) // 16) * 16
ST5 = -(-((EDGES + (2 * P - 1) * NT) // (2 * P)) // 8) * 16
SLOTS = ST * P
SLOTS5 = ST5 * P
PAIRS = ST5 // 2
ROWS = EDGES // P
TAIL = EDGES - ROWS * P
COLS = ROWS + 2
SU = 10
SB = ROWS // SU
EW = 2 + D
ER_W = EW + 2
H2, C2 = 4, 64
H3, C3 = 8, 32
W3 = D + H3
W2 = C2 + H2
ACC1 = 2 * (D + 1)
ACC2 = D + H2
G = 7
NG = NT // G
HALF = ST // 2
CFG = {"p1": (4, 4, ST, 1), "p2": (8, 2, ST, 1), "p3": (8, 4, ST, 1), "p5": (8, 4, ST5, 2)}
U = 8
BIG = 1e30
EPS = 1e-5
assert ROWS == SB * SU and SB % 2 == 1 and NG * G == NT and C2 * H2 == D and C3 * H3 == D


def gnn_kernel(nc, x, src2, dst2, dst_next, dst_tail, pairs, edge_attr, w0t, b0, g0, be0, w1t, b1, g1, be1, lw1, lb1, lw2, lb2, lga, lbe,
               aw, awlr, ab, gw, gsrc, gdst, gb, gga, gbe, out):
    ctx = ExitStack()
    made = {}

    def sb(name, shape, dt=F32):
        return ctx.enter_context(nc.sbuf_tensor(name, shape, dt))

    def sig(name):
        if name not in made:
            made[name] = ctx.enter_context(nc.semaphore(name))
        return made[name]

    def dram(name, shape, dt=F32):
        return nc.dram_tensor(name, shape, dt, kind="Internal").ap()

    by_src = dram("by_src", (SLOTS, EW))
    by_low = dram("by_low", (P * COLS, 2), I32)
    by_dst = dram("by_dst", (SLOTS5, 2), I32)
    h1_tab = dram("h1_tab", (NODES_UP, D))
    x2_tab = dram("x2_tab", (NODES_UP, D))
    p2_tab = dram("p2_tab", (NODES_UP, W2))
    x3_tab = dram("x3_tab", (NODES_UP, D))
    p3_tab = dram("p3_tab", (NODES_UP, W3))

    with ctx:
        acc = sb("acc", [P, NT * ACC1])

        def space(n, dt=F32, wide=1):
            v = acc[:, n * COLS:(n + wide) * COLS]
            return v if dt is F32 else v.bitcast(dt)

        key, seg, other, mask, rank, zero, place = (space(n) for n in range(7))
        src_i, dst_i, tmp_i = (space(n, I32) for n in range(7, 10))
        pair_i = space(10, I32, 2).rearrange("p (c w) -> p c w", w=2)
        reach = acc[0:NT, 14 * COLS:14 * COLS + ST]
        slot_no = acc[0:NT, 16 * COLS:16 * COLS + ST]
        next_i = space(18, I32)[:, 0:ROWS]
        tail_i = space(19, I32)[0:1, 0:TAIL]
        RB = -(-ST5 // P)
        LATE = NT * ACC1 - 4 * RB * P
        dst_rows = acc[:, LATE:LATE + RB * 2 * P].bitcast(I32).rearrange("p (t e w) -> p t e w", t=RB, w=2)
        dst_rowf = acc[:, LATE + RB * 2 * P:LATE + RB * 4 * P].rearrange("p (t w e) -> p t w e", t=RB, w=2)
        assert LATE >= NT * ACC2 and 26 * COLS + 6 * P <= NT * ACC1

        ring_e = sb("ring_e", [P, 2 * SU, ER_W])
        ring_x = sb("ring_x", [P, 16, W3])
        hot = sb("hot", [P, 16, P])
        hot_t = sb("hot_t", [P, U, P])
        idx_ring = sb("idx_ring", [P, 4 * U], I32)
        pair_ring = sb("pair_ring", [P, 2 * SU, 2], I32)
        seg_a, seg_b = sb("seg_a", [P, ST], BF16), sb("seg_b", [P, ST5], BF16)
        idx_a, idx_b = sb("idx_a", [P, ST], I16), sb("idx_b", [P, ST5], I16)
        tile_a, tile_b = sb("tile_a", [1, ST], I32), sb("tile_b", [1, PAIRS], I32)
        from_b = hot_t[0:1, :, :].rearrange("p a b -> p (a b)")[:, 0:PAIRS].bitcast(I32)
        seg_off = sb("seg_off", [P, PAIRS])
        flag_i = sb("flag_i", [1, 2], I32)
        last_a = sb("last_a", [1, NT], I32)
        lane = sb("lane", [P, P])
        lane1 = sb("lane1", [P, P])
        ident = sb("ident", [P, P])
        below = acc[:, 26 * COLS:26 * COLS + P]
        upto = acc[:, 26 * COLS + P:26 * COLS + 2 * P]
        ones = sb("ones", [P, P])
        counts = acc[:, 26 * COLS + 2 * P:26 * COLS + 3 * P]
        start_m1 = acc[:, 26 * COLS + 3 * P:26 * COLS + 4 * P]
        small = sb("small", [P, 8])
        small_i = sb("small_i", [P, 8], I32)
        spread = acc[:, 26 * COLS + 4 * P:26 * COLS + 5 * P]
        wsq = sb("wsq", [P, 2, D])
        lw1s = sb("lw1s", [P, 4, 2 * D])
        lw2s = sb("lw2s", [P, 4, D])
        aws = sb("aws", [P, 2, C2])
        awlrs = sb("awlrs", [C2, 2 * H2])
        rows = sb("rows", [1, 3, D])
        lb1s = sb("lb1s", [P, 4])
        vec = sb("vec", [P, 6, D])
        V_G0, V_BE0, V_G1, V_BE1, V_LGA, V_LBE = range(6)
        V_GSRC, V_GDST, V_GB, V_GGA, V_GBE = range(5)
        abv = sb("abv", [P, C2])
        rdeg = sb("rdeg", [P, NT])
        el = sb("el", [P, NT * H2])
        ma = sb("ma", [P, NT * 2 * H3])
        xin2, ub = (sb(n, [P, G, D]) for n in ("xin2", "ub"))
        stat = sb("stat", [P, G, 6])
        mv = sb("mv", [P, G, 2])
        sd = sb("sd", [P, 4, G])
        behind = [NT * W3]

        def tail(parts, n):
            behind[0] += n
            return acc[0:parts, behind[0] - n:behind[0]]

        cmp = tail(P, 2 * U * H3).rearrange("p (a n) -> p a n", a=2)
        rowsb = tail(U * H3, 2 * P).rearrange("p (a n) -> p a n", a=2)
        lastm, pen, scan, sv = (tail(U * H3, P) for _ in range(4))
        svt = tail(P, U * (H3 + 1)).rearrange("p (u h) -> p u h", u=U)
        cand = tail(P, U * H3).rearrange("p (u h) -> p u h", u=U)
        ees = tail(P, U * 2 * H3).rearrange("p (u h) -> p u h", u=U)
        zz = tail(P, 4 * U * H3).rearrange("p (s u h) -> p s u h", s=4, u=U)
        more_hots = tail(P, 2 * U * P).rearrange("p (c n) -> p c n", n=P)
        present = sb("present", [P, U])
        mold = sb("mold", [P, 2, 2 * H3])
        resc = sb("resc", [P, 4, 2, H3])
        zl = sb("zl", [P, 2, U, H2])
        ps = ctx.enter_context(nc.psum_tensor("ps", [P, 8, 512], F32))
        psf = ps[:, :, :].rearrange("p a b -> p (a b)")

        acc1 = acc[:, :].rearrange("p (k a w) -> p k a w", a=2, w=D + 1)
        hot_f = hot[:, :, :].rearrange("p b c -> p (b c)")
        ring_ef = ring_e[:, :, :].rearrange("p b c -> p (b c)")
        ring_xf = ring_x[:, :, :].rearrange("p b c -> p (b c)")
        xin = hot_f[:, 0:G * D].rearrange("p (t w) -> p t w", w=D)
        op_t = ring_ef[:, 0:4 * G * P]
        hid_t = ring_xf[:, 0:4 * G * P]
        prj2 = ring_ef[:, 4 * G * P:4 * G * P + G * W2].rearrange("p (t w) -> p t w", w=W2)
        out1 = ring_xf[:, 0:G * D].rearrange("p (t w) -> p t w", w=D)
        prj3 = ring_xf[:, 0:G * W3].rearrange("p (t w) -> p t w", w=W3)
        mring = ring_ef[:, 0:2 * U * ACC2].rearrange("p (a u w) -> p a u w", a=2, u=U)
        self_t = hot_t[:, :, :].rearrange("p a b -> p (a b)")[:, 0:8 * G * H3].rearrange("p (s t h) -> p s t h", s=8, h=H3)
        p3_rows = ring_xf[:, 0:4 * U * W2].rearrange("p (c w) -> p c w", w=W2)
        more_rows = ring_ef[:, 0:2 * U * W3].rearrange("p (c w) -> p c w", w=W3)
        none_i = seg_b[:, :].bitcast(I32)
        zero_row = ring_x[:, 0, 0:EW]

        def slot(s, b, u):
            return b * CFG[s][0] + u

        def two_of(b, ours, more):
            return (ours if b < 2 else more)[:, (b % 2) * U:(b % 2 + 1) * U, :]

        def rows5(b):
            return two_of(b, ring_x, more_rows)

        def hots(s, b):
            if s in ("p3", "p5"):
                return two_of(b, hot, more_hots)
            return hot[:, b * CFG[s][0]:(b + 1) * CFG[s][0], :]

        def at(j, n):
            return isinstance(j, int) and j == n

        def batch(s, i, b):
            ring = CFG[s][1]
            return (i * ring + b, i + b // ring, b % ring)

        def visits(eng, s, visit):
            ring = CFG[s][1]

            def round_(i, first, last):
                n = ring + batches(s) % ring if last else ring
                for b in range(n):
                    visit(i, b, n - b if last else None)
            peeled(eng, batches(s) // ring, round_)

        def beats(eng, s, depth, beat):
            for n in range(1, depth):
                beat(*[batch(s, 0, n - 1 - k) if k < n else None for k in range(depth)])
            visits(eng, s, lambda i, b, left: beat(*[batch(s, i, b + k) if left is None or left > k else None
                                                     for k in reversed(range(depth))]))

        def batches(s):
            return CFG[s][2] // CFG[s][0]

        def earlier(s):
            return [q for q in CFG if q < s]

        def sums_before(s):
            return sum(CFG[q][2] // CFG[q][3] for q in earlier(s))

        def hots_before(s):
            return sum(batches(q) for q in earlier(s))

        def rounds_before(s, b):
            return sum(len(range(b, batches(q), CFG[q][1])) for q in earlier(s) if CFG[q][1] > b)

        def got(s, b, i):
            return sum(16 * CFG[q][0] * len(range(b, batches(q), CFG[q][1])) for q in earlier(s) if CFG[q][1] > b) + 16 * CFG[s][0] * i

        def used(s, i, b):
            u, ring, _, unit = CFG[s]
            return (i * ring + (b - ring + 1)) * (u // unit) + sums_before(s)

        ORDER = {"src": 0, "dst_tiles": 1, "low": 2, "dst": 3}
        COUNTED = {"src": 0, "dst_tiles": NT, "low": 2 * NT, "dst": 2 * NT + P}
        PLACED = {"src": 0, "low": NT, "dst": NT + P}
        SENT = {"src": 0, "low": 1, "dst": 2}
        STAGE = {"d0": 0, "d1": 1, "d2": 2, "d3": 3}
        NORM = {"d0a": (0, 1), "d1a": (NG, 4), "d1b": (NG + 1, 4), "d1d": (NG + 2, 4), "d1e": (NG + 3, 4),
                "d2a": (5 * NG, 1), "d3a": (6 * NG, 2), "d3b": (6 * NG + 1, 2)}
        TURN = {"d0a": (0, 1), "d1a": (NG, 3), "d1c": (NG + 1, 3), "d1f": (NG + 2, 3), "d2b": (4 * NG, 1)}

        PARTS = ((0, 0, 4), (1, 4, G))

        def nth(of, s, g, h):
            return g * (2 * of[s][1]) + (2 * of[s][0] + h)

        def pt(t):
            h = int(t >= PARTS[1][1])
            at_ = 2048 * h + 1024 + (t - PARTS[h][1]) * D
            return psf[:, at_:at_ + D]

        block = ctx.enter_context(nc.Block())
        LOADS = 4 + 4 + 3 + 3 + 6

        def peeled(eng, n, body):
            body(0, True, False)
            with eng.Fori(1, n - 1) as i:
                body(i, False, False)
            body(n - 1, False, True)

        def sent(s, b, batches=None):
            whole = 16 * (SU * (SB // 2 + 1) if b == 0 else SU * (SB // 2) + 2)
            return SENT[s] * whole + (whole if batches is None else 16 * SU * batches)

        @block.sync
        def _(sp):
            def load(dst, src):
                sp.dma_start(dst, src).then_inc(sig("loaded"), 16)

            load(src_i, src2)
            load(dst_i, dst2)
            load(next_i, dst_next)
            load(tail_i, dst_tail)
            for w, d in ((wsq, w0t), (lw1s, lw1), (lw2s, lw2), (aws, aw)):
                load(w[:, :, :], d.rearrange("(a p) n -> p a n", p=P))
            load(awlrs[:, :], awlr)
            load(lb1s[:, :], lb1)
            load(abv[:, :], ab.partition_broadcast(P))
            for n, d in enumerate((b0, b1, lb2)):
                load(rows[0:1, n, :], d.rearrange("(a n) -> a n", a=1))
            for n, d in enumerate((g0, be0, g1, be1, lga, lbe)):
                load(vec[:, n, :], d.partition_broadcast(P))

            sp.wait_ge(sig("cleared"), 3)
            tiles = by_src.rearrange("(t p) w -> p t w", p=P)
            spare = EDGES // P
            n_pre = 0
            for t in range(spare, ST, G):
                n = min(G, ST - t)
                sp.dma_start(tiles[:, t:t + n, :], ring_x[:, 0:1, 0:EW].broadcast_to([P, n, EW]))\
                  .then_inc(sig("src_prefill"), 16)
                n_pre += 1
            sp.wait_ge(sig("src_prefill"), 16 * n_pre)
            sp.wait_ge(sig("src_tables"), 1)
            with sp.Fori(0, NT) as k:
                last = nc.sync.value_load(last_a[0:1, bass.ds(k, 1)], min_val=0, max_val=ST - 1)
                sp.dma_start(by_src[bass.ds(last * P, P), :], zero_row).then_inc(sig("src_prefill"), 16)
                sp.wait_ge(sig("src_prefill"), 16 * (k + n_pre + 1))
                sp.sem_inc(sig("sp_pace"), 1)
            sp.sem_inc(sig("src_prefilled"), 1)

            attr = edge_attr[0:ROWS * P, :].rearrange("(p c) w -> p c w", c=ROWS)

            def attr_pair(i, first, last):
                for b in range(2):
                    if not first:
                        sp.wait_ge(sig(f"sent{b}"), sent("src", b, i))
                    sp.dma_start(ring_e[:, b * SU:(b + 1) * SU, 2:EW], attr[:, bass.ds((2 * i + b) * SU, SU), :])\
                      .then_inc(sig(f"attr{b}"), 16)

            peeled(sp, SB // 2, attr_pair)
            sp.wait_ge(sig("sent0"), sent("src", 0, SB // 2))
            sp.dma_start(ring_e[:, 0:SU, 2:EW], attr[:, (SB - 1) * SU:SB * SU, :]).then_inc(sig("attr0"), 16)
            sp.wait_ge(sig("sent1"), sent("src", 1, SB // 2))
            sp.dma_start(ring_e[0:TAIL, SU, 2:EW], edge_attr[ROWS * P:EDGES, :]).then_inc(sig("attr1"), 16)

            sp.wait_ge(sig("flagged"), 1)
            with sp.If(nc.sync.value_load(flag_i[0:1, 0:1], min_val=0, max_val=1)):
                sp.dma_start(by_dst.rearrange("(t p e) w -> p t (e w)", p=P, t=4),
                             none_i.unsqueeze(1).broadcast_to([P, 4, SLOTS5 // P // 2])).then_inc(sig("dst_prefill"), 16)
                for b in range(2):
                    sp.wait_ge(sig(f"sent{b}"), sent("low", b))
                sp.dma_start(pair_i, by_low.rearrange("(p c) w -> p c w", c=COLS)).then_inc(sig("low_back"), 16)

            for b in range(2):
                sp.wait_ge(sig(f"sent{b}"), sent("src", b))

            def e_round(i, first, last):
                u, ring = CFG["p1"][0:2]
                for b in range(ring):
                    if not first:
                        sp.wait_ge(sig("sum"), used("p1", i, b))
                    sp.dma_start(ring_e[:, slot("p1", b, 0):slot("p1", b, u), 0:EW],
                                 tiles[:, bass.ds((ring * i + b) * u, u), :]).then_inc(sig(f"p1_rows{b}"), 16)

            peeled(sp, batches("p1") // CFG["p1"][1], e_round)

            def nodes(t, g):
                return t[bass.ds(g * (G * P), G * P), :].rearrange("(t p) w -> p t w", p=P)

            for s, ins, outs in (("d0", [(x, xin)], [(h1_tab, ub)]),
                                 ("d1", [(h1_tab, xin), (x, xin2)], [(x2_tab, out1), (p2_tab, prj2)]),
                                 ("d2", [(x2_tab, xin)], [(x3_tab, xin2), (p3_tab, prj3)]),
                                 ("d3", [(x3_tab, xin), (p3_tab, prj3)], [(out, ub)])):
                def rows_in(g, which=slice(None)):
                    for t, s_in in ins[which]:
                        sp.dma_start(s_in[:, :, :], nodes(t, g)).then_inc(sig(f"{s}_in"), 16)

                def results_out(g):
                    sp.wait_ge(sig("result"), STAGE[s] * NG + g + 1)
                    for t, s_out in outs:
                        sp.dma_start(nodes(t, g), s_out[:, :, :]).then_inc(sig(f"{s}_stored"), 16)
                    sp.wait_ge(sig(f"{s}_stored"), 16 * len(outs) * (g + 1))
                    sp.sem_inc(sig("free"), 1)

                sp.wait_ge(sig("free"), STAGE[s] * (NG + 1) + 1)
                rows_in(0)
                with sp.Fori(0, NG - 1) as g:
                    if s == "d1":
                        sp.wait_ge(sig("taken"), nth(TURN, "d1c", g, 1) + 1)
                        rows_in(g + 1, slice(0, 1))
                        sp.wait_ge(sig("ln_normed"), nth(NORM, "d1e", g, 1) + 1)
                        rows_in(g + 1, slice(1, 2))
                        results_out(g)
                    else:
                        if s == "d0":
                            sp.wait_ge(sig("operand"), 2 * g + 2)
                        else:
                            sp.wait_ge(sig("consumed"), g + (1 if s == "d2" else NG + 1))
                        rows_in(g + 1)
                        results_out(g)
                results_out(NG - 1)
                if s == "d0":
                    with sp.If(nc.sync.value_load(flag_i[0:1, 1:2], min_val=0, max_val=1)):
                        with sp.Fori(0, PAIRS) as q:
                            at = nc.sync.value_load(from_b[0:1, bass.ds(q, 1)], min_val=0, max_val=EDGES)
                            sp.dma_start(by_dst[bass.ds(q * (2 * P), 2 * P), :], pairs[bass.ds(at, 2 * P), :])\
                              .then_inc(sig("copied"), 16)
                        sp.wait_ge(sig("copied"), 16 * PAIRS)
                if s == "d1":
                    with sp.If(nc.sync.value_load(flag_i[0:1, 0:1], min_val=0, max_val=1)):
                        for b in range(2):
                            sp.wait_ge(sig(f"sent{b}"), sent("dst", b))
                    for t in range(RB):
                        n = min(P, ST5 - t * P)
                        sp.dma_start(dst_rows[0:n, t], by_dst[t * P * P:(t * P + n) * P, :]
                                     .rearrange("(s e) w -> s e w", e=P)).then_inc(sig("dst_back"), 16)
                for w in {"d0": [w1t], "d1": [gw]}.get(s, []):
                    sp.dma_start(wsq[:, :, :], w.rearrange("(a p) n -> p a n", p=P)).then_inc(sig(f"{s}_weights"), 16)
                if s == "d1":
                    for n, d in enumerate((gsrc, gdst, gb, gga, gbe)):
                        sp.dma_start(vec[:, n, :], d.partition_broadcast(P)).then_inc(sig("d1_vectors"), 16)

        @block.gpsimd
        def _(pool):
            pool.iota(lane[:, :], pattern=[[1, P]], base=0, channel_multiplier=0,
                      allow_small_or_imprecise_dtypes=True).then_inc(sig("made"), 1)
            pool.iota(lane1[:, :], pattern=[[1, P]], base=1, channel_multiplier=0,
                      allow_small_or_imprecise_dtypes=True).then_inc(sig("made"), 1)
            pool.iota(slot_no, pattern=[[1, ST]], base=0, channel_multiplier=0,
                      allow_small_or_imprecise_dtypes=True).then_inc(sig("made"), 1)
            for t, v in ((ident, 0.0), (below, 1.0), (upto, 1.0), (ones, 1.0)):
                pool.memset(t[:, :], v).then_inc(sig("made"), 1)
            pool.wait_ge(sig("made"), 7)
            for t, op, fill in ((ident, ALU.not_equal, 1.0), (below, ALU.is_gt, 0.0), (upto, ALU.is_ge, 0.0)):
                pool.affine_select(out=t[:, :], in_=t[:, :], compare_op=op, fill=fill, base=0,
                                   pattern=[[1, P]], channel_multiplier=-1).then_inc(sig("made"), 1)

            def scatter(s, table, bound, source):
                def send(b, n, waits):
                    for name, value in waits:
                        pool.wait_ge(sig(name), value)
                    pool.sem_inc(sig("pool_pace"), 1)
                    for u in range(n):
                        pool.indirect_dma_start(
                            table, bass.IndirectOffsetOnAxis(ap=idx_ring[:, b * SU + u:b * SU + u + 1], axis=0), source(b, u), None,
                            bounds_check=bound, oob_is_err=False).then_inc(sig(f"sent{b}"), 16)

                def waits(b, i):
                    w = [(f"staged{b}", SENT[s] * (SB // 2 + 1) + i + 1)]
                    return w + [(f"attr{b}", 16 * (i + 1))] * (s == "src")

                def pair(i, first, last):
                    for b in range(2):
                        send(b, SU, waits(b, i))

                peeled(pool, SB // 2, pair)
                send(0, SU, waits(0, SB // 2))
                send(1, 2, waits(1, SB // 2))

            pool.wait_ge(sig("src_prefilled"), 1)
            scatter("src", by_src, SLOTS - 1, lambda b, u: ring_e[:, b * SU + u, 0:EW])
            pool.wait_ge(sig("flagged"), 1)
            with pool.If(nc.gpsimd.value_load(flag_i[0:1, 0:1], min_val=0, max_val=1)):
                scatter("low", by_low, P * COLS - 1, lambda b, u: pair_ring[:, b * SU + u, :])
                pool.wait_ge(sig("dst_prefill"), 16)
                scatter("dst", by_dst, SLOTS5 - 1, lambda b, u: pair_ring[:, b * SU + u, :])

            def gather(s, table, width, freed="sum"):
                u_n, ring = CFG[s][0:2]

                def visit(i, b, left):
                    j, i, b = batch(s, i, b)
                    pool.wait_ge(sig(f"idx{b}"), i + (rounds_before(s, b) + 1))
                    if not at(i, 0) and s != "p5":
                        pool.wait_ge(sig(freed), used(s, i, b) if freed == "sum" else ring * i + (b - ring + 1))
                    pool.sem_inc(sig("pool_pace"), 1)
                    for u in range(u_n):
                        if not at(i, 0) and s == "p5" and u % 2 == 0:
                            pool.wait_ge(sig("sum"), used(s, i, b) - (u_n // 2 - 1 - u // 2))
                            pool.sem_inc(sig("pool_pace"), 1)
                        n = slot(s, b, u)
                        rows = p3_rows[:, n, :] if s == "p3" else rows5(b)[:, u, :] if s == "p5" else ring_x[:, n, 0:width]
                        pool.indirect_dma_start(
                            rows, None, table, bass.IndirectOffsetOnAxis(ap=idx_ring[:, n:n + 1], axis=0)
                        ).then_inc(sig(f"got{b}"), 16)

                visits(pool, s, visit)

            gather("p1", x, D)
            pool.wait_ge(sig("operand"), 2 * NG)
            pool.memset(acc1[:, :, 0, 0:D], 0.0).then_inc(sig("sums_cleared"), 1)
            pool.wait_ge(sig("d0_stored"), 16 * NG)
            gather("p2", h1_tab, D)
            pool.wait_ge(sig("d1_stored"), 32 * NG)
            gather("p3", p2_tab, W2, "p3_msg")
            pool.wait_ge(sig("d2_stored"), 32 * NG)
            gather("p5", p3_tab, W3)

        @block.scalar
        def _(act):
            def copy(dst, src):
                return act.activation(dst, src, ACT.Copy)

            def stage(s, parts):
                act.wait_ge(sig("placed"), 3 * (PLACED[s] + (NT if s != "low" else P)))

                def put(b, c, n):
                    for dst, src in parts(b, c, n):
                        copy(dst, src)
                    copy(idx_ring[:, b * SU:b * SU + n], place[:, bass.ds(c, n)]).then_inc(sig(f"staged{b}"), 1)

                def pair(i, first, last):
                    for b in range(2):
                        if not first:
                            act.wait_ge(sig(f"sent{b}"), sent(s, b, i))
                        put(b, (2 * i + b) * SU, SU)

                peeled(act, SB // 2, pair)
                for b, n in ((0, SU), (1, 2)):
                    act.wait_ge(sig(f"sent{b}"), sent(s, b, SB // 2))
                    put(b, (SB - 1 + b) * SU, n)

            stage("src", lambda b, c, n: [(ring_e[:, b * SU:b * SU + n, 0], seg[:, bass.ds(c, n)]),
                                          (ring_e[:, b * SU:b * SU + n, 1], other[:, bass.ds(c, n)])])
            act.wait_ge(sig("flagged"), 1)
            with act.If(nc.scalar.value_load(flag_i[0:1, 0:1], min_val=0, max_val=1)):
                for s, prev in (("low", "src"), ("dst", "low")):
                    for b in range(2):
                        act.wait_ge(sig(f"sent{b}"), sent(prev, b))
                    stage(s, lambda b, c, n: [(pair_ring[:, b * SU:b * SU + n, :], pair_i[:, bass.ds(c, n), :])])
                for b in range(2):
                    act.wait_ge(sig(f"sent{b}"), sent("dst", b))

            def p1_round(i, first, last):
                u, ring = CFG["p1"][0:2]
                for b in range(ring):
                    act.wait_ge(sig(f"p1_rows{b}"), 16 * (i + 1))
                    if not first:
                        act.wait_ge(sig(f"got{b}"), got("p1", b, i))
                    c = (ring * i + b) * u
                    n = slot("p1", b, 0)
                    copy(idx_ring[:, n:n + u], ring_e[:, n:n + u, 1]).then_inc(sig(f"idx{b}"), 1)
                    copy(idx_a[:, bass.ds(c, u)], ring_e[:, n:n + u, 1]).then_inc(sig("kept"), 1)
                    copy(seg_a[:, bass.ds(c, u)], ring_e[:, n:n + u, 0]).then_inc(sig(f"segs{b}"), 1)

            peeled(act, batches("p1") // CFG["p1"][1], p1_round)

            def give_idx(s, idx, i, b, first):
                u, ring = CFG[s][0:2]
                if not first:
                    act.wait_ge(sig(f"got{b}"), got(s, b, i))
                n = slot(s, b, 0)
                copy(idx_ring[:, n:n + u], idx[:, bass.ds((ring * i + b) * u, u)]).then_inc(sig(f"idx{b}"), 1)

            def norm(s, g, dst, src):
                for h, t0, t1 in PARTS:
                    act.wait_ge(sig("ln_var"), nth(NORM, s, g, h) + 1)
                    act.activation(sd[:, 1, t0:t1], sd[:, 0, t0:t1], ACT.Sqrt).then_inc(sig("ln_sqrt"), 1)
                    act.wait_ge(sig("ln_rstd"), nth(NORM, s, g, h) + 1)
                    for t in range(t0, t1):
                        a = act.activation(dst[:, t, :], src(t), ACT.Identity, bias=sd[:, 3, t:t + 1], scale=sd[:, 2, t:t + 1])
                    a.then_inc(sig("ln_normed"), 1)

            def take_t(s, g, per, dst):
                for h, t0, t1 in PARTS:
                    act.wait_ge(sig("turned"), nth(TURN, s, g, h) + 1)
                    n = (t1 - t0) * per * P
                    for c in range(0, n, 512):
                        m = min(512, n - c)
                        a = copy(dst[:, 2048 * h + c:2048 * h + c + m], psf[:, 2048 * h + c:2048 * h + c + m])
                    a.then_inc(sig("taken"), 1)

            with act.Fori(0, NG) as g:
                take_t("d0a", g, 2, op_t)
                norm("d0a", g, ub, pt)
                for h, t0, t1 in PARTS:
                    act.wait_ge(sig("d0_affine"), 2 * g + (h + 1))
                    a = act.activation(ub[:, t0:t1, :], ub[:, t0:t1, :], ACT.Silu)
                a.then_inc(sig("result"), 1)

            act.wait_ge(sig("kept"), batches("p1"))

            def p2_round(i, first, last):
                for b in range(CFG["p2"][1]):
                    give_idx("p2", idx_a, i, b, first)

            peeled(act, batches("p2") // CFG["p2"][1], p2_round)

            with act.Fori(0, NG) as g:
                take_t("d1a", g, 2, op_t)
                norm("d1a", g, ub, pt)
                for h, t0, t1 in PARTS:
                    act.wait_ge(sig("d1_affine"), 2 * g + (h + 1))
                    act.activation(ub[:, t0:t1, :], ub[:, t0:t1, :], ACT.Silu).then_inc(sig("d1_silu"), 1)
                norm("d1b", g, ub, lambda t: ub[:, t, :])
                take_t("d1c", g, 4, op_t)
                for h, t0, t1 in PARTS:
                    act.wait_ge(sig("d1_hidden"), 2 * g + (h + 1))
                    n = (t1 - t0) * P
                    for m in range(4):
                        a = act.activation(hid_t[:, 2048 * h + m * n:2048 * h + (m + 1) * n], ps[:, 4 * h + m, 0:n],
                                           ACT.Silu, bias=lb1s[:, m:m + 1])
                    a.then_inc(sig("d1_hid_t"), 1)
                norm("d1d", g, xin2, pt)
                norm("d1e", g, out1, lambda t: xin2[:, t, :])
                take_t("d1f", g, 2, op_t)
                for h, t0, t1 in PARTS:
                    act.wait_ge(sig("d1_proj"), 2 * g + (h + 1))
                    copy(prj2[:, t0:t1, 0:C2], psf[:, 2048 * h + 1024:2048 * h + 1024 + (t1 - t0) * C2]
                         .rearrange("p (t w) -> p t w", w=C2)).then_inc(sig("d1_projc"), 1)
                for h, t0, t1 in PARTS:
                    act.wait_ge(sig("d1_projt"), 2 * g + (h + 1))
                    copy(hot_t[0:C2, t0:t1, :].rearrange("p a b -> p (a b)"), psf[0:C2, 2048 * h:2048 * h + (t1 - t0) * P])\
                        .then_inc(sig("d1_projtc"), 1)

            def take_hots(s, j):
                act.wait_ge(sig(f"{s}_hot_t"), j + 1)
                for h in range(2):
                    copy(hot_t[:, 4 * h:4 * h + 4, :].rearrange("p a b -> p (a b)"), ps[:, 4 + h, :])\
                        .then_inc(sig(f"{s}_hot_tc"), 1)

            def p3_beat(a, b, c):
                if a:
                    j, i, buf = a
                    if at(j, 0):
                        for n in range(4):
                            give_idx("p3", idx_a, 0, n, True)
                    elif not (at(j, 1) or at(j, batches("p3") - 2) or at(j, batches("p3") - 1)):
                        give_idx("p3", idx_a, i + (buf + 2) // 4, (buf + 2) % 4, False)
                if b:
                    j, _, buf = b
                    act.wait_ge(sig("p3_leaky"), j + 1)
                    if not (at(j, 0) or at(j, 1)):
                        act.wait_ge(sig("sum"), (j - 1) * U + sums_before("p3"))
                    act.activation(mring[:, buf % 2, :, D:D + H2], zl[:, 1], ACT.Exp).then_inc(sig("p3_exp"), 1)
                if a:
                    if not at(a[0], 0):
                        act.wait_ge(sig("p3_el"), a[0])
                    take_hots("p3", a[0])

            beats(act, "p3", 3, p3_beat)

            with act.Fori(0, NG) as g:
                for h, t0, t1 in PARTS:
                    act.wait_ge(sig("d2_low"), 2 * g + (h + 1))
                    act.activation(xin2[:, t0:t1, :], xin2[:, t0:t1, :], ACT.Exp).then_inc(sig("d2_exp"), 1)
                norm("d2a", g, xin2, lambda t: ub[:, t, :])
                take_t("d2b", g, 2, op_t)
                for h, t0, t1 in PARTS:
                    act.wait_ge(sig("d2_proj"), 2 * g + (h + 1))
                    for t in range(t0, t1):
                        a = copy(prj3[:, t, 0:D], pt(t))
                    a.then_inc(sig("d2_projc"), 1)

            def p5_beat(a, b, c, d):
                if a:
                    j, i, buf = a
                    if at(j, 0):
                        for n in range(4):
                            give_idx("p5", idx_b, 0, n, True)
                    elif not (at(j, 1) or at(j, 2) or at(j, batches("p5") - 1)):
                        give_idx("p5", idx_b, i + (buf + 1) // 4, (buf + 1) % 4, False)
                    if not at(j, 0):
                        act.wait_ge(sig("p5_rows_t"), j)
                    copy(cmp[:, 1, :].rearrange("p (u h) -> p u h", h=H3),
                         seg_b[:, bass.ds(j * U, U)].unsqueeze(2).broadcast_to([P, U, H3]))
                    act.wait_ge(sig(f"got{buf}"), got("p5", buf, i + 1))
                    copy(cmp[:, 0, :].rearrange("p (u h) -> p u h", h=H3), rows5(buf)[:, :, D:W3])\
                        .then_inc(sig("p5_cmp"), 1)
                    act.wait_ge(sig("p5_rows_t"), j + 1)
                    if not at(j, 0):
                        act.wait_ge(sig("p5_top"), j)
                    copy(rowsb[:, :, :], ps[0:U * H3, 6, 0:2 * P].rearrange("p (a e) -> p a e", a=2))\
                        .then_inc(sig("p5_rows_c"), 1)
                if b:
                    j = b[0]
                    act.wait_ge(sig("p5_fade"), j + 1)
                    act.activation(resc[:, 3, b[2] % 2, :], resc[:, 2, 0, :], ACT.Exp).then_inc(sig("p5_fade_e"), 1)
                    act.wait_ge(sig("p5_spread"), j + 1)
                    copy(ees[:, :, :], ps[:, 7, 128:128 + U * 2 * H3].rearrange("p (u h) -> p u h", h=2 * H3))\
                        .then_inc(sig("p5_spread_c"), 1)
                if a:
                    act.wait_ge(sig("p5_top_t"), a[0] + 1)
                    copy(svt[:, :, 0:H3], ps[:, 6, 256:256 + U * H3].rearrange("p (u h) -> p u h", h=H3))\
                        .then_inc(sig("p5_top_c"), 1)
                    take_hots("p5", a[0])
                if b:
                    j, _, buf = b
                    act.wait_ge(sig("p5_logit"), j + 1)
                    act.activation(rows5(buf)[:, :, D:W3], zz[:, 2], ACT.Exp).then_inc(sig("p5_exp"), 1)

            beats(act, "p5", 4, p5_beat)

            with act.Fori(0, NG) as g:
                act.wait_ge(sig("d3_logit"), g + 1)
                act.activation(self_t[:, 5], self_t[:, 4], ACT.Exp).then_inc(sig("d3_exp"), 1)
                norm("d3a", g, ub, lambda t: ub[:, t, :])
                norm("d3b", g, ub, lambda t: xin2[:, t, :])
                act.wait_ge(sig("ln_normed"), nth(NORM, "d3b", g, 1) + 1)
                act.sem_inc(sig("result"), 1)

        @block.vector
        def _(dve):
            own = {"base": 0, "i": 0, "per": 0, "n": 0, "name": "v_step"}

            def step(ins):
                ins.then_inc(sig(own["name"]), 1)
                own["n"] += 1
                dve.wait_ge(sig(own["name"]), own["i"] * own["per"] + (own["base"] + own["n"]))

            def groups(per, body):
                own.update(base=own["base"] + own["n"], per=per, n=0)
                with dve.Fori(0, NG) as g:
                    own["i"] = g
                    body(g)
                    assert own["n"] == per, own["n"]
                own.update(base=own["base"] + NG * per, i=0, per=0, n=0)

            def hold():
                dve.sem_inc(sig("v_pace"), 1)

            def copy(dst, src):
                return dve.tensor_copy(dst, src)

            def ts(dst, src, s1, s2, o1, o2=None):
                return dve.tensor_scalar(out=dst, in0=src, scalar1=s1, scalar2=s2, op0=o1, **({"op1": o2} if o2 is not None else {}))

            def tt(dst, a, b, op):
                return dve.tensor_tensor(out=dst, in0=a, in1=b, op=op)

            def stt(dst, a, s, b, o1, o2):
                return dve.scalar_tensor_tensor(out=dst, in0=a, scalar=s, in1=b, op0=o1, op1=o2)

            dve.memset(ring_e[:, :, :], 1.0).then_inc(sig("cleared"), 1)
            dve.memset(ring_x[:, :, :], 0.0).then_inc(sig("cleared"), 1)
            dve.memset(none_i, -1).then_inc(sig("cleared"), 1)
            dve.memset(zero, 0.0).then_inc(sig("cleared"), 1)
            dve.wait_ge(sig("cleared"), 4)
            dve.wait_ge(sig("loaded"), 16 * LOADS)
            dve.wait_ge(sig("made"), 10)

            def order(s, nb, pad=0, tables=(), places=True):
                stretches = (ST if pad == P else PAIRS) // 2
                with dve.Fori(0, nb) as k:
                    dve.tensor_scalar(out=mask, in0=key, scalar1=lane[:, bass.ds(k, 1)], scalar2=None, op0=ALU.is_equal,
                                      op1=ALU.add, accum_out=counts[:, bass.ds(k, 1)]).then_inc(sig("counted"), 1)
                    dve.wait_ge(sig("counted"), k + (COUNTED[s] + 1))
                dve.wait_ge(sig("total"), ORDER[s] + 1)
                if pad:
                    shift = pad.bit_length() - 1
                    step(ts(small_i[0:NT, 0:1], ps[0:NT, 7, 0:1], float(pad - 1), None, ALU.add))
                    step(ts(small_i[0:NT, 1:2], small_i[0:NT, 0:1], shift, None, ALU.logical_shift_right))
                    step(copy(small[0:NT, 1:2], small_i[0:NT, 1:2]))
                    step(stt(small[0:NT, 3:4], small[0:NT, 1:2], -float(pad), ps[0:NT, 7, 0:1], ALU.mult, ALU.add))
                    ts(spread[0:NT, :], ones[0:NT, :], small[0:NT, 1:2], float(pad), ALU.mult, ALU.mult).then_inc(sig("spread"), 1)
                else:
                    ts(spread[:, :], ones[:, :], ps[:, 7, 0:1], None, ALU.mult).then_inc(sig("spread"), 1)
                dve.wait_ge(sig("start"), ORDER[s] + 1)
                step(ts(start_m1[:, 0:nb], ps[:, 7, 128:128 + nb], -1.0, None, ALU.add))
                if "last" in tables:
                    step(ts(last_a[0:1, :], ps[0:1, 7, 16:16 + NT], -1.0, 0.0, ALU.add, ALU.max))
                    dve.sem_inc(sig("src_tables"), 1)
                if tables:
                    step(copy(small[0:NT, 2:3], ps[0:NT, 7, 8:9]))
                    step(tt(small[0:NT, 2:3], small[0:NT, 2:3], small[0:NT, 1:2], ALU.add))
                    ts(reach[:, 0:2 * stretches], slot_no[:, 0:2 * stretches], small[0:NT, 2:3], None, ALU.is_ge)\
                        .then_inc(sig("reach"), 1)
                    dve.wait_ge(sig("cover"), ORDER[s] + 1)
                    for h in range(2):
                        part = slice(h * stretches, (h + 1) * stretches)
                        table = tile_a if pad == P else tile_b
                        step(ts(table[0:1, part], ps[0:1, 5 + h, 0:stretches], float(NT - 1), None, ALU.min))
                        if "from" in tables:
                            step(ts(seg_off[:, part], ps[:, 5 + h, 0:stretches], -float(P), 1.0, ALU.mult, ALU.add))
                            step(stt(rank[0:1, part], slot_no[0:1, part], float(pad), ps[0:1, 3 + h, 0:stretches],
                                     ALU.mult, ALU.add))
                            step(ts(from_b[0:1, part], rank[0:1, part], float(EDGES), None, ALU.min))
                if not places:
                    return
                with dve.Fori(0, nb) as k:
                    done = 3 * k + 3 * PLACED[s]
                    ts(mask, key, lane[:, bass.ds(k, 1)], None, ALU.is_equal).then_inc(sig("placed"), 1)
                    dve.wait_ge(sig("placed"), done + 1)
                    dve.tensor_tensor_scan(out=rank, data0=mask, data1=zero, initial=start_m1[:, bass.ds(k, 1)],
                                           op0=ALU.add, op1=ALU.add).then_inc(sig("placed"), 1)
                    dve.wait_ge(sig("placed"), done + 2)
                    hold()
                    dve.copy_predicated(place, mask.bitcast(U32), rank).then_inc(sig("placed"), 1)
                    dve.wait_ge(sig("placed"), done + 3)

            NOWHERE = float(4 * SLOTS)
            step(ts(tmp_i, src_i, 7, None, ALU.logical_shift_right))
            step(copy(key, tmp_i))
            step(copy(seg, src_i))
            step(stt(seg, key, -float(P), seg, ALU.mult, ALU.add))
            step(ts(seg, seg, 1.0, None, ALU.add))
            step(copy(other, dst_i))
            step(dve.memset(place, NOWHERE))
            order("src", NT, P, ("last",))

            step(tt(mask[:, 0:ROWS], dst_i[:, 0:ROWS], next_i, ALU.is_gt))
            step(dve.tensor_reduce(out=small[:, 4:5], in_=mask[:, 0:ROWS], axis=AX, op=ALU.max))
            step(tt(rank[0:1, 0:TAIL - 1], tail_i[:, 0:TAIL - 1], tail_i[:, 1:TAIL], ALU.is_gt))
            step(dve.tensor_reduce(out=small[0:1, 5:6], in_=rank[0:1, 0:TAIL - 1], axis=AX, op=ALU.max))
            tt(small[0:1, 4:5], small[0:1, 4:5], small[0:1, 5:6], ALU.add).then_inc(sig("checked"), 1)
            dve.wait_ge(sig("violations"), 1)
            step(ts(small[0:1, 6:7], ps[0:1, 7, 500:501], 1.0, None, ALU.min))
            step(copy(flag_i[0:1, 0:1], small[0:1, 6:7]))
            step(ts(flag_i[0:1, 1:2], small[0:1, 6:7], -1.0, 1.0, ALU.mult, ALU.add))
            step(ts(tmp_i, dst_i, 7, None, ALU.logical_shift_right))
            step(copy(key, tmp_i))
            order("dst_tiles", NT, 2 * P, ("from",), places=False)
            dve.sem_inc(sig("flagged"), 1)

            with dve.If(nc.vector.value_load(flag_i[0:1, 0:1], min_val=0, max_val=1)):
                outside = dict(own)
                own.update(base=0, i=0, per=0, n=0, name="v_branch")
                step(ts(tmp_i, dst_i, P - 1, None, ALU.bitwise_and))
                for b in range(2):
                    dve.wait_ge(sig(f"sent{b}"), sent("src", b))
                step(dve.memset(place, NOWHERE))
                step(copy(key, tmp_i))
                step(copy(pair_i[:, :, 0], dst_i))
                step(copy(pair_i[:, :, 1], src_i))
                order("low", P)
                for b in range(2):
                    dve.wait_ge(sig(f"sent{b}"), sent("low", b))
                dve.wait_ge(sig("low_back"), 16)
                step(dve.memset(place, NOWHERE))
                step(ts(tmp_i, pair_i[:, :, 0], 7, None, ALU.logical_shift_right))
                step(copy(key, tmp_i))
                order("dst", NT, 2 * P)
                for b in range(2):
                    dve.wait_ge(sig(f"staged{b}"), 3 * (SB // 2 + 1))
                own.update(outside)
            for b in range(2):
                dve.wait_ge(sig(f"staged{b}"), SB // 2 + 1)

            def clear(n):
                step(dve.memset(acc[:, 0:n], 0.0))

            clear(NT * ACC1)

            def one_hot(s, seg_of, j, b, part=None):
                u = CFG[s][0]
                if part is not None:
                    m = tt(hots(s, b)[:, part, :], lane1[:, :], seg_of[:, bass.ds(j * u + part, 1)].broadcast_to([P, P]), ALU.is_equal)
                    if part == u - 1:
                        m.then_inc(sig("hot"), 1)
                    return
                tt(hots(s, b), lane1[:, :].unsqueeze(1).broadcast_to([P, u, P]),
                   seg_of[:, bass.ds(j * u, u)].unsqueeze(2).broadcast_to([P, u, P]), ALU.is_equal).then_inc(sig("hot"), 1)

            def tiles_of(table, j, n):
                return nc.values_load_multi_w_load_instructions(
                    table[0:1, bass.ds(j * n, n)], engines=[mybir.EngineType.DVE], min_val=0, max_val=NT - 1,
                    skip_runtime_bounds_check_because="the tables hold numbers of node tiles, capped at the last")[1]

            def add_sums(s, j, first, k, width, beside=None, part=slice(None)):
                n = CFG[s][0] // CFG[s][3]
                for v in range(n)[part]:
                    dve.wait_ge(sig("sum"), j * n + (sums_before(s) + v + 1))
                    if s == "p1":
                        halves = [(0, D, 2 * (v % 4), 0, ACC1), (D + 1, 2 * (D + 1), 2 * (v % 4) + 1, 0, ACC1)]
                    else:
                        h, stride = width // 2, ACC1 if s == "p2" else width
                        halves = [(0, h, v % 4, 0, stride), (h, width, v % 4, h, stride)]
                    for m, (a0, a1, bank, c0, stride) in enumerate(halves):
                        if not (first and v == 0):
                            dve.wait_ge(sig("add"), j * (2 * n) + (2 * sums_before(s) + 2 * v - 1 + m))
                        a = acc[:, bass.ds(k[v] * stride + a0, a1 - a0)]
                        tt(a, a, ps[:, bank, c0:c0 + a1 - a0], ALU.add).then_inc(sig("add"), 1)
                        if beside:
                            beside(v, m)

            def sum_pass(s):
                u, ring = CFG[s][0:2]

                def hots(i, b):
                    if s == "p1":
                        dve.wait_ge(sig(f"segs{b}"), i + 1)
                    one_hot(s, seg_a, ring * i + b, b)

                def round_(i, first, last):
                    for b in range(ring):
                        k = tiles_of(tile_a, ring * i + b, u)
                        if not (last and b == ring - 1):
                            hots(i + (b + 1) // ring, (b + 1) % ring)
                        add_sums(s, ring * i + b, first and b == 0, k, D)

                hots(0, 0)
                peeled(dve, batches(s) // ring, round_)

            def ln_stats(s, g, part, src):
                h, t0, t1 = part
                for t in range(t0, t1):
                    m = dve.bn_stats(stat[:, t, :], src(t))
                step(m)
                hold()
                for t in range(t0, t1):
                    m = dve.bn_aggr(mv[:, t, :], stat[:, t, :])
                step(m)
                ts(sd[:, 0, t0:t1], mv[:, t0:t1, 1], EPS, None, ALU.add).then_inc(sig("ln_var"), 1)
                dve.wait_ge(sig("ln_sqrt"), nth(NORM, s, g, h) + 1)
                step(dve.reciprocal(sd[:, 2, t0:t1], sd[:, 1, t0:t1]))
                stt(sd[:, 3, t0:t1], mv[:, t0:t1, 0], -1.0, sd[:, 2, t0:t1], ALU.mult, ALU.mult).then_inc(sig("ln_rstd"), 1)

            def over(v, n):
                return vec[:, v:v + 1, :].broadcast_to([P, n, D])

            def affine(s, g, part, buf, gamma, beta):
                h, t0, t1 = part
                b = buf[:, t0:t1, :]
                dve.wait_ge(sig("ln_normed"), nth(NORM, s, g, h) + 1)
                step(tt(b, b, over(gamma, t1 - t0), ALU.mult))
                return tt(b, b, over(beta, t1 - t0), ALU.add)

            sum_pass("p1")
            deg = acc[:, :].rearrange("p (k w) -> p k w", w=ACC1)[:, :, ACC1 - 1]
            dve.wait_ge(sig("add"), 2 * ST)
            step(ts(rdeg[:, :], deg, 1.0, None, ALU.max))
            step(dve.reciprocal(rdeg[:, :], rdeg[:, :]))

            def layer_in(g):
                for h, t0, t1 in PARTS:
                    for t in range(t0, t1):
                        k = g * G + t
                        a = acc[:, bass.ds(k * ACC1, D)]
                        m = stt(ub[:, t, :], a, rdeg[:, bass.ds(k, 1)], xin[:, t, :], ALU.mult, ALU.add)
                    m.then_inc(sig("operand"), 1)

            def stored(s, g):
                dve.wait_ge(sig("free"), STAGE[s] * (NG + 1) + g + 1)

            def first_layer(g):
                dve.wait_ge(sig("d0_in"), 16 * (g + 1))
                stored("d0", g)
                layer_in(g)
                for part in PARTS:
                    dve.wait_ge(sig("d0_mm"), 2 * g + (part[0] + 1))
                    ln_stats("d0a", g, part, pt)
                for part in PARTS:
                    affine("d0a", g, part, ub, V_G0, V_BE0).then_inc(sig("d0_affine"), 1)

            dve.sem_inc(sig("free"), 1)
            groups(8, first_layer)
            dve.wait_ge(sig("sums_cleared"), 1)

            sum_pass("p2")
            dve.wait_ge(sig("add"), 4 * ST)
            def second_layer(g):
                dve.wait_ge(sig("d1_in"), 32 * (g + 1))
                layer_in(g)
                dve.wait_ge(sig("operand"), 2 * g + (2 * NG + 2))
                hold()
                copy(xin[:, :, :], acc[:, bass.ds(g * (G * ACC1), G * ACC1)].rearrange("p (t w) -> p t w", w=ACC1)
                     [:, :, D + 1:2 * D + 1]).then_inc(sig("d1_edges"), 1)
                for part in PARTS:
                    dve.wait_ge(sig("d1_mm"), 2 * g + (part[0] + 1))
                    ln_stats("d1a", g, part, pt)
                for part in PARTS:
                    affine("d1a", g, part, ub, V_G1, V_BE1).then_inc(sig("d1_affine"), 1)
                stored("d1", g)
                for part in PARTS:
                    h, t0, t1 = part
                    dve.wait_ge(sig("d1_silu"), 2 * g + (h + 1))
                    step(tt(ub[:, t0:t1, :], ub[:, t0:t1, :], xin2[:, t0:t1, :], ALU.add))
                    ln_stats("d1b", g, part, lambda t: ub[:, t, :])
                for part in PARTS:
                    dve.wait_ge(sig("d1_mm2"), 2 * g + (part[0] + 1))
                    ln_stats("d1d", g, part, pt)
                for part in PARTS:
                    h, t0, t1 = part
                    step(affine("d1d", g, part, xin2, V_LGA, V_LBE))
                    for _ in range(2):
                        step(tt(xin2[:, t0:t1, :], xin2[:, t0:t1, :], ub[:, t0:t1, :], ALU.add))
                    ln_stats("d1e", g, part, lambda t: xin2[:, t, :])
                for h, t0, t1 in PARTS:
                    dve.wait_ge(sig("d1_elr"), 2 * g + (h + 1))
                    hold()
                    n = t1 - t0
                    lr = psf[:, 2048 * h + 512:2048 * h + 512 + n * 2 * H2].rearrange("p (t w) -> p t w", w=2 * H2)
                    step(copy(el[:, bass.ds(g * (G * H2) + t0 * H2, n * H2)].rearrange("p (t w) -> p t w", w=H2), lr[:, :, 0:H2]))
                    m = copy(prj2[:, t0:t1, C2:W2], lr[:, :, H2:2 * H2])
                m.then_inc(sig("result"), 1)

            dve.sem_inc(sig("free"), 1)
            groups(2 * (4 * 3 + 1 + 1 + 2 + 2 + 1), second_layer)
            clear(NT * ACC2)

            dve.wait_ge(sig("dst_back"), 16 * RB)
            step(dve.memset(dst_rowf, 0.0))
            for w in range(2):
                n = ST5 - (RB - 1) * P
                step(copy(dst_rowf[:, 0:RB - 1, w, :], dst_rows[:, 0:RB - 1, :, w]))
                step(copy(dst_rowf[0:n, RB - 1, w, :], dst_rows[0:n, RB - 1, :, w]))
            dve.sem_inc(sig("dst_rowf"), 1)
            dve.wait_ge(sig("dst_cols"), 1)
            step(tt(seg_b[:, :].rearrange("p (q t) -> p q t", t=2), psf[:, 0:ST5].rearrange("p (q t) -> p q t", t=2),
                    seg_off[:, :].unsqueeze(2).broadcast_to([P, PAIRS, 2]), ALU.add))
            step(ts(idx_b[:, :], psf[:, 1024:1024 + ST5], 0.0, None, ALU.max))

            def p3_message(j, buf, u):
                if u == 0:
                    dve.wait_ge(sig("p3_exp"), j + 1)
                m = tt(mring[:, buf % 2, u, 0:D].rearrange("p (h c) -> p h c", c=C2),
                       p3_rows[:, buf * U + u, 0:C2].unsqueeze(1).broadcast_to([P, H2, C2]),
                       mring[:, buf % 2, u, D:D + H2].unsqueeze(2).broadcast_to([P, H2, C2]), ALU.mult)
                if u == U - 1:
                    m.then_inc(sig("p3_msg"), 1)

            def p3_beat(a, b, c):
                if c:
                    k = tiles_of(tile_a, c[0], U)
                if b:
                    j, i, buf = b
                    dve.wait_ge(sig("p3_el"), j + 1)
                    dve.wait_ge(sig(f"got{buf}"), got("p3", buf, i + 1))
                    tt(zl[:, 0], ps[:, 6 + buf % 2, 0:U * H2].rearrange("p (u h) -> p u h", h=H2),
                       p3_rows[:, buf * U:(buf + 1) * U, C2:W2], ALU.add).then_inc(sig("p3_z"), 1)
                if a:
                    one_hot("p3", seg_a, a[0], a[2])
                if b:
                    dve.wait_ge(sig("p3_z"), j + 1)
                    stt(zl[:, 1], zl[:, 0], 0.2, zl[:, 0], ALU.mult, ALU.max).then_inc(sig("p3_leaky"), 1)
                if c:
                    add_sums("p3", c[0], False, k, ACC2, (lambda v, m: p3_message(j, buf, v) if m == 1 else None) if b else None)
                elif b:
                    for u in range(U):
                        p3_message(j, buf, u)

            beats(dve, "p3", 3, p3_beat)

            dve.wait_ge(sig("add"), 6 * ST)
            dve.wait_ge(sig("d1_vectors"), 16 * 5)

            def third_layer(g):
                a3 = acc[:, bass.ds(g * (G * ACC2), G * ACC2)].rearrange("p (t w) -> p t w", w=ACC2)
                rs = sd[:, :, :].rearrange("p a b -> p (a b)").rearrange("p (t h) -> p t h", h=H2)
                step(ts(rs, a3[:, :, D:ACC2], 1e-12, None, ALU.max))
                step(dve.reciprocal(rs, rs))
                for h, t0, t1 in PARTS:
                    for t in range(t0, t1):
                        m = tt(ub[:, t, :].rearrange("p (h c) -> p h c", c=C2), a3[:, t, 0:D].rearrange("p (h c) -> p h c", c=C2),
                               rs[:, t, :].unsqueeze(2).broadcast_to([P, H2, C2]), ALU.mult)
                    step(m)
                    ubh = ub[:, t0:t1, :].rearrange("p t (h c) -> p (t h) c", c=C2)
                    step(tt(ubh, ubh, abv[:, :].unsqueeze(1).broadcast_to([P, (t1 - t0) * H2, C2]), ALU.add))
                    if h == 0:
                        stored("d2", g)
                    ts(xin2[:, t0:t1, :], ub[:, t0:t1, :], 0.0, None, ALU.min).then_inc(sig("d2_low"), 1)
                for part in PARTS:
                    h, t0, t1 = part
                    b = ub[:, t0:t1, :]
                    dve.wait_ge(sig("d2_exp"), 2 * g + (h + 1))
                    step(stt(b, b, 0.0, xin2[:, t0:t1, :], ALU.max, ALU.add))
                    dve.wait_ge(sig("d2_in"), 16 * (g + 1))
                    step(stt(b, b, -1.0, xin[:, t0:t1, :], ALU.add, ALU.add))
                    if h == 1:
                        dve.sem_inc(sig("consumed"), 1)
                    ln_stats("d2a", g, part, lambda t: ub[:, t, :])
                mag = ma[:, bass.ds(g * (G * 2 * H3), G * 2 * H3)].rearrange("p (t w) -> p t w", w=2 * H3)
                for h, t0, t1 in PARTS:
                    dve.wait_ge(sig("d2_projc"), 2 * g + (h + 1))
                    for n, v in enumerate((V_GSRC, V_GDST)):
                        step(tt(ub[:, t0:t1, :], prj3[:, t0:t1, 0:D], over(v, t1 - t0), ALU.mult))
                        step(dve.tensor_reduce(out=mag[:, t0:t1, n * H3:(n + 1) * H3],
                                               in_=ub[:, t0:t1, :].rearrange("p t (h c) -> p t h c", c=C3), axis=AX, op=ALU.add))
                hold()
                copy(prj3[:, :, D:W3], mag[:, :, 0:H3]).then_inc(sig("result"), 1)

            dve.sem_inc(sig("free"), 1)
            groups(2 + 2 * (2 + 2 + 3 + 4), third_layer)
            clear(NT * W3)
            step(dve.memset(lastm[:, :], 1.0))
            step(dve.memset(pen[:, :], -BIG))
            step(dve.memset(svt[:, :, :], 1.0))

            def leaky(dst, src):
                return stt(dst, src, 0.2, src, ALU.mult, ALU.max)

            V = U // 2

            def chain(name, per, j, beside=None):
                n = [0]

                def put(ins, wait=True):
                    n[0] += 1
                    ins.then_inc(sig(name), 1)
                    if beside:
                        beside(n[0])
                    if wait:
                        dve.wait_ge(sig(name), j * per + n[0])

                put.end = lambda: n[0] == per
                return put

            def maxima(j):
                dve.wait_ge(sig("p5_rows_c"), j + 1)
                f = chain("p5_scan", 3, j)
                f(tt(lastm[:, 0:P - 1], rowsb[:, 1, 0:P - 1], rowsb[:, 1, 1:P], ALU.not_equal))
                f(ts(pen[:, 1:P], lastm[:, 0:P - 1], -BIG, None, ALU.mult))
                f(dve.tensor_tensor_scan(out=scan[:, :], data0=pen[:, :], data1=rowsb[:, 0, :], initial=0.0,
                                         op0=ALU.add, op1=ALU.max))
                assert f.end()
                tt(sv[:, :], scan[:, :], lastm[:, :], ALU.mult).then_inc(sig("p5_top"), 1)

            def new_maxima(j, k, beside):
                dve.wait_ge(sig("p5_max"), j + 1)
                f = chain("p5_front", 7 + V, j, beside)
                mx = ps[:, 7, 0:U * (H3 + 1)].rearrange("p (u w) -> p u w", w=H3 + 1)
                f(ts(present[:, :], mx[:, :, H3], 1.0, -1.0, ALU.min, ALU.add))
                f(stt(cand[:, :, :], present[:, :].unsqueeze(2).broadcast_to([P, U, H3]), BIG, mx[:, :, 0:H3], ALU.mult, ALU.add))
                pair = cand[:, :, :].rearrange("p (v t) h -> p v t h", t=2)
                f(tt(pair[:, :, 0, :], pair[:, :, 0, :], pair[:, :, 1, :], ALU.max), False)
                f(copy(mold[:, 0, :], ma[:, bass.ds(k[0] * (2 * H3), 2 * H3)]))
                for v in range(V):
                    m = ma[:, bass.ds(k[v] * (2 * H3), H3)]
                    f(tt(m, m, pair[:, v, 0, :], ALU.max))
                dve.sem_inc(sig("p5_newmax"), 1)
                f(copy(mold[:, 1, :], ma[:, bass.ds(k[0] * (2 * H3), 2 * H3)]))
                f(tt(resc[:, 0], mold[:, :, 0:H3], mold[:, :, H3:2 * H3], ALU.add))
                f(leaky(resc[:, 1], resc[:, 0]))
                tt(resc[:, 2, 0, :], resc[:, 1, 0, :], resc[:, 1, 1, :], ALU.subtract).then_inc(sig("p5_fade"), 1)
                assert f.end()

            def fade(j, buf, k):
                dve.wait_ge(sig("p5_fade_e"), j + 1)
                a = acc[:, bass.ds(k[0] * W3, D)].rearrange("p (h c) -> p h c", c=C3)
                tt(a, a, resc[:, 3, buf % 2, :].unsqueeze(2).broadcast_to([P, H3, C3]), ALU.mult).then_inc(sig("p5_faded"), 1)
                a = acc[:, bass.ds(k[0] * W3 + D, H3)]
                tt(a, a, resc[:, 3, buf % 2, :], ALU.mult).then_inc(sig("p5_faded"), 1)

            def logits(j, b):
                dve.wait_ge(sig("p5_spread_c"), j + 1)
                f = chain("p5_back", 3, j)
                f(tt(zz[:, 0], ees[:, :, H3:2 * H3], rows5(b)[:, :, D:W3], ALU.add), False)
                f(tt(zz[:, 1], ees[:, :, H3:2 * H3], ees[:, :, 0:H3], ALU.add))
                f(leaky(zz[:, 0:2], zz[:, 0:2]))
                assert f.end()
                tt(zz[:, 2], zz[:, 0], zz[:, 1], ALU.subtract).then_inc(sig("p5_logit"), 1)

            def p5_message(j, b, u):
                if u == 0:
                    dve.wait_ge(sig("p5_exp"), j + 1)
                v = rows5(b)[:, u, 0:D].rearrange("p (h c) -> p h c", c=C3)
                m = tt(v, v, rows5(b)[:, u, D:W3].unsqueeze(2).broadcast_to([P, H3, C3]), ALU.mult)
                if u == U - 1:
                    m.then_inc(sig("p5_msg"), 1)

            def p5_beat(a, b, c, d):
                if b:
                    k_max = tiles_of(tile_b, b[0], V)
                if d:
                    k = tiles_of(tile_b, d[0], V)
                if b:
                    new_maxima(b[0], k_max, (lambda n: one_hot("p5", seg_b, a[0], a[2], n - 1)
                                                                  if n <= U else None) if a else None)
                elif a:
                    one_hot("p5", seg_b, a[0], a[2])
                def adds(part):
                    if d:
                        add_sums("p5", d[0], False, k, W3, (lambda v, m: p5_message(c[0], c[2], 2 * v + m)) if c else None, part)

                if d:
                    dve.wait_ge(sig("p5_faded"), 2 * (d[0] + 1))
                elif c:
                    for u in range(U):
                        p5_message(c[0], c[2], u)
                adds(slice(0, 2))
                if c:
                    k_fade = tiles_of(tile_b, c[0], V)
                if a:
                    maxima(a[0])
                adds(slice(2, 4))
                if c:
                    if d:
                        dve.wait_ge(sig("add"), (d[0] + 1) * (2 * V) + 2 * sums_before("p5"))
                    fade(c[0], c[2], k_fade)
                if b:
                    logits(b[0], b[2])

            beats(dve, "p5", 4, p5_beat)

            dve.wait_ge(sig("add"), 6 * ST + ST5)
            def fourth_layer(g):
                a3 = acc[:, bass.ds(g * (G * W3), G * W3)].rearrange("p (t w) -> p t w", w=W3)
                mag = ma[:, bass.ds(g * (G * 2 * H3), G * 2 * H3)].rearrange("p (t w) -> p t w", w=2 * H3)
                dve.wait_ge(sig("d3_in"), 32 * (g + 1))
                step(tt(self_t[:, 0], prj3[:, :, D:W3], mag[:, :, H3:2 * H3], ALU.add))
                step(tt(self_t[:, 1], mag[:, :, 0:H3], mag[:, :, H3:2 * H3], ALU.add))
                step(leaky(self_t[:, 2], self_t[:, 0]))
                step(leaky(self_t[:, 3], self_t[:, 1]))
                tt(self_t[:, 4], self_t[:, 2], self_t[:, 3], ALU.subtract).then_inc(sig("d3_logit"), 1)
                dve.wait_ge(sig("d3_exp"), g + 1)
                step(tt(self_t[:, 6], a3[:, :, D:W3], self_t[:, 5], ALU.add))
                step(dve.reciprocal(self_t[:, 7], self_t[:, 6]))
                stored("d3", g)
                for part in PARTS:
                    h, t0, t1 = part
                    b = ub[:, t0:t1, :]
                    for t in range(t0, t1):
                        u3 = ub[:, t, :].rearrange("p (h c) -> p h c", c=C3)
                        m = tt(u3, prj3[:, t, 0:D].rearrange("p (h c) -> p h c", c=C3),
                               self_t[:, 5, t, :].unsqueeze(2).broadcast_to([P, H3, C3]), ALU.mult)
                    step(m)
                    step(tt(b, b, a3[:, t0:t1, 0:D], ALU.add))
                    for t in range(t0, t1):
                        u3 = ub[:, t, :].rearrange("p (h c) -> p h c", c=C3)
                        m = tt(u3, u3, self_t[:, 7, t, :].unsqueeze(2).broadcast_to([P, H3, C3]), ALU.mult)
                    step(m)
                    step(tt(b, b, over(V_GB, t1 - t0), ALU.add))
                    ln_stats("d3a", g, part, lambda t: ub[:, t, :])
                for part in PARTS:
                    h, t0, t1 = part
                    step(affine("d3a", g, part, ub, V_GGA, V_GBE))
                    step(tt(xin2[:, t0:t1, :], ub[:, t0:t1, :], xin[:, t0:t1, :], ALU.add))
                    if h == 1:
                        dve.sem_inc(sig("consumed"), 1)
                    ln_stats("d3b", g, part, lambda t: xin2[:, t, :])

            dve.sem_inc(sig("free"), 1)
            groups(4 + 2 + 2 * (4 + 2 * 3 + 2 + 1), fourth_layer)

        @block.tensor
        def _(pe):
            def mm(dst, lhs, rhs, start=True, stop=True):
                return pe.matmul(dst, lhsT=lhs, rhs=rhs, start=start, stop=stop)

            def hold():
                pe.sem_inc(sig("t_pace"), 1)

            def totals(s, nb, pad=0, tables=False, weigh=False):
                pe.wait_ge(sig("counted"), COUNTED[s] + nb)
                mm(ps[0:nb, 7, 0:1], counts[:, 0:nb], ones[:, 0:1]).then_inc(sig("total"), 1)
                pe.wait_ge(sig("spread"), ORDER[s] + 1)
                if pad:
                    mm(ps[0:NT, 7, 8:9], below[0:NT, 0:NT], small[0:NT, 1:2])
                    mm(ps[0:1, 7, 16:16 + NT], small[0:NT, 1:2], upto[0:NT, 0:NT])
                mm(ps[:, 7, 128:128 + nb], below[:, :], counts[:, 0:nb], stop=False)
                mm(ps[:, 7, 128:128 + nb], spread[0:nb, :], below[0:nb, 0:nb], start=False).then_inc(sig("start"), 1)
                if tables:
                    n = (ST if pad == P else PAIRS) // 2
                    pe.wait_ge(sig("reach"), ORDER[s] + 1)
                    for h in range(2):
                        m = mm(ps[:, 5 + h, 0:n], ones[0:NT, :], reach[:, h * n:(h + 1) * n])
                        if weigh:
                            m = mm(ps[0:1, 3 + h, 0:n], small[0:NT, 3:4], reach[:, h * n:(h + 1) * n])
                    m.then_inc(sig("cover"), 1)

            pe.wait_ge(sig("made"), 10)
            pe.wait_ge(sig("loaded"), 16 * LOADS)
            totals("src", NT, P, tables=True)
            pe.wait_ge(sig("checked"), 1)
            mm(ps[0:1, 7, 500:501], small[:, 4:5], ones[:, 0:1]).then_inc(sig("violations"), 1)
            totals("dst_tiles", NT, 2 * P, tables=True, weigh=True)
            pe.wait_ge(sig("flagged"), 1)
            with pe.If(nc.tensor.value_load(flag_i[0:1, 0:1], min_val=0, max_val=1)):
                totals("low", P)
                totals("dst", NT, 2 * P)

            def sums(s, j, b, first, width, src, part=slice(None)):
                u_n, _, _, unit = CFG[s]
                n = u_n // unit
                pe.wait_ge(sig("hot"), j + (hots_before(s) + 1))
                for v in range(n)[part]:
                    if not (first and v < 4):
                        pe.wait_ge(sig("add"), j * (2 * n) + (2 * sums_before(s) + 2 * (v - 3)))
                    for t in range(unit):
                        c = slot(s, b, v * unit + t)
                        one = hots(s, b)[:, v * unit + t, :]
                        if s == "p1":
                            mm(ps[:, 2 * (v % 4), 0:D], one, ring_x[:, c, 0:D])
                            m = mm(ps[:, 2 * (v % 4) + 1, 0:D + 1], one, ring_e[:, c, 2:EW + 1])
                        else:
                            m = mm(ps[:, v % 4, 0:width], one, src(b, v * unit + t), start=t == 0, stop=t == unit - 1)
                    m.then_inc(sig("sum"), 1)

            def sum_pass(s, width, src):
                ring = CFG[s][1]

                def round_(i, first, last):
                    for b in range(ring):
                        pe.wait_ge(sig(f"got{b}"), got(s, b, i + 1))
                        if s == "p1":
                            pe.wait_ge(sig(f"p1_rows{b}"), 16 * (i + 1))
                        sums(s, ring * i + b, b, first and b == 0, width, src)
                peeled(pe, batches(s) // ring, round_)

            def turn(h, parts):
                for n, v in enumerate(parts):
                    m = pe.transpose(psf[:, 2048 * h + n * P:2048 * h + (n + 1) * P], v, ident[:, :])
                m.then_inc(sig("turned"), 1)

            def tile_by_tile(buf, t0, t1):
                return [buf[:, t, c * P:(c + 1) * P] for t in range(t0, t1) for c in range(2)]

            def product(o, h, i, wts, stop=True, start=True):
                for c in range(2):
                    b = 2048 * h + (2 * i + c) * P
                    m = mm(o, op_t[:, b:b + P], wts[:, c, :], start=start and c == 0, stop=c == 1)
                return m

            def layer(s, g, wts, row, name):
                for h, t0, t1 in PARTS:
                    pe.wait_ge(sig("operand"), 2 * g + (2 * STAGE[s] * NG + h + 1))
                    turn(h, tile_by_tile(ub, t0, t1))
                for h, t0, t1 in PARTS:
                    pe.wait_ge(sig("taken"), nth(TURN, name, g, h) + 1)
                    for t in range(t0, t1):
                        mm(pt(t), ones[0:1, :], rows[0:1, row, :], stop=False)
                        m = product(pt(t), h, t - t0, wts, start=False)
                    m.then_inc(sig(f"{s}_mm"), 1)

            sum_pass("p1", D, None)
            with pe.Fori(0, NG) as g:
                layer("d0", g, wsq, 0, "d0a")
            sum_pass("p2", D, lambda b, u: ring_x[:, b * U + u, 0:D])
            pe.wait_ge(sig("d0_weights"), 16)
            with pe.Fori(0, NG) as g:
                layer("d1", g, wsq, 1, "d1a")
                for h, t0, t1 in PARTS:
                    pe.wait_ge(sig("ln_normed"), nth(NORM, "d1b", g, h) + 1)
                    pe.wait_ge(sig("d1_edges"), g + 1)
                    turn(h, [buf[:, t, c * P:(c + 1) * P] for buf in (ub, xin) for c in range(2) for t in range(t0, t1)])
                for h, t0, t1 in PARTS:
                    pe.wait_ge(sig("taken"), nth(TURN, "d1c", g, h) + 1)
                    n = (t1 - t0) * P
                    for m_ in range(4):
                        for c in range(4):
                            m = mm(ps[:, 4 * h + m_, 0:n], lw1s[:, c, m_ * P:(m_ + 1) * P],
                                   op_t[:, 2048 * h + c * n:2048 * h + (c + 1) * n], start=c == 0, stop=c == 3)
                    m.then_inc(sig("d1_hidden"), 1)
                for h, t0, t1 in PARTS:
                    pe.wait_ge(sig("d1_hid_t"), 2 * g + (h + 1))
                    for t in range(t0, t1):
                        mm(pt(t), ones[0:1, :], rows[0:1, 2, :], stop=False)
                        for c in range(4):
                            b = 2048 * h + c * (t1 - t0) * P + (t - t0) * P
                            m = mm(pt(t), hid_t[:, b:b + P], lw2s[:, c, :], start=False, stop=c == 3)
                    m.then_inc(sig("d1_mm2"), 1)
                for h, t0, t1 in PARTS:
                    pe.wait_ge(sig("ln_normed"), nth(NORM, "d1e", g, h) + 1)
                    turn(h, tile_by_tile(out1, t0, t1))
                for h, t0, t1 in PARTS:
                    pe.wait_ge(sig("taken"), nth(TURN, "d1f", g, h) + 1)
                    for i in range(t1 - t0):
                        o = 2048 * h + 1024 + i * C2
                        m = product(psf[:, o:o + C2], h, i, aws)
                    m.then_inc(sig("d1_proj"), 1)
                for h, t0, t1 in PARTS:
                    pe.wait_ge(sig("d1_projc"), 2 * g + (h + 1))
                    hold()
                    for t in range(t0, t1):
                        o = 2048 * h + (t - t0) * P
                        m = pe.transpose(psf[0:C2, o:o + P], prj2[:, t, 0:C2], ident[:, :])
                    m.then_inc(sig("d1_projt"), 1)
                for h, t0, t1 in PARTS:
                    pe.wait_ge(sig("d1_projtc"), 2 * g + (h + 1))
                    for t in range(t0, t1):
                        o = 2048 * h + 512 + (t - t0) * 2 * H2
                        m = mm(psf[:, o:o + 2 * H2], hot_t[0:C2, t, :], awlrs[:, :])
                    m.then_inc(sig("d1_elr"), 1)

            def turn_hots(s, j, b, first):
                pe.wait_ge(sig("hot"), j + (hots_before(s) + 1))
                if not first:
                    pe.wait_ge(sig(f"{s}_hot_tc"), 2 * j)
                for u in range(U):
                    m = pe.transpose(ps[:, 4 + u // 4, (u % 4) * P:(u % 4 + 1) * P], hots(s, b)[:, u, :], ident[:, :])
                m.then_inc(sig(f"{s}_hot_t"), 1)

            def tiles_of(table, j, n):
                return nc.values_load_multi_w_load_instructions(
                    table[0:1, bass.ds(j * n, n)], engines=[mybir.EngineType.PE], min_val=0, max_val=NT - 1,
                    skip_runtime_bounds_check_because="the tables hold numbers of node tiles, capped at the last")[1]

            pe.wait_ge(sig("dst_rowf"), 1)
            for t in range(RB):
                n = min(P, ST5 - t * P)
                for w in range(2):
                    m = pe.transpose(psf[:, w * 1024 + t * P:w * 1024 + t * P + n], dst_rowf[0:n, t, w, :], ident[0:n, 0:n])
            m.then_inc(sig("dst_cols"), 1)

            def p3_beat(a, b, c):
                def some(part):
                    if c:
                        j, _, buf = c
                        pe.wait_ge(sig("p3_msg"), j + 1)
                        sums("p3", j, buf, at(j, 0), ACC2, lambda b, u: mring[:, b % 2, u, :], part)

                some(slice(0, 4))
                if a:
                    turn_hots("p3", a[0], a[2], at(a[0], 0))
                some(slice(4, 8))
                if a:
                    j, _, buf = a
                    k = tiles_of(tile_a, j, U)
                    pe.wait_ge(sig("p3_hot_tc"), 2 * (j + 1))
                    for u in range(U):
                        m = mm(ps[:, 6 + buf % 2, u * H2:(u + 1) * H2], hot_t[:, u, :], el[:, bass.ds(k[u] * H2, H2)])
                    m.then_inc(sig("p3_el"), 1)

            beats(pe, "p3", 3, p3_beat)

            pe.wait_ge(sig("d1_weights"), 16)
            with pe.Fori(0, NG) as g:
                for h, t0, t1 in PARTS:
                    pe.wait_ge(sig("ln_normed"), nth(NORM, "d2a", g, h) + 1)
                    turn(h, tile_by_tile(xin2, t0, t1))
                for h, t0, t1 in PARTS:
                    pe.wait_ge(sig("taken"), nth(TURN, "d2b", g, h) + 1)
                    for t in range(t0, t1):
                        m = product(pt(t), h, t - t0, wsq)
                    m.then_inc(sig("d2_proj"), 1)

            n5 = U * H3

            def p5_beat(a, b, c, d):
                if d:
                    pe.wait_ge(sig("p5_msg"), d[0] + 1)
                    sums("p5", d[0], d[2], at(d[0], 0), W3, lambda b, u: rows5(b)[:, u, :])
                if a:
                    j, _, buf = a
                    pe.wait_ge(sig("p5_cmp"), j + 1)
                    if not at(j, 0):
                        pe.wait_ge(sig("p5_rows_c"), j)
                    hold()
                    for w in range(2):
                        m = pe.transpose(ps[0:n5, 6, w * P:(w + 1) * P], cmp[:, w, :], ident[:, :])
                    m.then_inc(sig("p5_rows_t"), 1)
                if b:
                    j = b[0]
                    k = tiles_of(tile_b, j, U // 2)
                    pe.wait_ge(sig("p5_newmax"), j + 1)
                    pe.wait_ge(sig("p5_hot_tc"), 2 * (j + 1))
                    for u in range(U):
                        m = mm(ps[:, 7, 128 + u * 2 * H3:128 + (u + 1) * 2 * H3], hot_t[:, u, :],
                               ma[:, bass.ds(k[u // 2] * (2 * H3), 2 * H3)])
                    m.then_inc(sig("p5_spread"), 1)
                if a:
                    turn_hots("p5", a[0], a[2], at(a[0], 0))
                if a:
                    j, _, buf = a
                    pe.wait_ge(sig("p5_top"), j + 1)
                    hold()
                    pe.transpose(ps[:, 6, 256:256 + n5], sv[:, :], ident[0:n5, 0:n5]).then_inc(sig("p5_top_t"), 1)
                    pe.wait_ge(sig("p5_top_c"), j + 1)
                    for u in range(U):
                        m = mm(ps[:, 7, u * (H3 + 1):(u + 1) * (H3 + 1)], hots("p5", buf)[:, u, :], svt[:, u, :])
                    m.then_inc(sig("p5_max"), 1)

            beats(pe, "p5", 4, p5_beat)


def kernel(x, src, dst, edge_attr_256, L0_gnn_W0, L0_gnn_b0, L0_gnn_g0, L0_gnn_beta0, L0_gnn_W1, L0_gnn_b1, L0_gnn_g1,
           L0_gnn_beta1, L1_gnn_W1, L1_gnn_b1, L1_gnn_W2, L1_gnn_b2, L1_gnn_gamma, L1_gnn_beta, L2_gnn_W, L2_gnn_Wl,
           L2_gnn_Wr, L2_gnn_b, L3_gnn_W, L3_gnn_att_src, L3_gnn_att_dst, L3_gnn_bias, L3_gnn_gamma, L3_gnn_beta):
    import numpy as np
    import concourse.bacc as bacc
    from concourse.bass_utils import run_bass_kernel_spmd

    def columns(a):
        c = np.full((P, COLS), NODES_UP, np.int32)
        c[:, 0:ROWS] = a[0:ROWS * P].reshape(P, ROWS)
        c[0:TAIL, ROWS] = a[ROWS * P:EDGES]
        return c

    def padded(a):
        c = np.zeros((NODES_UP, D), np.float32)
        c[0:NODES] = a
        return c

    src, dst = np.asarray(src), np.asarray(dst)
    both = np.full((EDGES + 2 * P, 2), -1, np.int32)
    both[0:EDGES, 0], both[0:EDGES, 1] = dst, src
    arrays = [
        padded(np.asarray(x)), columns(src), columns(dst), dst[1:ROWS * P + 1].reshape(P, ROWS),
        dst[ROWS * P:EDGES].reshape(1, TAIL), both, np.asarray(edge_attr_256),
        np.asarray(L0_gnn_W0).T, L0_gnn_b0, L0_gnn_g0, L0_gnn_beta0,
        np.asarray(L0_gnn_W1).T, L0_gnn_b1, L0_gnn_g1, L0_gnn_beta1,
        L1_gnn_W1, np.asarray(L1_gnn_b1).reshape(4, P).T, L1_gnn_W2, L1_gnn_b2, L1_gnn_gamma, L1_gnn_beta,
        L2_gnn_W, np.concatenate([np.asarray(L2_gnn_Wl).T, np.asarray(L2_gnn_Wr).T], axis=1), L2_gnn_b,
        L3_gnn_W, np.asarray(L3_gnn_att_src).reshape(-1), np.asarray(L3_gnn_att_dst).reshape(-1),
        L3_gnn_bias, L3_gnn_gamma, L3_gnn_beta,
    ]
    names = ["x", "src", "dst", "dst_next", "dst_tail", "pairs", "edge_attr", "w0t", "b0", "g0", "be0", "w1t", "b1", "g1", "be1", "lw1", "lb1", "lw2",
             "lb2", "lga", "lbe", "aw", "awlr", "ab", "gw", "gsrc", "gdst", "gb", "gga", "gbe"]
    arrays = {f"in_{n}": np.ascontiguousarray(np.asarray(a)) for n, a in zip(names, arrays)}
    nc = bacc.Bacc("TRN2", target_bir_lowering=False, num_devices=1)
    aps = [nc.dram_tensor(n, a.shape, mybir.dt.from_np(a.dtype), kind="ExternalInput").ap() for n, a in arrays.items()]
    out = nc.dram_tensor("out_x", (NODES_UP, D), F32, kind="ExternalOutput").ap()
    gnn_kernel(nc, *aps, out)
    r = run_bass_kernel_spmd(nc, [arrays], core_ids=[0])
    return np.asarray(r.results[0]["out_x"])[0:NODES]
```
